# Optimizing a Trainium2 kernel written in Bass

```python
import numpy as np
import jax
import jax.numpy as jnp

def _softmax(x, axis=-1):
    return jax.nn.softmax(x, axis=axis)

def _gelu(x):
    return jax.nn.gelu(x, approximate=True)

def _silu(x):
    return jax.nn.silu(x)

def _sigmoid(x):
    return jax.nn.sigmoid(x)

def _layernorm(x, axis=-1, eps=1e-05):
    m = jnp.mean(x, axis=axis, keepdims=True)
    v = jnp.var(x, axis=axis, keepdims=True)
    return (x - m) / jnp.sqrt(v + eps)

def _scatter_add(tgt, idx, src, axis=0):
    return tgt.at[idx].add(src)

def _segment_sum(src, seg, n):
    return jax.ops.segment_sum(src, seg, n)
kernel_name = 'mk_macaron_d1_jaxref_r8_90f061'

def setup_inputs(seed: int=0):
    np.random.seed(seed)
    _w = jnp.asarray

    def _L0_attn_setup():
        import jax, jax.numpy as jnp
        import numpy as np
        D_MODEL = 128
        EXPAND = 2
        HEADDIM = 64
        D_STATE = 128
        D_CONV = 4
        D_INNER = EXPAND * D_MODEL
        NHEADS = D_INNER // HEADDIM
        CONV_DIM = D_INNER + 2 * D_STATE
        EPS = 1e-05

        def _causal_depthwise_conv(u, w, b):
            B, L, C = u.shape
            up = jnp.pad(u, ((0, 0), (D_CONV - 1, 0), (0, 0)))
            y = b
            for k in range(D_CONV):
                y = y + up[:, k:k + L, :] * w[:, k]
            return y

        def _rms(v):
            return v * jax.lax.rsqrt(jnp.mean(v * v, axis=-1, keepdims=True) + EPS)
        key = jax.random.key(seed)
        ks = jax.random.split(key, 8)
        d_in_proj = 2 * D_INNER + 2 * D_STATE + NHEADS
        x = jax.random.normal(ks[0], (2, 256, D_MODEL), jnp.float32)
        W_in = jax.random.normal(ks[1], (D_MODEL, d_in_proj), jnp.float32) * D_MODEL ** (-0.5)
        conv_w = jax.random.normal(ks[2], (CONV_DIM, D_CONV), jnp.float32) * 0.2
        conv_b = jnp.zeros((CONV_DIM,), jnp.float32)
        dt = jnp.exp(jax.random.uniform(ks[3], (NHEADS,), jnp.float32, minval=np.log(0.001), maxval=np.log(0.1)))
        dt_bias = dt + jnp.log(-jnp.expm1(-dt))
        A_log = jnp.log(jax.random.uniform(ks[4], (NHEADS,), jnp.float32, minval=1.0, maxval=16.0))
        D = jnp.ones((NHEADS,), jnp.float32)
        norm_w = jnp.ones((D_INNER,), jnp.float32)
        W_out = jax.random.normal(ks[5], (D_INNER, D_MODEL), jnp.float32) * D_INNER ** (-0.5)
        return dict(x=x, W_in=W_in, conv_w=conv_w, conv_b=conv_b, dt_bias=dt_bias, A_log=A_log, D=D, norm_w=norm_w, W_out=W_out)
    _L0_attn_in = _L0_attn_setup()

    def _L0_ffn_setup():
        import jax, jax.numpy as jnp
        import numpy as np
        TOP_K = 2
        key = jax.random.key(seed)
        k0, k1, k2, k3, k4 = jax.random.split(key, 5)
        B, S, D, H, E = (4, 256, 128, 256, 8)
        x = jax.random.normal(k0, (B, S, D), dtype=jnp.float32)
        router_w = jax.random.normal(k1, (E, D), dtype=jnp.float32) * D ** (-0.5)
        w_gate = jax.random.normal(k2, (E, D, H), dtype=jnp.float32) * D ** (-0.5)
        w_up = jax.random.normal(k3, (E, D, H), dtype=jnp.float32) * D ** (-0.5)
        w_down = jax.random.normal(k4, (E, H, D), dtype=jnp.float32) * H ** (-0.5)
        return {'x': x, 'router_w': router_w, 'w_gate': w_gate, 'w_up': w_up, 'w_down': w_down}
    _L0_ffn_in = _L0_ffn_setup()
    _d = {'L0_attn_x': _L0_attn_in['x'], 'L0_attn_W_in': _L0_attn_in['W_in'], 'L0_attn_conv_w': _L0_attn_in['conv_w'], 'L0_attn_conv_b': _L0_attn_in['conv_b'], 'L0_attn_dt_bias': _L0_attn_in['dt_bias'], 'L0_attn_A_log': _L0_attn_in['A_log'], 'L0_attn_D': _L0_attn_in['D'], 'L0_attn_norm_w': _L0_attn_in['norm_w'], 'L0_attn_W_out': _L0_attn_in['W_out'], 'L0_ffn_router_w': _L0_ffn_in['router_w'], 'L0_ffn_w_gate': _L0_ffn_in['w_gate'], 'L0_ffn_w_up': _L0_ffn_in['w_up'], 'L0_ffn_w_down': _L0_ffn_in['w_down']}
    _x0 = _d['L0_attn_x']
    _d['L0_attn_x'] = jax.random.normal(jax.random.fold_in(jax.random.key(seed), 1), (8, 1024, 128), dtype=_x0.dtype)
    del _x0
    return _d

def reference(L0_attn_x, L0_attn_W_in, L0_attn_conv_w, L0_attn_conv_b, L0_attn_dt_bias, L0_attn_A_log, L0_attn_D, L0_attn_norm_w, L0_attn_W_out, L0_ffn_router_w, L0_ffn_w_gate, L0_ffn_w_up, L0_ffn_w_down):

    def _L0_attn_ref(x, W_in, conv_w, conv_b, dt_bias, A_log, D, norm_w, W_out):
        import jax, jax.numpy as jnp
        import numpy as np
        D_MODEL = 128
        EXPAND = 2
        HEADDIM = 64
        D_STATE = 128
        D_CONV = 4
        D_INNER = EXPAND * D_MODEL
        NHEADS = D_INNER // HEADDIM
        CONV_DIM = D_INNER + 2 * D_STATE
        EPS = 1e-05

        def _causal_depthwise_conv(u, w, b):
            B, L, C = u.shape
            up = jnp.pad(u, ((0, 0), (D_CONV - 1, 0), (0, 0)))
            y = b
            for k in range(D_CONV):
                y = y + up[:, k:k + L, :] * w[:, k]
            return y

        def _rms(v):
            return v * jax.lax.rsqrt(jnp.mean(v * v, axis=-1, keepdims=True) + EPS)
        b, l, _ = x.shape
        zxbcdt = x @ W_in
        z = zxbcdt[..., :D_INNER]
        xBC = zxbcdt[..., D_INNER:D_INNER + CONV_DIM]
        dt = jax.nn.softplus(zxbcdt[..., -NHEADS:] + dt_bias)
        xBC = jax.nn.silu(_causal_depthwise_conv(xBC, conv_w, conv_b))
        xs = xBC[..., :D_INNER].reshape(b, l, NHEADS, HEADDIM)
        Bm = xBC[..., D_INNER:D_INNER + D_STATE]
        Cm = xBC[..., D_INNER + D_STATE:]
        A = -jnp.exp(A_log)
        decay = jnp.exp(dt * A)

        def step(h, inp):
            dec_t, dt_t, x_t, B_t, C_t = inp
            h = h * dec_t[:, :, None, None] + (dt_t[:, :, None] * x_t)[..., None] * B_t[:, None, None, :]
            y_t = jnp.einsum('bhpn,bn->bhp', h, C_t)
            return (h, y_t)
        h0 = jnp.zeros((b, NHEADS, HEADDIM, D_STATE), x.dtype)
        xs_t = (decay.transpose(1, 0, 2), dt.transpose(1, 0, 2), xs.transpose(1, 0, 2, 3), Bm.transpose(1, 0, 2), Cm.transpose(1, 0, 2))
        _, ys = jax.lax.scan(step, h0, xs_t)
        y = ys.transpose(1, 0, 2, 3) + D[None, None, :, None] * xs
        y = y.reshape(b, l, D_INNER)
        y = _rms(y * jax.nn.silu(z)) * norm_w
        out = y @ W_out
        return _rms(out) + x

    def _L0_ffn_ref(x, router_w, w_gate, w_up, w_down):
        import jax, jax.numpy as jnp
        import numpy as np
        TOP_K = 2
        B, S, D = x.shape
        E = router_w.shape[0]
        xt = x.reshape(-1, D)
        logits = xt @ router_w.T
        topk_vals, topk_idx = jax.lax.top_k(logits, TOP_K)
        g = jax.nn.sigmoid(topk_vals)
        g = g / (g.sum(axis=-1, keepdims=True) + 1e-10)
        out = jnp.zeros_like(xt)
        for e in range(E):
            ge = jnp.sum(jnp.where(topk_idx == e, g, jnp.zeros_like(g)), axis=-1)
            h = jax.nn.silu(xt @ w_gate[e]) * (xt @ w_up[e])
            out = out + ge[:, None] * (h @ w_down[e])
        return out.reshape(B, S, D)
    x = L0_attn_x
    x = x + 0.5 * _L0_ffn_ref(_layernorm(x, axis=-1), L0_ffn_router_w, L0_ffn_w_gate, L0_ffn_w_up, L0_ffn_w_down)
    x = x + _L0_attn_ref(_layernorm(x, axis=-1), L0_attn_W_in, L0_attn_conv_w, L0_attn_conv_b, L0_attn_dt_bias, L0_attn_A_log, L0_attn_D, L0_attn_norm_w, L0_attn_W_out)
    x = x + 0.5 * _L0_ffn_ref(_layernorm(x, axis=-1), L0_ffn_router_w, L0_ffn_w_gate, L0_ffn_w_up, L0_ffn_w_down)
    return x

_drawn_inputs = setup_inputs


def setup_inputs(seed=0):
    import zlib

    import numpy as np

    out = dict(_drawn_inputs(seed))
    spreads = {'L0_attn_conv_b': (0.0, 0.1), 'L0_attn_D': (1.0, 0.2), 'L0_attn_norm_w': (1.0, 0.2)}
    factors = {'L0_attn_A_log': 52.552}
    for name, (base, spread) in spreads.items():
        noise = np.random.default_rng([zlib.crc32(name.encode()), seed]).standard_normal(out[name].shape)
        drawn = base * np.exp(spread * noise) if base else spread * noise
        out[name] = jnp.asarray(drawn.astype(out[name].dtype))
    for name, factor in factors.items():
        out[name] = (out[name] * factor).astype(out[name].dtype)
    return out
```

```python
import concourse.bass as bass
from concourse import mybir
from contextlib import ExitStack

P = 128
D = 128
BATCH, SEQ = 8, 1024
N = BATCH * SEQ
TILES = N // P
E = 8
H = 256
T = 512
SLOTS_MAX = 2 * N // T + E - 1
ROWS = SLOTS_MAX * T
WROW = 2 * H + 2 * D
LN_EPS = 1e-5
INNER = 2 * D
HEADS, HD = 4, 64
STATE = 128
CONV = INNER + 2 * STATE
CH = CONV // P
CONV_K = 4
ZW = INNER + HEADS
CT = SEQ // P
FLOOR = -110.0

fp32 = mybir.dt.float32
f32r = mybir.dt.float32r
bf16 = mybir.dt.bfloat16
i32 = mybir.dt.int32
ALU = mybir.AluOpType
ACT = mybir.ActivationFunctionType
AX = mybir.AxisListType
ds = bass.ds


class Chain:

    def __init__(self, eng, sem, base=0):
        self.eng, self.sem, self.base, self.n = eng, sem, base, 0

    def __call__(self, ins):
        ins.then_inc(self.sem, 1)
        self.n += 1
        self.eng.wait_ge(self.sem, self.base + self.n)


def bc(ap, shape):
    return ap.broadcast_to(shape)


def build(nc, io, out):
    ctx = ExitStack()
    with ctx:
        def sb(name, shape, dt=fp32):
            return ctx.enter_context(nc.sbuf_tensor(name, shape, dt))

        def sem(name):
            return ctx.enter_context(nc.semaphore(name))

        banks = [ctx.enter_context(nc.psum_tensor(f"bank{i}", [P, 512], fp32)) for i in range(8)]

        x_sb = sb("x_sb", [P, TILES, D])
        xn_sb = sb("xn_sb", [P, TILES, D])

        ident = sb("ident", [P, P])
        before_bf = sb("before_bf", [P, P], bf16)
        ones_bf = sb("ones_bf", [P, P], bf16)
        upto = sb("upto", [P, P])
        after = sb("after", [P, P])
        ones = sb("ones", [P, P])
        rank8 = sb("rank8", [P, E])
        earlier8 = sb("earlier8", [P, E, E])
        thresh = sb("thresh", [P, N // T])
        slot_no = sb("slot_no", [P, SLOTS_MAX])
        part_no = sb("part_no", [P, 1])
        eps_sb = sb("eps_sb", [P, 1])

        rw_sb = sb("rw_sb", [D, E])

        wc = [sb("wc_high", [D, CONV_K, CONV], f32r), sb("wc_low", [D, CONV_K, CONV], f32r)]
        wz = [sb("wz_high", [D, ZW], f32r), sb("wz_low", [D, ZW], f32r)]
        conv_b = sb("conv_b", [P, CH])
        w_out = sb("w_out", [P, 2, D])
        dt_bias = sb("dt_bias", [P, HEADS])
        neg_a = sb("neg_a", [P, HEADS])
        d_skip = sb("d_skip", [P, HEADS])

        w_dram = nc.dram_tensor("w_split", (E * P, 2 * WROW), fp32, kind="Internal").ap()
        xd_dram = nc.dram_tensor("x_dispatched", (ROWS, D), fp32, kind="Internal").ap()
        yd_dram = nc.dram_tensor("y_dispatched", (ROWS, D), fp32, kind="Internal").ap()

        s_x = sem("x_loaded")
        s_raw = [sem("raw_loaded0"), sem("raw_loaded1")]
        s_split = sem("weights_split")
        s_wst = [sem("weights_stored0"), sem("weights_stored1")]
        s_zero = sem("zero_made")
        s_init = sem("dispatch_cleared")
        s_cst = sem("constants_chain")
        with (nc.sbuf_tensor("w_raw", [P, 2, WROW], fp32) as w_raw, nc.sbuf_tensor("w_out0", [P, 2 * WROW], f32r) as w_out0,
              nc.sbuf_tensor("w_out1", [P, 2 * WROW], f32r) as w_out1, nc.Block() as block):
            w_slot = [w_out0, w_out1]

            @block.sync
            def _(sp):
                sp.dma_start(x_sb[:], io["x"].rearrange("(t p) d -> p t d", p=P)).then_inc(s_x, 16)
                sp.dma_start(rw_sb[:], io["router_wT"]).then_inc(s_x, 16)
                for e in range(E):
                    if e >= 2:
                        sp.wait_ge(s_split, e - 1)
                    raw = w_raw[:, e % 2, :]
                    sp.dma_start(raw[:, 0:H], io["w_gate"][e]).then_inc(s_raw[e % 2], 16)
                    sp.dma_start(raw[:, H:2 * H], io["w_up"][e]).then_inc(s_raw[e % 2], 16)
                    sp.dma_start(raw[:, 2 * H:].rearrange("p (c d) -> p c d", c=2),
                                 io["w_down"][e].rearrange("(c p) d -> p c d", p=P)).then_inc(s_raw[e % 2], 16)
                sp.wait_ge(s_x, 32)

            @block.scalar
            def _(act):
                act.wait_ge(s_zero, 1)
                zsrc = xn_sb[:, 0:ROWS // P // 4, :]
                for k in range(4):
                    q = ROWS // 4
                    act.dma_start(xd_dram[k * q:(k + 1) * q, :].rearrange("(p t) d -> p t d", p=P),
                                  zsrc).then_inc(s_init, 16)
                for e in range(E):
                    act.wait_ge(s_split, e + 1)
                    act.dma_start(w_dram[e * P:(e + 1) * P, :], w_slot[e % 2][:].bitcast(fp32)).then_inc(s_wst[e % 2], 16)
                act.wait_ge(s_init, 64)
                act.wait_ge(s_wst[0], 16 * E // 2)
                act.wait_ge(s_wst[1], 16 * E // 2)

            @block.vector
            def _(dve):
                nc.vector.memset(xn_sb[:, 0:ROWS // P // 4, :], 0.0).then_inc(s_zero, 1)
                hi_done = sem("weights_high")
                for e in range(E):
                    dve.wait_ge(s_raw[e % 2], 48 * (e // 2 + 1))
                    if e >= 2:
                        dve.wait_ge(s_wst[e % 2], 16 * (e // 2))
                    w = w_slot[e % 2]
                    nc.vector.tensor_copy(w[:, 0:WROW], w_raw[:, e % 2, :]).then_inc(hi_done, 1)
                    dve.wait_ge(hi_done, e + 1)
                    nc.vector.tensor_tensor(w[:, WROW:], w_raw[:, e % 2, :], w[:, 0:WROW].bitcast(fp32),
                                            ALU.subtract).then_inc(s_split, 1)

            @block.gpsimd
            def _(pool):
                c = Chain(pool, s_cst)
                nc.gpsimd.memset(ones[:], 1.0)
                nc.gpsimd.memset(ones_bf[:], 1.0)
                nc.gpsimd.memset(ident[:], 0.0)
                nc.gpsimd.memset(eps_sb[:], LN_EPS)
                c(nc.gpsimd.memset(earlier8[:], 1.0))
                up = dict(pattern=[[1, P]], base=0, channel_multiplier=-1, fill=0.0)
                nc.gpsimd.affine_select(out=before_bf[:], in_=ones_bf[:], compare_op=ALU.is_gt, **up)
                nc.gpsimd.affine_select(out=upto[:], in_=ones[:], compare_op=ALU.is_ge, **up)
                nc.gpsimd.affine_select(out=after[:], in_=ones[:], compare_op=ALU.is_gt, pattern=[[-1, P]], base=0,
                                        channel_multiplier=1, fill=0.0)
                nc.gpsimd.affine_select(out=ident[:], in_=ident[:], compare_op=ALU.not_equal, pattern=[[-1, P]],
                                        base=0, channel_multiplier=1, fill=1.0)
                nc.gpsimd.affine_select(out=earlier8[:], in_=earlier8[:], compare_op=ALU.is_gt,
                                        pattern=[[1, E], [-1, E]], base=0, channel_multiplier=0, fill=0.0)
                io_ = dict(allow_small_or_imprecise_dtypes=True)
                nc.gpsimd.iota(rank8[:], pattern=[[-1, E]], base=E, channel_multiplier=0, **io_)
                nc.gpsimd.iota(thresh[:], pattern=[[T, N // T]], base=0, channel_multiplier=0, **io_)
                nc.gpsimd.iota(slot_no[:], pattern=[[1, SLOTS_MAX]], base=0, channel_multiplier=0, **io_)
                c(nc.gpsimd.iota(part_no[:], pattern=[[0, 1]], base=0, channel_multiplier=1, **io_))

        gate = sb("gate", [P, 2, TILES])
        w_rows = sb("w_rows", [P, SLOTS_MAX], i32)
        row = [sb("row1", [P, TILES], i32), sb("row2", [P, TILES], i32)]

        def route(tag):
            with ExitStack() as tmp:
                route_in(tag, lambda name, shape, dt=fp32: tmp.enter_context(nc.sbuf_tensor(f"{tag}_{name}", shape, dt)))

        def route_in(tag, tb):
            stats = tb("stats", [P, TILES, 6])
            mv = tb("mv", [P, TILES, 2])
            rstd = tb("rstd", [P, TILES])
            sd = tb("sd", [P, TILES])
            xT = [tb(f"xT{i}", [D, 512]) for i in range(2)]
            logit = tb("logit", [P, TILES, E])
            sel = [tb("sel1", [P, TILES, E]), tb("sel2", [P, TILES, E])]
            best = tb("best", [P, 2, TILES])
            gsum = tb("gsum", [P, TILES])
            work = tb("work", [P, TILES, E])
            work2 = tb("work2", [P, TILES])
            selb = tb("selb", [P, TILES, E], bf16)
            count = [tb("count0", [P, TILES, E]), tb("count1", [P, TILES, E])]
            cmp16 = tb("cmp16", [P, E, N // T])
            need = tb("need", [P, E])
            cmp8 = tb("cmp8", [P, E, E])
            first = tb("first", [P, E])
            cmpslot = tb("cmpslot", [P, SLOTS_MAX, E])
            expert = tb("expert", [P, SLOTS_MAX])
            QN = TILES // 4
            s_st = sem(f"{tag}_stats")
            s_mv = sem(f"{tag}_moments")
            s_sd = sem(f"{tag}_deviation")
            s_rs = sem(f"{tag}_rstd")
            s_xn = sem(f"{tag}_normed")
            s_tr = sem(f"{tag}_transposed")
            s_xT = sem(f"{tag}_xT_in_sbuf")
            s_lg = sem(f"{tag}_logits_made")
            s_lc = sem(f"{tag}_logits_copied")
            s_ch = sem(f"{tag}_chain")
            s_best = sem(f"{tag}_best_found")
            s_gt = sem(f"{tag}_sigmoid")
            s_selb = sem(f"{tag}_selected")
            s_cnt = sem(f"{tag}_counted")
            s_row = sem(f"{tag}_rows_known")
            s_sent = sem(f"{tag}_rows_sent")
            with nc.Block() as block:
                @block.vector
                def _(dve):
                    with dve.Fori(0, TILES) as t:
                        nc.vector.bn_stats(stats[:, ds(t, 1), :], x_sb[:, ds(t, 1), :]).then_inc(s_st, 1)
                    dve.wait_ge(s_st, TILES)
                    for t in range(TILES):
                        last = nc.vector.bn_aggr(mv[:, t, :], stats[:, t, :])
                    last.then_inc(s_mv, 1)
                    dve.wait_ge(s_sd, 1)
                    nc.vector.reciprocal(rstd[:], sd[:]).then_inc(s_rs, 1)
                    dve.wait_ge(s_rs, 1)

                    def norm(q):
                        for j in range(4):
                            last = nc.vector.tensor_scalar(xn_sb[:, ds(q * 4 + j, 1), :], x_sb[:, ds(q * 4 + j, 1), :],
                                                           mv[:, ds(q * 4 + j, 1), 0], rstd[:, ds(q * 4 + j, 1)],
                                                           ALU.subtract, ALU.mult)
                        last.then_inc(s_xn, 1)

                    def take_logits(q, s):
                        dve.wait_ge(s_lg, q + 1)
                        nc.vector.tensor_copy(logit[:, ds(q * 4, 4), :],
                                              banks[2 + s][:, 0:4 * E].rearrange("p (j e) -> p j e", e=E)).then_inc(s_lc, 1)

                    norm(0)
                    norm(1)
                    with dve.Fori(0, QN // 2 - 1) as i:
                        for s in range(2):
                            norm(2 * i + 2 + s)
                            take_logits(2 * i + s, s)
                    take_logits(QN - 2, 0)
                    take_logits(QN - 1, 1)
                    dve.wait_ge(s_lc, QN)

                    c = Chain(dve, s_ch)
                    lg = logit
                    full = [P, TILES, E]
                    for k in range(2):
                        c(nc.vector.tensor_reduce(best[:, k, :], lg[:], AX.X, ALU.max))
                        c(nc.vector.tensor_tensor(work[:], lg[:], bc(best[:, k, :].unsqueeze(2), full), ALU.is_equal))
                        c(nc.vector.tensor_tensor(work[:], work[:], bc(rank8[:].unsqueeze(1), full), ALU.mult))
                        c(nc.vector.tensor_reduce(work2[:], work[:], AX.X, ALU.max))
                        c(nc.vector.tensor_tensor(sel[k][:], work[:], bc(work2[:].unsqueeze(2), full), ALU.is_equal))
                        if k == 0:
                            c(nc.vector.scalar_tensor_tensor(out=logit[:], in0=sel[0][:], scalar=-3e38, in1=logit[:],
                                                             op0=ALU.mult, op1=ALU.add))
                    nc.vector.engine_nop().then_inc(s_best, 1) if False else None
                    nc.vector.tensor_tensor(selb[:], sel[0][:], sel[1][:], ALU.add).then_inc(s_selb, 1)

                    dve.wait_ge(s_cnt, 1)
                    tot = banks[1].rearrange("p (t e) -> p t e", e=E)
                    c(nc.vector.tensor_copy(count[0][:], tot))
                    a, b = count
                    step = 1
                    while step < TILES:
                        c(nc.vector.tensor_copy(b[:, 0:step, :], a[:, 0:step, :]))
                        c(nc.vector.tensor_tensor(b[:, step:, :], a[:, step:, :], a[:, 0:TILES - step, :], ALU.add))
                        a, b = b, a
                        step *= 2
                    n16 = [P, E, N // T]
                    c(nc.vector.tensor_tensor(cmp16[:], bc(a[:, TILES - 1, :].unsqueeze(2), n16),
                                              bc(thresh[:].unsqueeze(1), n16), ALU.is_gt))
                    c(nc.vector.tensor_reduce(need[:], cmp16[:], AX.X, ALU.add))
                    c(nc.vector.tensor_tensor(cmp8[:], bc(need[:].unsqueeze(1), [P, E, E]), earlier8[:], ALU.mult))
                    c(nc.vector.tensor_reduce(first[:], cmp8[:], AX.X, ALU.add))
                    ns = [P, SLOTS_MAX, E]
                    c(nc.vector.tensor_tensor(cmpslot[:], bc(slot_no[:].unsqueeze(2), ns), bc(first[:].unsqueeze(1), ns),
                                              ALU.is_ge))
                    c(nc.vector.tensor_reduce(expert[:], cmpslot[:], AX.X, ALU.add))
                    c(nc.vector.tensor_scalar(expert[:], expert[:], -1.0, float(P), ALU.add, ALU.mult))
                    c(nc.vector.tensor_scalar(w_rows[:], expert[:], part_no[:, 0:1], None, ALU.add))
                    c(nc.vector.tensor_tensor(a[:], a[:], tot, ALU.subtract))
                    c(nc.vector.tensor_tensor(a[:], a[:], banks[0].rearrange("p (t e) -> p t e", e=E), ALU.add))
                    c(nc.vector.tensor_scalar(first[:], first[:], float(T), None, ALU.mult))
                    c(nc.vector.tensor_tensor(a[:], a[:], bc(first[:].unsqueeze(1), full), ALU.add))
                    for k in range(2):
                        c(nc.vector.tensor_tensor(work[:], a[:], sel[k][:], ALU.mult))
                        c(nc.vector.tensor_reduce(work2[:], work[:], AX.X, ALU.add))
                        c(nc.vector.tensor_copy(row[k][:], work2[:]))
                    nc.vector.tensor_copy(gsum[:], work2[:]).then_inc(s_row, 1)
                    dve.wait_ge(s_gt, 1)
                    dve.wait_ge(s_row, 1)
                    c(nc.vector.tensor_tensor(gsum[:], gate[:, 0, :], gate[:, 1, :], ALU.add))
                    c(nc.vector.tensor_scalar(gsum[:], gsum[:], 1e-10, None, ALU.add))
                    c(nc.vector.reciprocal(gsum[:], gsum[:]))
                    for k in range(2):
                        c(nc.vector.scalar_tensor_tensor(out=gate[:, k, :], in0=gate[:, k, :], scalar=0.5, in1=gsum[:],
                                                         op0=ALU.mult, op1=ALU.mult))

                @block.scalar
                def _(act):
                    act.wait_ge(s_mv, 1)
                    nc.scalar.activation(sd[:], mv[:, :, 1], ACT.Sqrt, bias=eps_sb[:, 0:1]).then_inc(s_sd, 1)
                    with act.Fori(0, QN // 2) as i:
                        for s in range(2):
                            act.wait_ge(s_tr, 2 * i + s + 1)
                            nc.scalar.activation(xT[s][:], banks[s][:], ACT.Copy).then_inc(s_xT, 1)
                    act.wait_ge(s_selb, 1)
                    nc.scalar.activation(gate[:], best[:], ACT.Sigmoid).then_inc(s_gt, 1)

                @block.tensor
                def _(pe):
                    def turn(q, s):
                        pe.wait_ge(s_xn, q + 1)
                        for j in range(4):
                            last = pe.transpose(banks[s][:, j * P:(j + 1) * P], xn_sb[:, 4 * q + j, :], ident[:])
                        last.then_inc(s_tr, 1)

                    def logits(q, s):
                        pe.wait_ge(s_xT, q + 1)
                        if q >= 2:
                            pe.wait_ge(s_lc, q - 1)
                        for j in range(4):
                            last = pe.matmul(banks[2 + s][:, j * E:(j + 1) * E], xT[s][:, j * P:(j + 1) * P], rw_sb[:],
                                             start=True, stop=True)
                        last.then_inc(s_lg, 1)

                    turn(0, 0)
                    turn(1, 1)
                    for q in range(QN):
                        logits(q, q % 2)
                        if q + 2 < QN:
                            turn(q + 2, q % 2)
                    pe.wait_ge(s_selb, 1)
                    flat = selb[:].rearrange("p t e -> p (t e)")
                    pe.matmul(banks[0][:], before_bf[:], flat, start=True, stop=True)
                    pe.matmul(banks[1][:], ones_bf[:], flat, start=True, stop=True).then_inc(s_cnt, 1)

                @block.gpsimd
                def _(pool):
                    pool.wait_ge(s_row, 1)
                    for t in range(TILES):
                        for k in range(2):
                            pool.indirect_dma_start(out=xd_dram, out_offset=bass.IndirectOffsetOnAxis(ap=row[k][:, t:t + 1], axis=0),
                                                    in_=xn_sb[:, t, :], in_offset=None).then_inc(s_sent, 16)
                    pool.wait_ge(s_sent, 16 * 2 * TILES)

        def experts(tag):
            with ExitStack() as tmp:
                experts_in(tag, lambda name, shape, dt=fp32: tmp.enter_context(nc.sbuf_tensor(f"{tag}_{name}", shape, dt)))

        def experts_in(tag, tb):
            w_slot = [tb(f"w_slot{i}", [P, 2 * WROW], f32r) for i in range(2)]
            xr = [tb(f"xr{i}", [P, 4, D]) for i in range(2)]
            xh = [tb(f"xh{i}", [D, T], f32r) for i in range(2)]
            xl = [tb(f"xl{i}", [D, T], f32r) for i in range(2)]
            sg = [tb(f"sg{i}", [P, T]) for i in range(2)]
            hf = [tb(f"hf{i}", [P, T]) for i in range(2)]
            hh = [[tb(f"hh{i}{c}", [P, T], f32r) for c in range(2)] for i in range(2)]
            hl = [[tb(f"hl{i}{c}", [P, T], f32r) for c in range(2)] for i in range(2)]
            oT = tb("oT", [D, T])
            yr = [tb(f"yr{i}", [P, 4, D]) for i in range(2)]
            s_w = [sem(f"{tag}_weights_in{i}") for i in range(2)]
            s_xr = [sem(f"{tag}_rows_in{i}") for i in range(2)]
            s_tr = sem(f"{tag}_x_turned")
            s_xh = sem(f"{tag}_x_high")
            s_xl = sem(f"{tag}_x_low")
            s_gu = sem(f"{tag}_gate_up")
            s_sg = sem(f"{tag}_silu")
            s_hf = sem(f"{tag}_hidden")
            s_hh = sem(f"{tag}_hidden_high")
            s_hl = sem(f"{tag}_hidden_low")
            s_dn = sem(f"{tag}_down")
            s_oT = sem(f"{tag}_down_copied")
            s_ot = sem(f"{tag}_out_turned")
            s_yr = sem(f"{tag}_out_rows")
            s_yo = [sem(f"{tag}_out_stored{i}") for i in range(2)]
            xd = xd_dram.rearrange("(t p j) d -> t p j d", p=P, j=4)
            yd = yd_dram.rearrange("(t p j) d -> t p j d", p=P, j=4)
            b_x, b_g, b_u, b_d, b_o = banks[0], banks[1:3], banks[3:5], banks[5], banks[6]
            LAST = SLOTS_MAX - 1

            with nc.Block() as block:
                @block.gpsimd
                def _(pool):
                    for t in range(SLOTS_MAX):
                        if t >= 2:
                            pool.wait_ge(s_dn, t - 1)
                        pool.indirect_dma_start(out=w_slot[t % 2][:].bitcast(fp32), out_offset=None, in_=w_dram,
                                                in_offset=bass.IndirectOffsetOnAxis(ap=w_rows[:, t:t + 1], axis=0)
                                                ).then_inc(s_w[t % 2], 16)

                @block.sync
                def _(sp):
                    def load(t, s):
                        sp.dma_start(xr[s][:], xd[ds(t, 1)].rearrange("o p j d -> (o p) j d")).then_inc(s_xr[s], 16)

                    def store(t, s):
                        sp.wait_ge(s_yr, t + 1)
                        sp.dma_start(yd[ds(t, 1)].rearrange("o p j d -> (o p) j d"), yr[s][:]).then_inc(s_yo[s], 16)

                    load(0, 0)
                    load(1, 1)
                    for t in range(2, SLOTS_MAX):
                        sp.wait_ge(s_tr, t - 1)
                        load(t, t % 2)
                        store(t - 2, t % 2)
                    store(LAST - 1, (LAST - 1) % 2)
                    store(LAST, LAST % 2)
                    for s in range(2):
                        sp.wait_ge(s_yo[s], 16 * ((SLOTS_MAX + 1 - s) // 2))

                @block.tensor
                def _(pe):
                    def turn(t, s, half):
                        pe.wait_ge(s_xr[s], 16 * (half + 1))
                        if not isinstance(t, int) or t >= 1:
                            pe.wait_ge(s_xl, t)
                        for j in range(4):
                            last = pe.transpose(b_x[:, j * P:(j + 1) * P], xr[s][:, j, :], ident[:])
                        last.then_inc(s_tr, 1)

                    def gate_up(t, s, half, later):
                        w = w_slot[s]
                        pe.wait_ge(s_w[s], 16 * (half + 1))
                        pe.wait_ge(s_xl, t + 1)
                        for c in range(2):
                            if later:
                                pe.wait_ge(s_hf, 2 * t - 1 + c)
                            for bank, at in ((b_g[c], c * P), (b_u[c], H + c * P)):
                                high, low = w[:, at:at + P], w[:, WROW + at:WROW + at + P]
                                pe.matmul(bank[:], high, xh[s][:], start=True, stop=False)
                                pe.matmul(bank[:], high, xl[s][:], start=False, stop=False)
                                last = pe.matmul(bank[:], low, xh[s][:], start=False, stop=True)
                            last.then_inc(s_gu, 1)

                    def down(t, s, later):
                        w = w_slot[s]
                        if later:
                            pe.wait_ge(s_oT, t)
                        for c in range(2):
                            pe.wait_ge(s_hl, 2 * t + c + 1)
                            at = 2 * H + c * D
                            high, low = w[:, at:at + D], w[:, WROW + at:WROW + at + D]
                            pe.matmul(b_d[:], high, hh[s][c][:], start=(c == 0), stop=False)
                            pe.matmul(b_d[:], high, hl[s][c][:], start=False, stop=False)
                            last = pe.matmul(b_d[:], low, hh[s][c][:], start=False, stop=(c == 1))
                        last.then_inc(s_dn, 1)

                    def turn_out(t, later):
                        pe.wait_ge(s_oT, t + 1)
                        if later:
                            pe.wait_ge(s_yr, t)
                        for j in range(4):
                            last = pe.transpose(b_o[:, j * P:(j + 1) * P], oT[:, j * P:(j + 1) * P], ident[:])
                        last.then_inc(s_ot, 1)

                    turn(0, 0, 0)
                    for t in range(SLOTS_MAX):
                        s = t % 2
                        gate_up(t, s, t // 2, t >= 1)
                        if t < LAST:
                            turn(t + 1, 1 - s, (t + 1) // 2)
                        if t >= 1:
                            turn_out(t - 1, t >= 2)
                        down(t, s, t >= 1)
                    turn_out(LAST, True)

                @block.scalar
                def _(act):
                    def x_high(t, s, later):
                        act.wait_ge(s_tr, t + 1)
                        if later:
                            act.wait_ge(s_gu, 2 * t - 2)
                        nc.scalar.activation(xh[s][:], b_x[:], ACT.Copy).then_inc(s_xh, 1)

                    def silu(t, later):
                        for c in range(2):
                            act.wait_ge(s_gu, 2 * t + c + 1)
                            if later:
                                act.wait_ge(s_hf, 2 * t - 1 + c)
                            nc.scalar.activation(sg[c][:], b_g[c][:], ACT.Silu).then_inc(s_sg, 1)

                    def out_copies(t, s, later, later2):
                        act.wait_ge(s_dn, t + 1)
                        if later:
                            act.wait_ge(s_ot, t)
                        nc.scalar.activation(oT[:], b_d[:], ACT.Copy).then_inc(s_oT, 1)
                        act.wait_ge(s_ot, t + 1)
                        if later2:
                            act.wait_ge(s_yo[s], later2)
                        nc.scalar.activation(yr[s][:].rearrange("p j d -> p (j d)"), b_o[:], ACT.Copy).then_inc(s_yr, 1)

                    x_high(0, 0, False)
                    for t in range(SLOTS_MAX):
                        s = t % 2
                        silu(t, t >= 1)
                        if t < LAST:
                            x_high(t + 1, 1 - s, t + 1 >= 2)
                        if t >= 1:
                            out_copies(t - 1, 1 - s, t >= 2, 16 * ((t - 1) // 2))
                    out_copies(LAST, LAST % 2, True, 16 * (LAST // 2))

                @block.vector
                def _(dve):
                    def x_low(t, s):
                        dve.wait_ge(s_xh, t + 1)
                        nc.vector.tensor_tensor(xl[s][:], b_x[:], xh[s][:].bitcast(fp32), ALU.subtract).then_inc(s_xl, 1)

                    def hidden(t, s, later):
                        for c in range(2):
                            dve.wait_ge(s_sg, 2 * t + c + 1)
                            nc.vector.tensor_tensor(hf[c][:], sg[c][:], b_u[c][:], ALU.mult).then_inc(s_hf, 1)
                        if later:
                            dve.wait_ge(s_dn, t - 1)
                        for c in range(2):
                            dve.wait_ge(s_hf, 2 * t + c + 1)
                            nc.vector.tensor_copy(hh[s][c][:], hf[c][:]).then_inc(s_hh, 1)
                        for c in range(2):
                            dve.wait_ge(s_hh, 2 * t + c + 1)
                            nc.vector.tensor_tensor(hl[s][c][:], hf[c][:], hh[s][c][:].bitcast(fp32),
                                                    ALU.subtract).then_inc(s_hl, 1)

                    x_low(0, 0)
                    for t in range(SLOTS_MAX):
                        s = t % 2
                        hidden(t, s, t >= 2)
                        if t < LAST:
                            x_low(t + 1, 1 - s)

        def prepare_mixer():
            s_in = sem("mixer_weights_in")
            s_ln = sem("mixer_bias_in")
            s_c = sem("mixer_weights_chain")
            s_a = sem("mixer_a_exp")
            s_al = sem("mixer_a_clamped")
            with ExitStack() as tmp:
                w_in = tmp.enter_context(nc.sbuf_tensor("w_in", [D, ZW + CONV], fp32))
                cw = tmp.enter_context(nc.sbuf_tensor("conv_w_rows", [D, CONV_K, CONV], fp32))
                scaled = tmp.enter_context(nc.sbuf_tensor("w_scaled", [D, CONV_K, CONV], fp32))
                norm_w = tmp.enter_context(nc.sbuf_tensor("norm_w", [P, 2], fp32))
                block = tmp.enter_context(nc.Block())

                @block.sync
                def _(sp):
                    sp.dma_start(w_in[:], io["W_in"]).then_inc(s_in, 16)
                    sp.dma_start(cw[:], io["conv_wT"].partition_broadcast(P)).then_inc(s_in, 16)
                    sp.dma_start(conv_b[:], io["conv_bT"]).then_inc(s_in, 16)
                    sp.dma_start(w_out[:], io["W_out"].rearrange("(c p) d -> p c d", p=P)).then_inc(s_in, 16)
                    sp.dma_start(norm_w[:], io["norm_wT"]).then_inc(s_in, 16)
                    sp.dma_start(dt_bias[:], io["dt_bias"].partition_broadcast(P)).then_inc(s_in, 16)
                    sp.dma_start(neg_a[:], io["A_log"].partition_broadcast(P)).then_inc(s_in, 16)
                    sp.dma_start(d_skip[:], io["D"].partition_broadcast(P)).then_inc(s_in, 16)

                @block.scalar
                def _(act):
                    act.wait_ge(s_al, 1)
                    nc.scalar.activation(neg_a[:], neg_a[:], ACT.Exp).then_inc(s_a, 1)

                @block.vector
                def _(dve):
                    c = Chain(dve, s_c)
                    dve.wait_ge(s_in, 16 * 8)
                    nc.vector.tensor_scalar(neg_a[:], neg_a[:], 88.0, None, ALU.min).then_inc(s_al, 1)
                    for k in range(CONV_K):
                        c(nc.vector.tensor_tensor(scaled[:, k, :], w_in[:, INNER:INNER + CONV], cw[:, k, :], ALU.mult))
                    c(nc.vector.tensor_copy(wc[0][:], scaled[:]))
                    c(nc.vector.tensor_tensor(wc[1][:], scaled[:], wc[0][:].bitcast(fp32), ALU.subtract))
                    for to, of in ((slice(0, INNER), slice(0, INNER)), (slice(INNER, ZW), slice(INNER + CONV, ZW + CONV))):
                        c(nc.vector.tensor_copy(wz[0][:, to], w_in[:, of]))
                        c(nc.vector.tensor_tensor(wz[1][:, to], w_in[:, of], wz[0][:, to].bitcast(fp32), ALU.subtract))
                    for k in range(2):
                        c(nc.vector.tensor_scalar(w_out[:, k, :], w_out[:, k, :], norm_w[:, k:k + 1], None, ALU.mult))
                    dve.wait_ge(s_a, 1)
                    c(nc.vector.tensor_scalar(neg_a[:], neg_a[:], -1.0, None, ALU.mult))

        def mixer(tmp):
            def tb(name, shape, dt=fp32):
                return tmp.enter_context(nc.sbuf_tensor(name, shape, dt))

            y_in = [[tb(f"y_in{i}{k}", [P, D]) for k in range(2)] for i in range(4)]
            xTb = [tb("xT_high", [D, 4 + SEQ], f32r), tb("xT_low", [D, 4 + SEQ], f32r)]
            cT = [[tb(f"cT{s}{k}", [P, SEQ]) for k in range(CH)] for s in range(2)]
            zr = [tb(f"z{s}", [P, CT, ZW]) for s in range(2)]
            dt = [tb(f"dt{s}", [P, CT, HEADS]) for s in range(2)]
            da = [tb(f"da{s}", [P, CT, HEADS]) for s in range(2)]
            e1 = tb("softplus_e", [P, CT, HEADS])
            e2 = tb("softplus_s", [P, CT, HEADS])
            e3 = tb("softplus_q", [P, CT, HEADS])
            tok = [tb(f"tok{i}", [P, INNER + STATE + 2 * HEADS]) for i in range(2)]
            exs = [tb(f"chunk_decay{i}", [P, 2 * HEADS]) for i in range(2)]
            dam = [tb(f"da_masked{i}", [P, HEADS, P]) for i in range(2)]
            seg = [tb(f"decay{i}", [P, HEADS, P]) for i in range(2)]
            gm = tb("g_masked", [P, P])
            mm = [tb(f"mix{i}", [P, HEADS, P]) for i in range(2)]
            xdt = [tb(f"x_dt{i}", [P, HEADS, HD]) for i in range(2)]
            xw = [tb(f"x_end{i}", [P, HEADS, HD]) for i in range(2)]
            xsd = [tb(f"x_skip{i}", [P, HEADS, HD]) for i in range(2)]
            state = tb("state", [STATE, HEADS, HD])
            y = [tb(f"y{i}", [P, HEADS, HD]) for i in range(2)]
            junk = tb("squares", [P, INNER])
            junk2 = tb("squares2", [P, D])
            yT = tb("yT", [P, INNER])
            ob = [tb(f"out_rows{s}", [P, CT, D]) for s in range(2)]
            ssq = [tb(f"ssq{s}", [P, CT]) for s in range(2)]
            ssq2 = [tb(f"ssq2{s}", [P, CT]) for s in range(2)]
            st = tb("ln_stats", [P, CT, 6])
            mvb = tb("ln_moments", [P, CT, 2])
            var = tb("ln_var", [P, CT])
            lnv = tb("ln_log", [P, CT])
            rsb = tb("ln_rstd", [P, CT])
            tn = tb("newton", [P, CT])
            lnv2 = tb("rms_log", [P, CT])
            var2 = tb("rms_var", [P, CT])
            stmp = tb("state_decayed", [STATE, HEADS, HD])
            r1 = tb("r1", [P, CT])
            r2 = tb("r2", [P, CT])

            b_acc, b_z, b_seg, b_g, b_tok, b_y, b_up = banks[0:2], banks[2], banks[3], banks[4], banks[5], banks[6], banks[7]

            s_yi = [sem(f"m_rows_back{i}") for i in range(4)]
            s_ya = sem("m_first_added")
            s_yb = sem("m_residual")
            s_bs = sem("m_ln_stats")
            s_lv = sem("m_ln_var")
            s_ll = sem("m_ln_log")
            s_lr = sem("m_ln_rstd")
            s_xn = sem("m_normed")
            s_tr = sem("m_turned")
            s_xh = sem("m_xT_high")
            s_xl = sem("m_xT_low")
            s_cv = sem("m_conv")
            s_ce = sem("m_conv_copied")
            s_z = sem("m_z")
            s_zc = sem("m_z_copied")
            s_si = sem("m_silu")
            s_sz = sem("m_silu_z")
            s_d0 = sem("m_dt_raw")
            s_d1 = sem("m_dt_exp")
            s_da = sem("m_da")
            s_dm = sem("m_da_masked")
            s_xd = sem("m_x_skip")
            s_tk = sem("m_tokens_turned")
            s_tc = sem("m_tokens_copied")
            s_g = sem("m_g")
            s_gm = sem("m_g_masked")
            s_sg = sem("m_segments")
            s_eg = sem("m_decays")
            s_mm = sem("m_mix")
            s_x1 = sem("m_x_dt")
            s_xw = sem("m_x_end")
            s_mid = sem("m_y_and_update")
            s_st = sem("m_state")
            s_yd = sem("m_y_read")
            s_y = sem("m_y")
            s_yt = sem("m_y_turned")
            s_yc = sem("m_y_copied")
            s_o = sem("m_out")
            s_oc = sem("m_out_copied")
            s_q1 = sem("m_ssq1")
            s_q2 = sem("m_ssq2")
            s_v1 = sem("m_rms_var")
            s_l1 = sem("m_rms_log")
            s_xa = sem("m_x_and_normed")
            s_x2 = sem("m_new_x")
            s_c = sem("m_chain")
            s_zz = sem("m_pad")

            B = BATCH
            CONVS = [1, 2, 1, 2, 1, 1, 0, 0]
            ZS = [2, 2, 2, 2, 0, 0, 0, 0]
            groups = [(k, h) for h in range(2) for k in range(CH)]

            with nc.Block() as block:
                @block.gpsimd
                def _(pool):
                    nc.gpsimd.memset(xTb[0][:, 0:4].bitcast(fp32), 0.0).then_inc(s_zz, 1)
                    nc.gpsimd.memset(xTb[1][:, 0:4].bitcast(fp32), 0.0).then_inc(s_zz, 1)

                    def gather(t):
                        if t >= 4:
                            pool.wait_ge(s_yb, t - 3)
                        for k in range(2):
                            pool.indirect_dma_start(out=y_in[t % 4][k][:], out_offset=None, in_=yd_dram,
                                                    in_offset=bass.IndirectOffsetOnAxis(ap=row[k][:, t:t + 1], axis=0)
                                                    ).then_inc(s_yi[t % 4], 16)

                    def mask(t):
                        b, c = divmod(t, CT)
                        pool.wait_ge(s_da, b + 1)
                        if t >= 2:
                            pool.wait_ge(s_sg, t - 1)
                        nc.gpsimd.tensor_tensor(dam[t % 2][:], bc(da[b % 2][:, c, :].unsqueeze(2), [P, HEADS, P]),
                                                bc(upto[:].unsqueeze(1), [P, HEADS, P]), ALU.mult).then_inc(s_dm, 1)

                    def skip(t):
                        pool.wait_ge(s_tc, t + 1)
                        if t >= 2:
                            pool.wait_ge(s_y, t - 1)
                        nc.gpsimd.tensor_tensor(xsd[t % 2][:], tok[t % 2][:, 0:INNER].rearrange("p (h d) -> p h d", d=HD),
                                                bc(d_skip[:].unsqueeze(2), [P, HEADS, HD]), ALU.mult).then_inc(s_xd, 1)

                    for t in range(2 * CT):
                        gather(t)
                    mask(0)
                    skip(0)
                    for t in range(TILES):
                        if t + 1 < TILES:
                            mask(t + 1)
                            skip(t + 1)
                        if t + 2 * CT < TILES:
                            gather(t + 2 * CT)
                        if t % CT == 2 and t >= CT:
                            pass

                @block.tensor
                def _(pe):
                    def turn(b):
                        pe.wait_ge(s_xn, b + 1)
                        for h in range(2):
                            if b or h:
                                pe.wait_ge(s_ce, 8 * b)
                            for j in range(4):
                                last = pe.transpose(b_acc[h][:, j * P:(j + 1) * P], xn_sb[:, CT * b + 4 * h + j, :], ident[:])
                            last.then_inc(s_tr, 1)

                    def conv(b, g):
                        n = 8 * b + g
                        k, h = groups[g]
                        pe.wait_ge(s_xl, 2 * b + 2)
                        if g >= 2:
                            pe.wait_ge(s_ce, n - 1)
                        acc = b_acc[n % 2]
                        i = 0
                        for tap in range(CONV_K):
                            at = 1 + tap + 512 * h
                            for w, x in ((0, 0), (0, 1), (1, 0)):
                                last = pe.matmul(acc[:], wc[w][:, tap, k * P:(k + 1) * P], xTb[x][:, at:at + 512],
                                                 start=(i == 0), stop=(i == 11))
                                i += 1
                        last.then_inc(s_cv, 1)

                    def zdt(b, c):
                        n = CT * b + c
                        pe.wait_ge(s_xl, 2 * b + 2)
                        z_bank_free(pe)
                        at = 4 + P * c
                        for i, (x, w) in enumerate(((0, 0), (0, 1), (1, 0))):
                            last = pe.matmul(b_z[:, 0:ZW], xTb[x][:, at:at + P], wz[w][:], start=(i == 0), stop=(i == 2))
                        last.then_inc(s_z, 1)
                        used[0] += 1

                    used = [0, 0]

                    def z_bank_free(pe):
                        if used[0]:
                            pe.wait_ge(s_zc, used[0])
                        if used[1]:
                            pe.wait_ge(s_q2, used[1])

                    def front(t):
                        b, c = divmod(t, CT)
                        cols = slice(c * P, (c + 1) * P)
                        cs = cT[b % 2]
                        pe.wait_ge(s_si, b + 1)
                        if t >= 1:
                            pe.wait_ge(s_eg, t)
                        for j, k in enumerate((0, 1, 2)):
                            pe.transpose(b_tok[:, j * P:(j + 1) * P], cs[k][:, cols], ident[:])
                        pe.wait_ge(s_da, b + 1)
                        at = INNER + STATE
                        pe.matmul(b_tok[:, at:at + HEADS], upto[:], da[b % 2][:, c, :], start=True, stop=True)
                        pe.matmul(b_tok[:, at + HEADS:at + 2 * HEADS], ones[:], da[b % 2][:, c, :], start=True,
                                  stop=True).then_inc(s_tk, 1)
                        if t >= 1:
                            pe.wait_ge(s_gm, t)
                        pe.matmul(b_g[:, 0:P], cs[2][:, cols], cs[3][:, cols], start=True, stop=True).then_inc(s_g, 1)
                        pe.wait_ge(s_dm, t + 1)
                        pe.matmul(b_seg[:], after[:], dam[t % 2][:].rearrange("p h i -> p (h i)"), start=True,
                                  stop=True).then_inc(s_sg, 1)

                    def mid(t):
                        b, c = divmod(t, CT)
                        i = t % 2
                        if t >= 1:
                            pe.wait_ge(s_yd, t)
                            pe.wait_ge(s_st, t)
                            pe.wait_ge(s_yc, t - 1) if t >= 2 else None
                        if c:
                            pe.matmul(b_y[:, INNER:], cT[b % 2][3][:, c * P:(c + 1) * P],
                                      state[:].rearrange("p h d -> p (h d)"), start=True, stop=True)
                        pe.wait_ge(s_mm, t + 1)
                        for h in range(HEADS):
                            pe.matmul(b_y[:, h * HD:(h + 1) * HD], mm[i][:, h, :], xdt[i][:, h, :], start=True, stop=True)
                        pe.wait_ge(s_xw, t + 1)
                        pe.matmul(b_up[:, 0:INNER], tok[i][:, INNER:INNER + STATE], xw[i][:].rearrange("p h d -> p (h d)"),
                                  start=True, stop=True).then_inc(s_mid, 1)

                    def turn_y(t):
                        pe.wait_ge(s_y, t + 1)
                        pe.wait_ge(s_st, t + 1)
                        for k in range(2):
                            last = pe.transpose(b_up[:, INNER + k * P:INNER + (k + 1) * P],
                                                y[t % 2][:].rearrange("p h d -> p (h d)")[:, k * P:(k + 1) * P], ident[:])
                        last.then_inc(s_yt, 1)

                    def project(t):
                        pe.wait_ge(s_yc, t + 1)
                        z_bank_free(pe)
                        for k in range(2):
                            last = pe.matmul(b_z[:, 0:D], yT[:, k * P:(k + 1) * P], w_out[:, k, :],
                                             start=(k == 0), stop=(k == 1))
                        last.then_inc(s_o, 1)
                        used[1] += 1

                    pe.wait_ge(s_zz, 2)
                    turn(0)
                    for g in range(8):
                        conv(0, g)
                    for c in range(CT):
                        zdt(0, c)
                    front(0)
                    for t in range(TILES):
                        b, c = divmod(t, CT)
                        more = b + 1 < B
                        if more and c == 0:
                            turn(b + 1)
                        if t + 1 < TILES:
                            front(t + 1)
                        if t >= 1:
                            turn_y(t - 1)
                        if more:
                            for g in range(sum(CONVS[:c]), sum(CONVS[:c + 1])):
                                conv(b + 1, g)
                        if t >= 1:
                            project(t - 1)
                        mid(t)
                        if more:
                            for k in range(sum(ZS[:c]), sum(ZS[:c + 1])):
                                zdt(b + 1, k)
                    turn_y(TILES - 1)
                    project(TILES - 1)

                @block.scalar
                def _(act):
                    def x_high(b):
                        for h in range(2):
                            act.wait_ge(s_tr, 2 * b + h + 1)
                            if b:
                                act.wait_ge(s_z, CT * b)
                                act.wait_ge(s_cv, 8 * b)
                            nc.scalar.activation(xTb[0][:, 4 + 512 * h:516 + 512 * h], b_acc[h][:], ACT.Copy).then_inc(s_xh, 1)

                    def conv_copy(b, g):
                        n = 8 * b + g
                        k, h = groups[g]
                        act.wait_ge(s_cv, n + 1)
                        nc.scalar.activation(cT[b % 2][k][:, 512 * h:512 * (h + 1)], b_acc[n % 2][:], ACT.Identity,
                                             bias=conv_b[:, k:k + 1]).then_inc(s_ce, 1)

                    def z_copy(b, c):
                        act.wait_ge(s_z, CT * b + c + 1)
                        nc.scalar.activation(zr[b % 2][:, c, :], b_z[:, 0:ZW], ACT.Copy).then_inc(s_zc, 1)

                    def silus(b):
                        act.wait_ge(s_ce, 8 * b + 8)
                        act.wait_ge(s_zc, CT * b + CT)
                        act.wait_ge(s_d0, b + 1)
                        for k in (2, 3, 0, 1):
                            last = nc.scalar.activation(cT[b % 2][k][:], cT[b % 2][k][:], ACT.Silu)
                        last.then_inc(s_si, 1)
                        nc.scalar.activation(zr[b % 2][:, :, 0:INNER], zr[b % 2][:, :, 0:INNER], ACT.Silu).then_inc(s_sz, 1)

                    def dt_exp(b):
                        act.wait_ge(s_d0, b + 1)
                        nc.scalar.activation(e2[:], e1[:], ACT.Exp, scale=-1.0).then_inc(s_d1, 1)

                    def ln_log(b):
                        act.wait_ge(s_lv, b + 1)
                        nc.scalar.activation(lnv[:], var[:], ACT.Ln).then_inc(s_ll, 1)
                        act.wait_ge(s_ll, 2 * b + 1)
                        nc.scalar.activation(rsb[:], lnv[:], ACT.Exp, scale=-0.5).then_inc(s_ll, 1)

                    def rms_log(b):
                        for k in range(2):
                            act.wait_ge(s_v1, 2 * b + k + 1)
                            nc.scalar.activation(lnv2[:], var2[:], ACT.Ln).then_inc(s_l1, 1)
                            act.wait_ge(s_l1, 4 * b + 2 * k + 1)
                            nc.scalar.activation((r1, r2)[k][:], lnv2[:], ACT.Exp, scale=-0.5).then_inc(s_l1, 1)

                    def front(t):
                        i = t % 2
                        act.wait_ge(s_tk, t + 1)
                        if t >= 2:
                            act.wait_ge(s_mid, t - 1)
                            act.wait_ge(s_y, t - 1)
                            act.wait_ge(s_xd, t - 1)
                        n = INNER + STATE
                        nc.scalar.activation(tok[i][:, 0:n], b_tok[:, 0:n], ACT.Copy).then_inc(s_tc, 1)
                        nc.scalar.activation(exs[i][:], b_tok[:, n:n + 2 * HEADS], ACT.Exp)
                        act.wait_ge(s_sg, t + 1)
                        nc.scalar.activation(seg[i][:].rearrange("p h i -> p (h i)"), b_seg[:], ACT.Exp).then_inc(s_eg, 1)

                    def y_copy(t):
                        act.wait_ge(s_yt, t + 1)
                        if t >= 1:
                            act.wait_ge(s_o, t)
                        nc.scalar.activation(yT[:], b_up[:, INNER:], ACT.Copy).then_inc(s_yc, 1)
                        if t % CT == 0 and t >= 2 * CT:
                            act.wait_ge(s_x2, t // CT - 1)
                        if t >= 1:
                            act.wait_ge(s_q1, t)
                        nc.scalar.activation(junk[:], y[t % 2][:].rearrange("p h d -> p (h d)"), ACT.Square,
                                             accum_out=ssq[t // CT % 2][:, t % CT:t % CT + 1]).then_inc(s_q1, 1)

                    def out_copy(t):
                        b, c = divmod(t, CT)
                        act.wait_ge(s_o, t + 1)
                        nc.scalar.activation(ob[b % 2][:, c, :], b_z[:, 0:D], ACT.Copy).then_inc(s_oc, 1)
                        if t >= 1:
                            act.wait_ge(s_q2, t)
                        nc.scalar.activation(junk2[:], b_z[:, 0:D], ACT.Square,
                                             accum_out=ssq2[b % 2][:, c:c + 1]).then_inc(s_q2, 1)

                    ln_log(0)
                    x_high(0)
                    for g in range(8):
                        conv_copy(0, g)
                    for c in range(CT):
                        z_copy(0, c)
                    silus(0)
                    dt_exp(0)
                    ln_log(1)
                    front(0)
                    for t in range(TILES):
                        b, c = divmod(t, CT)
                        more = b + 1 < B
                        if more and c == 0:
                            x_high(b + 1)
                        if t + 1 < TILES:
                            front(t + 1)
                        if t >= 1:
                            y_copy(t - 1)
                        if more:
                            for g in range(sum(CONVS[:c]), sum(CONVS[:c + 1])):
                                conv_copy(b + 1, g)
                        if t >= 1:
                            out_copy(t - 1)
                        if more:
                            for k in range(sum(ZS[:c]), sum(ZS[:c + 1])):
                                z_copy(b + 1, k)
                            if c == 5:
                                silus(b + 1)
                                dt_exp(b + 1)
                        if b >= 1 and c == 0:
                            rms_log(b - 1)
                        if c == 7 and b + 2 < B:
                            ln_log(b + 2)
                    y_copy(TILES - 1)
                    out_copy(TILES - 1)
                    rms_log(B - 1)

                @block.vector
                def _(dve):
                    ch = Chain(dve, s_c)

                    def newton(r, v, tmp_):
                        ch(nc.vector.tensor_tensor(tmp_[:], r[:], r[:], ALU.mult))
                        ch(nc.vector.tensor_tensor(tmp_[:], tmp_[:], v[:], ALU.mult))
                        ch(nc.vector.tensor_scalar(tmp_[:], tmp_[:], -0.5, 1.5, ALU.mult, ALU.add))
                        ch(nc.vector.tensor_tensor(r[:], r[:], tmp_[:], ALU.mult))

                    def residual(t):
                        c = t % CT
                        dve.wait_ge(s_yi[t % 4], 32 * (t // 4 + 1))
                        nc.vector.scalar_tensor_tensor(out=x_sb[:, t, :], in0=y_in[t % 4][0][:], scalar=gate[:, 0, t:t + 1],
                                                       in1=x_sb[:, t, :], op0=ALU.mult, op1=ALU.add).then_inc(s_ya, 1)
                        dve.wait_ge(s_ya, t + 1)
                        nc.vector.scalar_tensor_tensor(out=x_sb[:, t, :], in0=y_in[t % 4][1][:], scalar=gate[:, 1, t:t + 1],
                                                       in1=x_sb[:, t, :], op0=ALU.mult, op1=ALU.add).then_inc(s_yb, 1)
                        dve.wait_ge(s_yb, t + 1)
                        ch(nc.vector.bn_stats(st[:, c, :], x_sb[:, t, :]))

                    def ln_var(b):
                        for c in range(CT):
                            last = nc.vector.bn_aggr(mvb[:, c, :], st[:, c, :])
                        ch(last)
                        nc.vector.tensor_scalar(var[:], mvb[:, :, 1], LN_EPS, None, ALU.add).then_inc(s_lv, 1)

                    def normalise(b):
                        dve.wait_ge(s_ll, 2 * b + 2)
                        dve.wait_ge(s_lv, b + 1)
                        newton(rsb, var, tn)
                        for c in range(CT):
                            last = nc.vector.tensor_scalar(xn_sb[:, CT * b + c, :], x_sb[:, CT * b + c, :],
                                                           mvb[:, c, 0:1], rsb[:, c:c + 1], ALU.subtract, ALU.mult)
                        last.then_inc(s_xn, 1)
                        dve.wait_ge(s_xn, b + 1)

                    def x_low(b):
                        for h in range(2):
                            dve.wait_ge(s_xh, 2 * b + h + 1)
                            cols = slice(4 + 512 * h, 516 + 512 * h)
                            nc.vector.tensor_tensor(xTb[1][:, cols], b_acc[h][:], xTb[0][:, cols].bitcast(fp32),
                                                    ALU.subtract).then_inc(s_xl, 1)

                    def dt_raw(b):
                        z = zr[b % 2]
                        dve.wait_ge(s_zc, CT * b + CT)
                        d = dt[b % 2]
                        ch(nc.vector.tensor_tensor(d[:], z[:, :, INNER:], bc(dt_bias[:].unsqueeze(1), [P, CT, HEADS]), ALU.add))
                        ch(nc.vector.tensor_scalar(e3[:], d[:], -1.0, None, ALU.mult))
                        nc.vector.tensor_tensor(e1[:], d[:], e3[:], ALU.max).then_inc(s_d0, 1)

                    def dt_end(b):
                        d = dt[b % 2]
                        dve.wait_ge(s_d1, b + 1)
                        ch(nc.vector.tensor_scalar(e3[:], e2[:], 2.0, None, ALU.add))
                        ch(nc.vector.reciprocal(e3[:], e3[:]))
                        ch(nc.vector.tensor_tensor(e2[:], e2[:], e3[:], ALU.mult))
                        ch(nc.vector.tensor_tensor(e1[:], e2[:], e2[:], ALU.mult))
                        ch(nc.vector.tensor_scalar(e3[:], e1[:], 2.0 / 15, 2.0 / 13, ALU.mult, ALU.add))
                        for n in (11, 9, 7, 5, 3, 1):
                            ch(nc.vector.tensor_tensor(e3[:], e3[:], e1[:], ALU.mult))
                            ch(nc.vector.tensor_scalar(e3[:], e3[:], 2.0 / n, None, ALU.add))
                        ch(nc.vector.tensor_tensor(e3[:], e3[:], e2[:], ALU.mult))
                        ch(nc.vector.scalar_tensor_tensor(out=d[:], in0=d[:], scalar=0.0, in1=e3[:], op0=ALU.max, op1=ALU.add))
                        ch(nc.vector.tensor_tensor(da[b % 2][:], d[:], bc(neg_a[:].unsqueeze(1), [P, CT, HEADS]), ALU.mult))
                        nc.vector.tensor_scalar(da[b % 2][:], da[b % 2][:], FLOOR, None, ALU.max).then_inc(s_da, 1)
                        dve.wait_ge(s_da, b + 1)

                    def mix(t):
                        b, c = divmod(t, CT)
                        i = t % 2
                        dve.wait_ge(s_g, t + 1)
                        if t >= 1:
                            dve.wait_ge(s_mm, t)
                        nc.vector.tensor_tensor(gm[:], b_g[:, 0:P], upto[:], ALU.mult).then_inc(s_gm, 1)
                        dve.wait_ge(s_tc, t + 1)
                        if t >= 2:
                            dve.wait_ge(s_mid, t - 1)
                        hd = [P, HEADS, HD]
                        nc.vector.tensor_tensor(xdt[i][:], tok[i][:, 0:INNER].rearrange("p (h d) -> p h d", d=HD),
                                                bc(dt[b % 2][:, c, :].unsqueeze(2), hd), ALU.mult).then_inc(s_x1, 1)
                        dve.wait_ge(s_eg, t + 1)
                        dve.wait_ge(s_gm, t + 1)
                        nc.vector.tensor_tensor(mm[i][:], seg[i][:], bc(gm[:].unsqueeze(1), [P, HEADS, P]), ALU.mult
                                                ).then_inc(s_mm, 1)
                        dve.wait_ge(s_x1, t + 1)
                        nc.vector.tensor_tensor(xw[i][:], xdt[i][:], bc(seg[i][:, :, P - 1:P], hd), ALU.mult).then_inc(s_xw, 1)

                    def after_mid(t):
                        b, c = divmod(t, CT)
                        i = t % 2
                        hd = [P, HEADS, HD]
                        up = b_up[:, 0:INNER].rearrange("p (h d) -> p h d", d=HD)
                        yd, yo = (b_y[:, n * INNER:(n + 1) * INNER].rearrange("p (h d) -> p h d", d=HD) for n in range(2))
                        if c:
                            ch(nc.vector.tensor_tensor(stmp[:], state[:], bc(exs[i][:, HEADS:].unsqueeze(2), hd), ALU.mult))
                        dve.wait_ge(s_mid, t + 1)
                        if c:
                            nc.vector.tensor_tensor(state[:], stmp[:], up, ALU.add).then_inc(s_st, 1)
                        else:
                            nc.vector.tensor_copy(state[:], up).then_inc(s_st, 1)
                        if t >= 2:
                            dve.wait_ge(s_yt, t - 1)
                            dve.wait_ge(s_q1, t - 1)
                        dve.wait_ge(s_xd, t + 1)
                        if c:
                            ch(nc.vector.tensor_tensor(y[i][:], yo, bc(exs[i][:, 0:HEADS].unsqueeze(2), hd), ALU.mult))
                            ch(nc.vector.tensor_tensor(y[i][:], y[i][:], xsd[i][:], ALU.add))
                            nc.vector.tensor_tensor(y[i][:], y[i][:], yd, ALU.add).then_inc(s_yd, 1)
                        else:
                            nc.vector.tensor_tensor(y[i][:], xsd[i][:], yd, ALU.add).then_inc(s_yd, 1)
                        dve.wait_ge(s_yd, t + 1)
                        dve.wait_ge(s_sz, b + 1)
                        nc.vector.tensor_tensor(y[i][:], y[i][:], zr[b % 2][:, c, 0:INNER].rearrange("p (h d) -> p h d", d=HD),
                                                ALU.mult).then_inc(s_y, 1)
                        dve.wait_ge(s_st, t + 1)

                    def finish(b):
                        s = b % 2
                        dve.wait_ge(s_q1, CT * b + CT)
                        nc.vector.tensor_scalar(var2[:], ssq[s][:], 1.0 / INNER, LN_EPS, ALU.mult, ALU.add).then_inc(s_v1, 1)
                        dve.wait_ge(s_v1, 2 * b + 1)
                        dve.wait_ge(s_l1, 4 * b + 2)
                        newton(r1, var2, tn)
                        dve.wait_ge(s_q2, CT * b + CT)
                        ch(nc.vector.tensor_tensor(tn[:], r1[:], r1[:], ALU.mult))
                        ch(nc.vector.tensor_tensor(tn[:], tn[:], ssq2[s][:], ALU.mult))
                        nc.vector.tensor_scalar(var2[:], tn[:], 1.0 / D, LN_EPS, ALU.mult, ALU.add).then_inc(s_v1, 1)
                        dve.wait_ge(s_v1, 2 * b + 2)
                        dve.wait_ge(s_l1, 4 * b + 4)
                        newton(r2, var2, tn)
                        ch(nc.vector.tensor_tensor(r2[:], r1[:], r2[:], ALU.mult))
                        rows = slice(CT * b, CT * b + CT)
                        ch(nc.vector.tensor_tensor(x_sb[:, rows, :], x_sb[:, rows, :], xn_sb[:, rows, :], ALU.add))
                        for c in range(CT):
                            last = nc.vector.scalar_tensor_tensor(out=x_sb[:, CT * b + c, :], in0=ob[s][:, c, :],
                                                                  scalar=r2[:, c:c + 1], in1=x_sb[:, CT * b + c, :],
                                                                  op0=ALU.mult, op1=ALU.add)
                        last.then_inc(s_x2, 1)

                    for t in range(CT):
                        residual(t)
                    ln_var(0)
                    normalise(0)
                    x_low(0)
                    dt_raw(0)
                    dt_end(0)
                    for t in range(CT, 2 * CT):
                        residual(t)
                    ln_var(1)
                    normalise(1)
                    mix(0)
                    for t in range(TILES):
                        b, c = divmod(t, CT)
                        more = b + 1 < B
                        if more and c == 0:
                            x_low(b + 1)
                        if t + 1 < TILES:
                            mix(t + 1)
                        after_mid(t)
                        if b + 2 < B:
                            residual(t + 2 * CT)
                            if c == 7:
                                pass
                        if more and c == 4:
                            dt_raw(b + 1)
                        if more and c == 5:
                            dt_end(b + 1)
                        if b >= 1 and c == 0:
                            finish(b - 1)
                        if c == 7 and b + 2 < B:
                            ln_var(b + 2)
                            normalise(b + 2)
                    finish(B - 1)

        def combine_only(tag):
            y_in = [[sb(f"{tag}_y_in{i}{k}", [P, D]) for k in range(2)] for i in range(4)]
            s_y = [sem(f"{tag}_rows_back{i}") for i in range(4)]
            s_a = sem(f"{tag}_first_added")
            s_b = sem(f"{tag}_second_added")
            s_o = sem(f"{tag}_stored")
            with nc.Block() as block:
                @block.gpsimd
                def _(pool):
                    for t in range(TILES):
                        if t >= 4:
                            pool.wait_ge(s_b, t - 3)
                        for k in range(2):
                            pool.indirect_dma_start(out=y_in[t % 4][k][:], out_offset=None, in_=yd_dram,
                                                    in_offset=bass.IndirectOffsetOnAxis(ap=row[k][:, t:t + 1], axis=0)
                                                    ).then_inc(s_y[t % 4], 16)

                @block.vector
                def _(dve):
                    for t in range(TILES):
                        dve.wait_ge(s_y[t % 4], 32 * (t // 4 + 1))
                        nc.vector.scalar_tensor_tensor(out=x_sb[:, t, :], in0=y_in[t % 4][0][:], scalar=gate[:, 0, t:t + 1],
                                                       in1=x_sb[:, t, :], op0=ALU.mult, op1=ALU.add).then_inc(s_a, 1)
                        dve.wait_ge(s_a, t + 1)
                        nc.vector.scalar_tensor_tensor(out=x_sb[:, t, :], in0=y_in[t % 4][1][:], scalar=gate[:, 1, t:t + 1],
                                                       in1=x_sb[:, t, :], op0=ALU.mult, op1=ALU.add).then_inc(s_b, 1)

                @block.sync
                def _(sp):
                    for g in range(8):
                        sp.wait_ge(s_b, 8 * (g + 1))
                        sp.dma_start(out[g * SEQ:(g + 1) * SEQ, :].rearrange("(t p) d -> p t d", p=P),
                                     x_sb[:, 8 * g:8 * g + 8, :]).then_inc(s_o, 16)
                    sp.wait_ge(s_o, 128)

        prepare_mixer()
        route("r1")
        experts("f1")
        with ExitStack() as tmp:
            mixer(tmp)
        route("r2")
        experts("f2")
        combine_only("c2")


_INS = ['x', 'router_wT', 'w_gate', 'w_up', 'w_down', 'W_in', 'conv_wT', 'conv_bT', 'dt_bias', 'A_log', 'D', 'norm_wT', 'W_out']


def kernel(**inputs):
    import numpy as np
    import concourse.bacc as bacc
    from concourse.bass_utils import run_bass_kernel_spmd as run

    given = {k.replace("L0_attn_", "").replace("L0_ffn_", ""): np.asarray(v) for k, v in inputs.items()}
    given["x"] = given["x"].reshape(N, D)
    given["router_wT"] = given["router_w"].T
    given["conv_wT"] = given["conv_w"].T
    given["conv_bT"] = given["conv_b"].reshape(CH, P).T
    given["norm_wT"] = given["norm_w"].reshape(2, P).T
    nc = bacc.Bacc("TRN2", target_bir_lowering=False, num_devices=1)
    arrays, io = {}, {}
    for name in _INS:
        a = np.ascontiguousarray(given[name])
        arrays[f"in_{name}_dram"] = a
        io[name] = nc.dram_tensor(f"in_{name}_dram", a.shape, mybir.dt.from_np(a.dtype), kind="ExternalInput").ap()
    out = nc.dram_tensor("out_dram", (N, D), fp32, kind="ExternalOutput").ap()
    build(nc, io, out)
    r = run(nc, [arrays], core_ids=[0])
    return r.results[0]["out_dram"].reshape(BATCH, SEQ, D)
```

```python
import concourse.bass as bass
from concourse import mybir
from contextlib import ExitStack

P = 128
D = 128
BATCH, SEQ = 8, 1024
N = BATCH * SEQ
TILES = N // P
E = 8
H = 256
XB = 4
T = 512
SLOTS_MAX = 2 * N // T + E - 1
ROWS = SLOTS_MAX * T
REGION = N + T
WROW = 2 * H + 2 * D
LN_EPS = 1e-5
INNER = 2 * D
HEADS, HD = 4, 64
STATE = 128
CONV = INNER + 2 * STATE
CH = CONV // P
CONV_K = 4
ZW = INNER + HEADS
CT = SEQ // P
FLOOR = -110.0

fp32 = mybir.dt.float32
f32r = mybir.dt.float32r
bf16 = mybir.dt.bfloat16
i32 = mybir.dt.int32
ALU = mybir.AluOpType
ACT = mybir.ActivationFunctionType
AX = mybir.AxisListType
ds = bass.ds


class Chain:

    def __init__(self, eng, sem, base=0):
        self.eng, self.sem, self.base, self.n = eng, sem, base, 0

    def __call__(self, ins):
        ins.then_inc(self.sem, 1)
        self.n += 1
        self.eng.wait_ge(self.sem, self.base + self.n)


def bc(ap, shape):
    return ap.broadcast_to(shape)


def build(nc, io, out):
    ctx = ExitStack()
    with ctx:
        def sb(name, shape, dt=fp32):
            return ctx.enter_context(nc.sbuf_tensor(name, shape, dt))

        def sem(name):
            return ctx.enter_context(nc.semaphore(name))

        banks = [ctx.enter_context(nc.psum_tensor(f"bank{i}", [P, 512], fp32)) for i in range(8)]

        x_sb = sb("x_sb", [P, TILES, D])
        xn_sb = sb("xn_sb", [P, TILES, D])

        ident = sb("ident", [P, P])
        before_bf = sb("before_bf", [P, P], bf16)
        ones_bf = sb("ones_bf", [P, P], bf16)
        upto = sb("upto", [P, P])
        after = sb("after", [P, P])
        ones = sb("ones", [P, P])
        rank8 = sb("rank8", [P, E])
        earlier8 = sb("earlier8", [P, E, E])
        thresh = sb("thresh", [P, N // T])
        region = sb("region", [P, E])
        region_step = sb("region_step", [P, E])
        zeros = sb("zeros", [P, T // P * D])
        slot_no = sb("slot_no", [P, SLOTS_MAX])

        rw_sb = sb("rw_sb", [D, E])

        wc = [sb("wc_high", [D, CONV_K, CONV], f32r), sb("wc_low", [D, CONV_K, CONV], f32r)]
        wz = [sb("wz_high", [D, ZW], f32r), sb("wz_low", [D, ZW], f32r)]
        conv_b = sb("conv_b", [P, CH])
        w_out = sb("w_out", [P, 2, D])
        dt_bias = sb("dt_bias", [P, HEADS])
        neg_a = sb("neg_a", [P, HEADS])
        d_skip = sb("d_skip", [P, HEADS])

        w_dram = nc.dram_tensor("w_split", (E * P, 2 * WROW), fp32, kind="Internal").ap()
        xd_dram = nc.dram_tensor("x_dispatched", (E * REGION, D), fp32, kind="Internal").ap()
        yd_dram = nc.dram_tensor("y_dispatched", (ROWS, D), fp32, kind="Internal").ap()

        class Setup:

            def __init__(self, tb):
                self.w_raw = tb("w_raw", [P, 2, WROW])
                self.w_two = [tb(f"w_two{i}", [P, 2 * WROW], f32r) for i in range(2)]
                self.w_in = tb("w_in", [D, ZW + CONV])
                self.cw = tb("conv_w_rows", [D, CONV_K, CONV])
                self.scaled = tb("w_scaled", [D, CONV_K, CONV])
                self.norm_w = tb("norm_w", [P, 2])
                self.s_x = [sem(f"x_loaded{b}") for b in range(BATCH)]
                self.s_rw = sem("router_loaded")
                self.s_const = sem("constants_made")
                self.s_raw = [sem("raw_loaded0"), sem("raw_loaded1")]
                self.s_high = sem("weights_high")
                self.s_split = sem("weights_split")
                self.s_wst = [sem("weights_stored0"), sem("weights_stored1")]
                self.s_in = sem("mixer_weights_in")
                self.s_a = sem("mixer_a_exp")
                self.s_al = sem("mixer_a_clamped")

            def sp(self, sp):
                for b in range(BATCH):
                    sp.dma_start(x_sb[:, CT * b:CT * b + CT, :],
                                 io["x"][b * SEQ:(b + 1) * SEQ, :].rearrange("(t p) d -> p t d", p=P)).then_inc(self.s_x[b], 16)
                    if b == 0:
                        sp.dma_start(rw_sb[:], io["router_wT"]).then_inc(self.s_rw, 16)
                for to, of in ((self.w_in[:], io["W_in"]), (self.cw[:], io["conv_wT"].partition_broadcast(P)),
                               (conv_b[:], io["conv_bT"]), (w_out[:], io["W_out"].rearrange("(c p) d -> p c d", p=P)),
                               (self.norm_w[:], io["norm_wT"]), (dt_bias[:], io["dt_bias"].partition_broadcast(P)),
                               (neg_a[:], io["A_log"].partition_broadcast(P)), (d_skip[:], io["D"].partition_broadcast(P))):
                    sp.dma_start(to, of).then_inc(self.s_in, 16)
                for e in range(E):
                    if e >= 2:
                        sp.wait_ge(self.s_split, e - 1)
                    raw = self.w_raw[:, e % 2, :]
                    sp.dma_start(raw[:, 0:H], io["w_gate"][e]).then_inc(self.s_raw[e % 2], 16)
                    sp.dma_start(raw[:, H:2 * H], io["w_up"][e]).then_inc(self.s_raw[e % 2], 16)
                    sp.dma_start(raw[:, 2 * H:].rearrange("p (c d) -> p c d", c=2),
                                 io["w_down"][e].rearrange("(c p) d -> p c d", p=P)).then_inc(self.s_raw[e % 2], 16)

            def act(self, act, q):
                act.wait_ge(self.s_split, q + 1)
                act.dma_start(w_dram[q * P:(q + 1) * P, :], self.w_two[q % 2][:].bitcast(fp32)).then_inc(self.s_wst[q % 2], 16)

            def act_end(self, act):
                act.wait_ge(self.s_al, 1)
                nc.scalar.activation(neg_a[:], neg_a[:], ACT.Exp).then_inc(self.s_a, 1)
                for i in range(2):
                    act.wait_ge(self.s_wst[i], 16 * E // 2)

            def dve(self, dve, e):
                dve.wait_ge(self.s_raw[e % 2], 48 * (e // 2 + 1))
                if e >= 2:
                    dve.wait_ge(self.s_wst[e % 2], 16 * (e // 2))
                w = self.w_two[e % 2]
                nc.vector.tensor_copy(w[:, 0:WROW], self.w_raw[:, e % 2, :]).then_inc(self.s_high, 1)
                dve.wait_ge(self.s_high, e + 1)
                nc.vector.tensor_tensor(w[:, WROW:], self.w_raw[:, e % 2, :], w[:, 0:WROW].bitcast(fp32),
                                        ALU.subtract).then_inc(self.s_split, 1)

            def dve_end(self, dve, c):
                dve.wait_ge(self.s_in, 16 * 8)
                nc.vector.tensor_scalar(neg_a[:], neg_a[:], 88.0, None, ALU.min).then_inc(self.s_al, 1)
                for k in range(CONV_K):
                    c(nc.vector.tensor_tensor(self.scaled[:, k, :], self.w_in[:, INNER:INNER + CONV], self.cw[:, k, :], ALU.mult))
                c(nc.vector.tensor_copy(wc[0][:], self.scaled[:]))
                c(nc.vector.tensor_tensor(wc[1][:], self.scaled[:], wc[0][:].bitcast(fp32), ALU.subtract))
                for to, of in ((slice(0, INNER), slice(0, INNER)), (slice(INNER, ZW), slice(INNER + CONV, ZW + CONV))):
                    c(nc.vector.tensor_copy(wz[0][:, to], self.w_in[:, of]))
                    c(nc.vector.tensor_tensor(wz[1][:, to], self.w_in[:, of], wz[0][:, to].bitcast(fp32), ALU.subtract))
                for k in range(2):
                    c(nc.vector.tensor_scalar(w_out[:, k, :], w_out[:, k, :], self.norm_w[:, k:k + 1], None, ALU.mult))
                dve.wait_ge(self.s_a, 1)
                c(nc.vector.tensor_scalar(neg_a[:], neg_a[:], -1.0, None, ALU.mult))

            def pool(self, pool):
                c = Chain(pool, sem("constants_chain"))
                nc.gpsimd.memset(ones[:], 1.0)
                nc.gpsimd.memset(ones_bf[:], 1.0)
                nc.gpsimd.memset(ident[:], 0.0)
                nc.gpsimd.memset(earlier8[:], 1.0)
                nc.gpsimd.memset(zeros[:], 0.0)
                c(nc.gpsimd.memset(region_step[:], float(REGION)))
                up = dict(pattern=[[1, P]], base=0, channel_multiplier=-1, fill=0.0)
                down = dict(pattern=[[-1, P]], base=0, channel_multiplier=1)
                nc.gpsimd.affine_select(out=ident[:], in_=ident[:], compare_op=ALU.not_equal, fill=1.0, **down)
                nc.gpsimd.affine_select(out=before_bf[:], in_=ones_bf[:], compare_op=ALU.is_gt, **up)
                nc.gpsimd.affine_select(out=upto[:], in_=ones[:], compare_op=ALU.is_ge, **up)
                nc.gpsimd.affine_select(out=after[:], in_=ones[:], compare_op=ALU.is_gt, fill=0.0, **down)
                nc.gpsimd.affine_select(out=earlier8[:], in_=earlier8[:], compare_op=ALU.is_gt,
                                        pattern=[[1, E], [-1, E]], base=0, channel_multiplier=0, fill=0.0)
                nc.gpsimd.memset(region_step[:, 0:1], 0.0)
                for to, pattern, base in ((rank8, [[-1, E]], E), (thresh, [[T, N // T]], 0), (slot_no, [[1, SLOTS_MAX]], 0),
                                          (region, [[REGION, E]], 0)):
                    last = nc.gpsimd.iota(to[:], pattern=pattern, base=base, channel_multiplier=0,
                                          allow_small_or_imprecise_dtypes=True)
                c(last)
                pool.sem_inc(self.s_const, 1)

        gate = sb("gate", [P, 2, TILES])
        slot_at = sb("slot_at", [P, 2, SLOTS_MAX], i32)
        row = [sb("row1", [P, TILES], i32), sb("row2", [P, TILES], i32)]
        row_y = [sb("row_y1", [P, TILES], i32), sb("row_y2", [P, TILES], i32)]

        def rsqrt(c, r, v, tmp):
            c(nc.vector.tensor_scalar(r.bitcast(i32), v.bitcast(i32), -0.5, float(0x5F3759DF), ALU.mult, ALU.add))
            for _ in range(3):
                c(nc.vector.tensor_tensor(tmp, r, r, ALU.mult))
                c(nc.vector.scalar_tensor_tensor(out=tmp, in0=tmp, scalar=-0.5, in1=v, op0=ALU.mult, op1=ALU.mult))
                c(nc.vector.scalar_tensor_tensor(out=r, in0=tmp, scalar=1.5, in1=r, op0=ALU.add, op1=ALU.mult))

        def route(tag):
            with ExitStack() as tmp:
                tb = lambda name, shape, dt=fp32: tmp.enter_context(nc.sbuf_tensor(f"{tag}_{name}", shape, dt))
                route_in(tag, tb, Setup(tb) if tag == "r1" else None)

        def route_in(tag, tb, setup):
            G = 8
            Q = TILES // G
            stats = tb("stats", [P, 2, G, 6])
            mv = tb("mv", [P, 2, G, 2])
            var = tb("var", [P, G])
            rstd = tb("rstd", [P, 2, G])
            shift = tb("shift", [P, 2, G])
            ntmp = tb("newton", [P, G])
            xT = [tb(f"xT{i}", [D, G * P]) for i in range(2)]
            logit = tb("logit", [P, G, E])
            sel = tb("sel", [P, 2, TILES, E])
            best = tb("best", [P, 2, TILES])
            gsum = tb("gsum", [P, TILES])
            work = tb("work", [P, G, E])
            work2 = tb("work2", [P, G])
            selb = [tb(f"selb{i}", [P, G, E], bf16) for i in range(2)]
            carry = [tb(f"carry{i}", [P, E], bf16) for i in range(2)]
            tsum = tb("tsum", [P, E])
            at = tb("at", [P, G, E])
            cmp16 = tb("cmp16", [P, E, N // T])
            need = tb("need", [P, E])
            total = tb("total", [P, 1])
            count = tb("count", [P, E])
            cmp8 = tb("cmp8", [P, E, E])
            first = tb("first", [P, E])
            offset = tb("offset", [P, E])
            step = tb("step", [P, E])
            cmpslot = tb("cmpslot", [P, SLOTS_MAX, E])
            slotf = tb("slotf", [P, 2, SLOTS_MAX])
            pad_at = tb("pad_at", [P, E], i32)
            big = tb("big", [P, TILES, E])
            big2 = tb("big2", [P, TILES])

            s_ms = sem(f"{tag}_moments")
            s_xn = sem(f"{tag}_normed")
            s_tr = sem(f"{tag}_transposed")
            s_xT = sem(f"{tag}_xT_in_sbuf")
            s_lg = sem(f"{tag}_logits_made")
            s_ch = sem(f"{tag}_chain")
            s_best = sem(f"{tag}_best_found")
            s_gt = sem(f"{tag}_sigmoid")
            s_selb = sem(f"{tag}_selected")
            s_cnt = sem(f"{tag}_counted")
            s_used = sem(f"{tag}_count_read")
            s_row = sem(f"{tag}_rows_known")
            s_total = sem(f"{tag}_totals")
            s_pad = sem(f"{tag}_pads_known")
            s_pw = sem(f"{tag}_pads_written")
            s_sent = sem(f"{tag}_rows_sent")
            b_x, b_l, b_p = (banks[0:2], banks[2:4]), banks[4:6], banks[6:8]
            with nc.Block() as block:
                @block.vector
                def _(dve):
                    c = Chain(dve, s_ch)

                    def moments(q):
                        i = q % 2
                        if q >= 2:
                            dve.wait_ge(s_xn, q - 1)
                        if setup:
                            dve.wait_ge(setup.s_x[q], 16)
                        for j in range(G):
                            last = nc.vector.bn_stats(stats[:, i, j, :], x_sb[:, G * q + j, :])
                        c(last)
                        for j in range(G):
                            last = nc.vector.bn_aggr(mv[:, i, j, :], stats[:, i, j, :])
                        c(last)
                        c(nc.vector.tensor_scalar(var[:], mv[:, i, :, 1], LN_EPS, None, ALU.add))
                        rsqrt(c, rstd[:, i, :], var[:], ntmp[:])
                        nc.vector.scalar_tensor_tensor(out=shift[:, i, :], in0=mv[:, i, :, 0], scalar=-1.0,
                                                       in1=rstd[:, i, :], op0=ALU.mult, op1=ALU.mult).then_inc(s_ms, 1)

                    def choose(q):
                        i = q % 2
                        tiles = slice(G * q, G * q + G)
                        full = [P, G, E]
                        dve.wait_ge(s_lg, q + 1)
                        c(nc.vector.tensor_copy(logit[:], b_l[i][:, 0:G * E].rearrange("p (j e) -> p j e", e=E)))
                        for k in range(2):
                            c(nc.vector.tensor_reduce(best[:, k, tiles], logit[:], AX.X, ALU.max))
                            c(nc.vector.tensor_tensor(work[:], logit[:], bc(best[:, k, tiles].unsqueeze(2), full), ALU.is_equal))
                            c(nc.vector.tensor_tensor(work[:], work[:], bc(rank8[:].unsqueeze(1), full), ALU.mult))
                            c(nc.vector.tensor_reduce(work2[:], work[:], AX.X, ALU.max))
                            c(nc.vector.tensor_tensor(sel[:, k, tiles, :], work[:], bc(work2[:].unsqueeze(2), full), ALU.is_equal))
                            if k == 0:
                                c(nc.vector.scalar_tensor_tensor(out=logit[:], in0=sel[:, 0, tiles, :], scalar=-3e38,
                                                                 in1=logit[:], op0=ALU.mult, op1=ALU.add))
                        nc.vector.tensor_tensor(selb[i][:], sel[:, 0, tiles, :], sel[:, 1, tiles, :], ALU.add
                                                ).then_inc(s_selb, 1)
                        dve.wait_ge(s_selb, q + 1)
                        c(nc.vector.tensor_reduce(tsum[:], selb[i][:].rearrange("p t e -> p e t"), AX.X, ALU.add))
                        if q >= 1:
                            dve.wait_ge(s_cnt, q)
                        c(nc.vector.tensor_tensor(carry[(q + 1) % 2][:], carry[i][:], tsum[:], ALU.add))

                    def place(q):
                        tiles = slice(G * q, G * q + G)
                        dve.wait_ge(s_cnt, q + 1)
                        c(nc.vector.tensor_tensor(at[:], b_p[q % 2][:, 0:G * E].rearrange("p (j e) -> p j e", e=E),
                                                  bc(region[:].unsqueeze(1), [P, G, E]), ALU.add))
                        for k in range(2):
                            c(nc.vector.tensor_tensor(work[:], at[:], sel[:, k, tiles, :], ALU.mult))
                            c(nc.vector.tensor_reduce(work2[:], work[:], AX.X, ALU.add))
                            c(nc.vector.tensor_copy(row[k][:, tiles], work2[:]))
                        nc.vector.tensor_copy(work2[:, 0:1], row[0][:, G * q:G * q + 1]).then_inc(s_row, 1)

                    c(nc.vector.memset(carry[0][:], 0.0))
                    moments(0)
                    moments(1)
                    if setup:
                        dve.wait_ge(setup.s_const, 1)
                    for q in range(Q):
                        choose(q)
                        if q + 2 < Q:
                            moments(q + 2)
                        place(q)
                        if setup:
                            setup.dve(dve, q)
                    dve.wait_ge(s_total, 1)
                    c(nc.vector.tensor_copy(count[:], b_l[0][:, 0:E]))
                    c(nc.vector.tensor_tensor(step[:], count[:], region[:], ALU.add))
                    nc.vector.tensor_copy(pad_at[:], step[:]).then_inc(s_pad, 1)
                    n16 = [P, E, N // T]
                    c(nc.vector.tensor_tensor(cmp16[:], bc(count[:].unsqueeze(2), n16), bc(thresh[:].unsqueeze(1), n16), ALU.is_gt))
                    c(nc.vector.tensor_reduce(need[:], cmp16[:], AX.X, ALU.add))
                    c(nc.vector.tensor_reduce(total[:], need[:], AX.X, ALU.add))
                    c(nc.vector.tensor_tensor(cmp8[:], bc(need[:].unsqueeze(1), [P, E, E]), earlier8[:], ALU.mult))
                    c(nc.vector.tensor_reduce(first[:], cmp8[:], AX.X, ALU.add))
                    c(nc.vector.scalar_tensor_tensor(out=offset[:], in0=first[:], scalar=-float(T), in1=region[:],
                                                     op0=ALU.mult, op1=ALU.add))
                    c(nc.vector.tensor_copy(step[:], region_step[:]))
                    c(nc.vector.scalar_tensor_tensor(out=step[:, 1:], in0=need[:, 0:E - 1], scalar=-float(T),
                                                     in1=region_step[:, 1:], op0=ALU.mult, op1=ALU.add))
                    ns = [P, SLOTS_MAX, E]
                    c(nc.vector.tensor_tensor(cmpslot[:], bc(slot_no[:].unsqueeze(2), ns), bc(first[:].unsqueeze(1), ns), ALU.is_ge))
                    c(nc.vector.tensor_reduce(slotf[:, 0, :], cmpslot[:], AX.X, ALU.add))
                    c(nc.vector.tensor_scalar(slotf[:, 0, :], slotf[:, 0, :], -1.0, float(P), ALU.add, ALU.mult))
                    c(nc.vector.tensor_tensor(cmpslot[:], cmpslot[:], bc(step[:].unsqueeze(1), ns), ALU.mult))
                    c(nc.vector.tensor_reduce(slotf[:, 1, :], cmpslot[:], AX.X, ALU.add))
                    c(nc.vector.scalar_tensor_tensor(out=slotf[:, 1, :], in0=slot_no[:], scalar=float(T), in1=slotf[:, 1, :],
                                                     op0=ALU.mult, op1=ALU.add))
                    c(nc.vector.scalar_tensor_tensor(out=slotf[:, 1, :], in0=slot_no[:], scalar=total[:, 0:1],
                                                     in1=slotf[:, 1, :], op0=ALU.is_lt, op1=ALU.mult))
                    c(nc.vector.tensor_copy(slot_at[:], slotf[:]))
                    full = [P, TILES, E]
                    for k in range(2):
                        c(nc.vector.tensor_tensor(big[:], sel[:, k, :, :], bc(offset[:].unsqueeze(1), full), ALU.mult))
                        c(nc.vector.tensor_reduce(big2[:], big[:], AX.X, ALU.add))
                        c(nc.vector.tensor_tensor(row_y[k][:], row[k][:], big2[:], ALU.subtract))
                    dve.wait_ge(s_gt, 1)
                    c(nc.vector.tensor_tensor(gsum[:], gate[:, 0, :], gate[:, 1, :], ALU.add))
                    c(nc.vector.tensor_scalar(gsum[:], gsum[:], 1e-10, None, ALU.add))
                    c(nc.vector.reciprocal(gsum[:], gsum[:]))
                    for k in range(2):
                        c(nc.vector.scalar_tensor_tensor(out=gate[:, k, :], in0=gate[:, k, :], scalar=0.5, in1=gsum[:],
                                                         op0=ALU.mult, op1=ALU.mult))
                    if setup:
                        setup.dve_end(dve, c)

                @block.scalar
                def _(act):
                    def norm(q):
                        i = q % 2
                        act.wait_ge(s_ms, q + 1)
                        for j in range(G):
                            last = nc.scalar.activation(xn_sb[:, G * q + j, :], x_sb[:, G * q + j, :], ACT.Identity,
                                                        bias=shift[:, i, j:j + 1], scale=rstd[:, i, j:j + 1])
                        last.then_inc(s_xn, 1)

                    if setup:
                        act.wait_ge(setup.s_x[0], 16)
                    norm(0)
                    for q in range(Q):
                        if q + 1 < Q:
                            if setup:
                                act.wait_ge(setup.s_x[q + 1], 16)
                            norm(q + 1)
                        if q >= 2:
                            act.wait_ge(s_lg, q - 1)
                        for h in range(2):
                            act.wait_ge(s_tr, 2 * q + h + 1)
                            nc.scalar.activation(xT[q % 2][:, 512 * h:512 * h + 512], b_x[q % 2][h][:], ACT.Copy
                                                 ).then_inc(s_xT, 1)
                        if setup and q >= 1:
                            setup.act(act, q - 1)
                    if setup:
                        setup.act(act, Q - 1)
                    act.wait_ge(s_selb, Q)
                    nc.scalar.activation(gate[:], best[:], ACT.Sigmoid).then_inc(s_gt, 1)
                    if setup:
                        setup.act_end(act)

                @block.tensor
                def _(pe):
                    b_x2 = b_x

                    def turn(q):
                        pe.wait_ge(s_xn, q + 1)
                        for h in range(2):
                            if q >= 2:
                                pe.wait_ge(s_xT, 2 * (q - 2) + h + 1)
                            for j in range(4):
                                last = pe.transpose(b_x[q % 2][h][:, j * P:(j + 1) * P], xn_sb[:, G * q + 4 * h + j, :], ident[:])
                            last.then_inc(s_tr, 1)

                    def logits(q):
                        pe.wait_ge(s_xT, 2 * q + 2)
                        if q >= 2:
                            pe.wait_ge(s_selb, q - 1)
                        for j in range(G):
                            last = pe.matmul(b_l[q % 2][:, j * E:(j + 1) * E], xT[q % 2][:, j * P:(j + 1) * P], rw_sb[:],
                                             start=True, stop=True)
                        last.then_inc(s_lg, 1)

                    def counts(q):
                        pe.wait_ge(s_selb, q + 1)
                        if q >= 2:
                            pe.wait_ge(s_row, q - 1)
                        s = selb[q % 2]
                        out3 = b_p[q % 2][:, 0:G * E]
                        pe.matmul(out3, before_bf[:], s[:].rearrange("p t e -> p (t e)"), start=True, stop=False)
                        for j in range(G - 1):
                            pe.matmul(b_p[q % 2][:, (j + 1) * E:G * E].rearrange("p (t e) -> p t e", e=E), ones_bf[:],
                                      bc(s[:, j:j + 1, :], [P, G - 1 - j, E]), start=False, stop=False)
                        pe.matmul(out3.rearrange("p (t e) -> p t e", e=E), ones_bf[:],
                                  bc(carry[q % 2][:].unsqueeze(1), [P, G, E]), start=False, stop=True).then_inc(s_cnt, 1)

                    if setup:
                        pe.wait_ge(setup.s_const, 1)
                        pe.wait_ge(setup.s_rw, 16)
                    turn(0)
                    for q in range(Q):
                        logits(q)
                        if q + 1 < Q:
                            turn(q + 1)
                        counts(q)
                    pe.wait_ge(s_row, Q)
                    pe.matmul(b_l[0][:, 0:E], ones_bf[:], carry[Q % 2][:], start=True, stop=True).then_inc(s_total, 1)

                @block.gpsimd
                def _(pool):
                    if setup:
                        setup.pool(pool)
                    for t in range(TILES):
                        if t % G == 0:
                            pool.wait_ge(s_row, t // G + 1)
                        for k in range(2):
                            pool.indirect_dma_start(out=xd_dram, out_offset=bass.IndirectOffsetOnAxis(ap=row[k][:, t:t + 1], axis=0),
                                                    in_=xn_sb[:, t, :], in_offset=None).then_inc(s_sent, 16)
                    pool.wait_ge(s_sent, 16 * 2 * TILES)

                @block.sync
                def _(sp):
                    if setup:
                        setup.sp(sp)
                    sp.wait_ge(s_pad, 1)
                    for e in range(E):
                        at_e = sp.value_load(pad_at[0:1, e:e + 1], min_val=0, max_val=E * REGION - T)
                        sp.dma_start(xd_dram[ds(at_e, T), :].rearrange("(p j) d -> p (j d)", p=P), zeros[:]).then_inc(s_pw, 16)
                    sp.wait_ge(s_pw, 16 * E)

        def experts(tag):
            with ExitStack() as tmp:
                experts_in(tag, lambda name, shape, dt=fp32: tmp.enter_context(nc.sbuf_tensor(f"{tag}_{name}", shape, dt)))

        def experts_in(tag, tb):
            w_slot = [tb(f"w_slot{i}", [P, 2 * WROW], f32r) for i in range(3)]
            xr = [tb(f"xr{i}", [P, 4, D]) for i in range(XB)]
            xh = [tb(f"xh{i}", [D, T], f32r) for i in range(2)]
            xl = [tb(f"xl{i}", [D, T], f32r) for i in range(2)]
            sg = [tb(f"sg{i}", [P, T]) for i in range(2)]
            hf = [tb(f"hf{i}", [P, T]) for i in range(2)]
            hh = [[tb(f"hh{i}{c}", [P, T], f32r) for c in range(2)] for i in range(2)]
            hl = [[tb(f"hl{i}{c}", [P, T], f32r) for c in range(2)] for i in range(2)]
            oT = [tb(f"oT{i}", [D, T]) for i in range(2)]
            yr = [tb(f"yr{i}", [P, 4, D]) for i in range(2)]
            s_w = [sem(f"{tag}_weights_in{i}") for i in range(3)]
            s_xr = [sem(f"{tag}_rows_in{i}") for i in range(XB)]
            s_tr = sem(f"{tag}_x_turned")
            s_xh = sem(f"{tag}_x_high")
            s_xl = sem(f"{tag}_x_low")
            s_gu = sem(f"{tag}_gate_up")
            s_sg = sem(f"{tag}_silu")
            s_hf = sem(f"{tag}_hidden")
            s_hh = sem(f"{tag}_hidden_high")
            s_hl = sem(f"{tag}_hidden_low")
            s_dn = sem(f"{tag}_down")
            s_oT = sem(f"{tag}_down_copied")
            s_ot = sem(f"{tag}_out_turned")
            s_yr = sem(f"{tag}_out_rows")
            s_yo = [sem(f"{tag}_out_stored{i}") for i in range(2)]
            yd = yd_dram.rearrange("(t p j) d -> t p j d", p=P, j=4)
            b_x, b_g, b_u, b_d, b_o = banks[0], banks[1:3], banks[3:5], banks[5], banks[6]
            LAST = SLOTS_MAX - 1

            with nc.Block() as block:
                @block.sync
                def _(sp):
                    def load(t, s):
                        at = sp.value_load(slot_at[0:1, 1, t:t + 1], min_val=0, max_val=E * REGION - T)
                        sp.dma_start(xr[s][:], xd_dram[ds(at, T), :].rearrange("(p j) d -> p j d", p=P)).then_inc(s_xr[s], 16)

                    def load_weights(t):
                        if t >= 3:
                            sp.wait_ge(s_dn, t - 2)
                        at = sp.value_load(slot_at[0:1, 0, t:t + 1], min_val=0, max_val=(E - 1) * P)
                        sp.dma_start(w_slot[t % 3][:].bitcast(fp32), w_dram[ds(at, P), :]).then_inc(s_w[t % 3], 16)

                    def store(t, s):
                        sp.wait_ge(s_yr, t + 1)
                        sp.dma_start(yd[ds(t, 1)].rearrange("o p j d -> (o p) j d"), yr[s][:]).then_inc(s_yo[s], 16)

                    for t in range(XB):
                        load(t, t)
                        if t < 3:
                            load_weights(t)
                    for t in range(XB, SLOTS_MAX + XB + 2):
                        if t < SLOTS_MAX:
                            sp.wait_ge(s_tr, t - XB + 1)
                            load(t, t % XB)
                        if t - 1 < SLOTS_MAX:
                            load_weights(t - 1)
                        if t >= XB + 2:
                            store(t - XB - 2, t % 2)
                    for s in range(2):
                        sp.wait_ge(s_yo[s], 16 * ((SLOTS_MAX + 1 - s) // 2))

                @block.tensor
                def _(pe):
                    def turn(t):
                        s = t % XB
                        pe.wait_ge(s_xr[s], 16 * (t // XB + 1))
                        if not isinstance(t, int) or t >= 1:
                            pe.wait_ge(s_xl, t)
                        for j in range(4):
                            last = pe.transpose(b_x[:, j * P:(j + 1) * P], xr[s][:, j, :], ident[:])
                        last.then_inc(s_tr, 1)

                    def gate_up(t, s, half, later):
                        w = w_slot[t % 3]
                        pe.wait_ge(s_w[t % 3], 16 * (t // 3 + 1))
                        pe.wait_ge(s_xl, t + 1)
                        for c in range(2):
                            if later:
                                pe.wait_ge(s_hf, 2 * t - 1 + c)
                            for bank, at in ((b_g[c], c * P), (b_u[c], H + c * P)):
                                high, low = w[:, at:at + P], w[:, WROW + at:WROW + at + P]
                                pe.matmul(bank[:], high, xh[s][:], start=True, stop=False)
                                pe.matmul(bank[:], high, xl[s][:], start=False, stop=False)
                                last = pe.matmul(bank[:], low, xh[s][:], start=False, stop=True)
                            last.then_inc(s_gu, 1)

                    def down(t, s, later):
                        w = w_slot[t % 3]
                        if later:
                            pe.wait_ge(s_oT, t)
                        for c in range(2):
                            pe.wait_ge(s_hl, 2 * t + c + 1)
                            at = 2 * H + c * D
                            high, low = w[:, at:at + D], w[:, WROW + at:WROW + at + D]
                            pe.matmul(b_d[:], high, hh[s][c][:], start=(c == 0), stop=False)
                            pe.matmul(b_d[:], high, hl[s][c][:], start=False, stop=False)
                            last = pe.matmul(b_d[:], low, hh[s][c][:], start=False, stop=(c == 1))
                        last.then_inc(s_dn, 1)

                    def turn_out(t, later):
                        pe.wait_ge(s_oT, t + 1)
                        if later:
                            pe.wait_ge(s_yr, t)
                        for j in range(4):
                            last = pe.transpose(b_o[:, j * P:(j + 1) * P], oT[t % 2][:, j * P:(j + 1) * P], ident[:])
                        last.then_inc(s_ot, 1)

                    turn(0)
                    for t in range(SLOTS_MAX):
                        s = t % 2
                        if t < LAST:
                            turn(t + 1)
                        gate_up(t, s, t // 2, t >= 1)
                        if t >= 1:
                            down(t - 1, 1 - s, t >= 2)
                        if t >= 2:
                            turn_out(t - 2, t >= 3)
                    down(LAST, LAST % 2, True)
                    turn_out(LAST - 1, True)
                    turn_out(LAST, True)

                @block.scalar
                def _(act):
                    def x_high(t, s, later):
                        act.wait_ge(s_tr, t + 1)
                        if later:
                            act.wait_ge(s_gu, 2 * t - 2)
                        nc.scalar.activation(xh[s][:], b_x[:], ACT.Copy).then_inc(s_xh, 1)

                    def silu(t, later):
                        for c in range(2):
                            act.wait_ge(s_gu, 2 * t + c + 1)
                            if later:
                                act.wait_ge(s_hf, 2 * t - 1 + c)
                            nc.scalar.activation(sg[c][:], b_g[c][:], ACT.Silu).then_inc(s_sg, 1)

                    def down_copy(t):
                        act.wait_ge(s_dn, t + 1)
                        if t >= 2:
                            act.wait_ge(s_ot, t - 1)
                        nc.scalar.activation(oT[t % 2][:], b_d[:], ACT.Copy).then_inc(s_oT, 1)

                    def out_copy(t, s, later2):
                        act.wait_ge(s_ot, t + 1)
                        if later2:
                            act.wait_ge(s_yo[s], later2)
                        nc.scalar.activation(yr[s][:].rearrange("p j d -> p (j d)"), b_o[:], ACT.Copy).then_inc(s_yr, 1)

                    x_high(0, 0, False)
                    for t in range(SLOTS_MAX):
                        s = t % 2
                        if t < LAST:
                            x_high(t + 1, 1 - s, t + 1 >= 2)
                        silu(t, t >= 1)
                        if t >= 1:
                            down_copy(t - 1)
                        if t >= 2:
                            out_copy(t - 2, s, 16 * ((t - 2) // 2))
                    down_copy(LAST)
                    out_copy(LAST - 1, 1 - LAST % 2, 16 * ((LAST - 1) // 2))
                    out_copy(LAST, LAST % 2, 16 * (LAST // 2))

                @block.vector
                def _(dve):
                    def x_low(t, s):
                        dve.wait_ge(s_xh, t + 1)
                        nc.vector.tensor_tensor(xl[s][:], b_x[:], xh[s][:].bitcast(fp32), ALU.subtract).then_inc(s_xl, 1)

                    def hidden(t, s, later):
                        for c in range(2):
                            dve.wait_ge(s_sg, 2 * t + c + 1)
                            if t >= 1:
                                dve.wait_ge(s_hl, 2 * t + c - 1)
                            nc.vector.tensor_tensor(hf[c][:], sg[c][:], b_u[c][:], ALU.mult).then_inc(s_hf, 1)
                        if later:
                            dve.wait_ge(s_dn, t - 1)
                        for c in range(2):
                            dve.wait_ge(s_hf, 2 * t + c + 1)
                            nc.vector.tensor_copy(hh[s][c][:], hf[c][:]).then_inc(s_hh, 1)
                        for c in range(2):
                            dve.wait_ge(s_hh, 2 * t + c + 1)
                            nc.vector.tensor_tensor(hl[s][c][:], hf[c][:], hh[s][c][:].bitcast(fp32),
                                                    ALU.subtract).then_inc(s_hl, 1)

                    x_low(0, 0)
                    for t in range(SLOTS_MAX):
                        s = t % 2
                        if t < LAST:
                            x_low(t + 1, 1 - s)
                        hidden(t, s, t >= 2)

        def mixer(tmp):
            def tb(name, shape, dt=fp32):
                return tmp.enter_context(nc.sbuf_tensor(name, shape, dt))

            y_in = [[tb(f"y_in{i}{k}", [P, D]) for k in range(2)] for i in range(4)]
            xTb = [tb("xT_high", [D, 4 + SEQ], f32r), tb("xT_low", [D, 4 + SEQ], f32r)]
            cT = [[tb(f"cT{s}{k}", [P, SEQ]) for k in range(CH)] for s in range(2)]
            zr = [tb(f"z{s}", [P, CT, ZW]) for s in range(2)]
            dt = [tb(f"dt{s}", [P, CT, HEADS]) for s in range(2)]
            da = [tb(f"da{s}", [P, CT, HEADS]) for s in range(2)]
            e1 = tb("softplus_e", [P, CT, HEADS])
            e2 = tb("softplus_s", [P, CT, HEADS])
            e3 = tb("softplus_q", [P, CT, HEADS])
            tok = [tb(f"tok{i}", [P, INNER + STATE + 2 * HEADS]) for i in range(2)]
            exs = [tb(f"chunk_decay{i}", [P, 2 * HEADS]) for i in range(2)]
            dam = [tb(f"da_masked{i}", [P, HEADS, P]) for i in range(2)]
            seg = [tb(f"decay{i}", [P, HEADS, P]) for i in range(2)]
            gm = tb("g_masked", [P, P])
            mm = [tb(f"mix{i}", [P, HEADS, P]) for i in range(2)]
            xdt = [tb(f"x_dt{i}", [P, HEADS, HD]) for i in range(2)]
            xw = [tb(f"x_end{i}", [P, HEADS, HD]) for i in range(2)]
            xsd = [tb(f"x_skip{i}", [P, HEADS, HD]) for i in range(2)]
            state = tb("state", [STATE, HEADS, HD])
            y = [tb(f"y{i}", [P, HEADS, HD]) for i in range(2)]
            junk = tb("squares", [P, INNER])
            junk2 = tb("squares2", [P, D])
            yT = tb("yT", [P, INNER])
            ob = [tb(f"out_rows{s}", [P, CT, D]) for s in range(2)]
            ssq = [tb(f"ssq{s}", [P, CT]) for s in range(2)]
            ssq2 = [tb(f"ssq2{s}", [P, CT]) for s in range(2)]
            st = tb("ln_stats", [P, CT, 6])
            mvb = tb("ln_moments", [P, CT, 2])
            var = tb("ln_var", [P, CT])
            rsb = tb("ln_rstd", [P, CT])
            shb = tb("ln_shift", [P, CT])
            tn = tb("newton", [P, CT])
            var2 = tb("rms_var", [P, CT])
            stmp = tb("state_decayed", [STATE, HEADS, HD])
            r2 = tb("r2", [P, CT])

            b_acc, b_z, b_seg, b_g, b_tok, b_y, b_up = banks[0:2], banks[2], banks[3], banks[4], banks[5], banks[6], banks[7]

            s_yi = [sem(f"m_rows_back{i}") for i in range(4)]
            s_ya = sem("m_first_added")
            s_yb = sem("m_residual")
            s_bs = sem("m_ln_stats")
            s_lv = sem("m_ln_var")
            s_ll = sem("m_ln_log")
            s_lr = sem("m_ln_rstd")
            s_xn = sem("m_normed")
            s_tr = sem("m_turned")
            s_xh = sem("m_xT_high")
            s_xl = sem("m_xT_low")
            s_cv = sem("m_conv")
            s_ce = sem("m_conv_copied")
            s_z = sem("m_z")
            s_zc = sem("m_z_copied")
            s_si = sem("m_silu")
            s_sz = sem("m_silu_z")
            s_d0 = sem("m_dt_raw")
            s_d1 = sem("m_dt_exp")
            s_da = sem("m_da")
            s_dm = sem("m_da_masked")
            s_xd = sem("m_x_skip")
            s_tk = sem("m_tokens_turned")
            s_tc = sem("m_tokens_copied")
            s_g = sem("m_g")
            s_gm = sem("m_g_masked")
            s_sg = sem("m_segments")
            s_eg = sem("m_decays")
            s_mm = sem("m_mix")
            s_x1 = sem("m_x_dt")
            s_xw = sem("m_x_end")
            s_mid = sem("m_y_and_update")
            s_st = sem("m_state")
            s_yd = sem("m_y_read")
            s_y = sem("m_y")
            s_yt = sem("m_y_turned")
            s_yc = sem("m_y_copied")
            s_o = sem("m_out")
            s_oc = sem("m_out_copied")
            s_q1 = sem("m_ssq1")
            s_q2 = sem("m_ssq2")
            s_v1 = sem("m_rms_var")
            s_l1 = sem("m_rms_log")
            s_xa = sem("m_x_and_normed")
            s_x2 = sem("m_new_x")
            s_c = sem("m_chain")
            s_zz = sem("m_pad")

            B = BATCH
            groups = [(k, h) for h in range(2) for k in range(CH)]
            CONVS = [[(1, 3)], [(1, 4)], [(1, 5)], [(1, 6)], [(1, 7)], [], [(2, 0), (2, 1)], [(2, 2)]]
            ZSTEPS = CT // 2
            AHEAD = 2 * CT + 4

            with nc.Block() as block:
                @block.gpsimd
                def _(pool):
                    nc.gpsimd.memset(xTb[0][:, 0:4].bitcast(fp32), 0.0).then_inc(s_zz, 1)
                    nc.gpsimd.memset(xTb[1][:, 0:4].bitcast(fp32), 0.0).then_inc(s_zz, 1)

                    def gather(t):
                        if t >= 4:
                            pool.wait_ge(s_yb, t - 3)
                        for k in range(2):
                            pool.indirect_dma_start(out=y_in[t % 4][k][:], out_offset=None, in_=yd_dram,
                                                    in_offset=bass.IndirectOffsetOnAxis(ap=row_y[k][:, t:t + 1], axis=0)
                                                    ).then_inc(s_yi[t % 4], 16)

                    def mask(t):
                        b, c = divmod(t, CT)
                        pool.wait_ge(s_da, b + 1)
                        if t >= 2:
                            pool.wait_ge(s_sg, t - 1)
                        nc.gpsimd.tensor_tensor(dam[t % 2][:], bc(da[b % 2][:, c, :].unsqueeze(2), [P, HEADS, P]),
                                                bc(upto[:].unsqueeze(1), [P, HEADS, P]), ALU.mult).then_inc(s_dm, 1)

                    def skip(t):
                        pool.wait_ge(s_tc, t + 1)
                        if t >= 2:
                            pool.wait_ge(s_y, t - 1)
                        nc.gpsimd.tensor_tensor(xsd[t % 2][:], tok[t % 2][:, 0:INNER].rearrange("p (h d) -> p h d", d=HD),
                                                bc(d_skip[:].unsqueeze(2), [P, HEADS, HD]), ALU.mult).then_inc(s_xd, 1)

                    for t in range(AHEAD + 2):
                        gather(t)
                    mask(0)
                    skip(0)
                    for t in range(TILES):
                        if t + 1 < TILES:
                            mask(t + 1)
                            skip(t + 1)
                        if t + AHEAD + 2 < TILES:
                            gather(t + AHEAD + 2)

                @block.tensor
                def _(pe):
                    def turn(b):
                        for h in range(2):
                            pe.wait_ge(s_xn, 2 * b + h + 1)
                            if b or h:
                                pe.wait_ge(s_ce, 8 * b)
                            for j in range(4):
                                last = pe.transpose(b_acc[h][:, j * P:(j + 1) * P], xn_sb[:, CT * b + 4 * h + j, :], ident[:])
                            last.then_inc(s_tr, 1)

                    def conv(b, g, first_tap=0, last_tap=CONV_K - 1):
                        n = 8 * b + g
                        k, h = groups[g]
                        if first_tap == 0:
                            pe.wait_ge(s_xl, 2 * b + 2)
                            if g >= 2:
                                pe.wait_ge(s_ce, n - 1)
                        acc = b_acc[n % 2]
                        for tap in range(first_tap, last_tap + 1):
                            at = 1 + tap + 512 * h
                            for i, (w, x) in enumerate(((0, 0), (0, 1), (1, 0))):
                                last = pe.matmul(acc[:], wc[w][:, tap, k * P:(k + 1) * P], xTb[x][:, at:at + 512],
                                                 start=(tap == 0 and i == 0), stop=(tap == CONV_K - 1 and i == 2))
                        if last_tap == CONV_K - 1:
                            last.then_inc(s_cv, 1)

                    def zdt(b, c):
                        n = CT * b + c
                        pe.wait_ge(s_xl, 2 * b + 2)
                        z_bank_free(pe)
                        at = 4 + P * c
                        for i, (x, w) in enumerate(((0, 0), (0, 1), (1, 0))):
                            last = pe.matmul(b_z[:, 0:ZW], xTb[x][:, at:at + P], wz[w][:], start=(i == 0), stop=(i == 2))
                        last.then_inc(s_z, 1)
                        used[0] += 1

                    used = [0, 0]

                    def z_bank_free(pe):
                        if used[0]:
                            pe.wait_ge(s_zc, used[0])
                        if used[1]:
                            pe.wait_ge(s_q2, used[1])

                    def front(t):
                        b, c = divmod(t, CT)
                        cols = slice(c * P, (c + 1) * P)
                        cs = cT[b % 2]
                        pe.wait_ge(s_si, b + 1)
                        if t >= 1:
                            pe.wait_ge(s_eg, t)
                        for j, k in enumerate((0, 1, 2)):
                            pe.transpose(b_tok[:, j * P:(j + 1) * P], cs[k][:, cols], ident[:])
                        pe.wait_ge(s_da, b + 1)
                        at = INNER + STATE
                        pe.matmul(b_tok[:, at:at + HEADS], upto[:], da[b % 2][:, c, :], start=True, stop=True)
                        pe.matmul(b_tok[:, at + HEADS:at + 2 * HEADS], ones[:], da[b % 2][:, c, :], start=True,
                                  stop=True).then_inc(s_tk, 1)
                        if t >= 1:
                            pe.wait_ge(s_gm, t)
                        pe.matmul(b_g[:, 0:P], cs[2][:, cols], cs[3][:, cols], start=True, stop=True).then_inc(s_g, 1)
                        pe.wait_ge(s_dm, t + 1)
                        pe.matmul(b_seg[:], after[:], dam[t % 2][:].rearrange("p h i -> p (h i)"), start=True,
                                  stop=True).then_inc(s_sg, 1)

                    def mid(t):
                        b, c = divmod(t, CT)
                        i = t % 2
                        if t >= 1:
                            pe.wait_ge(s_yd, t)
                            pe.wait_ge(s_st, t)
                            pe.wait_ge(s_yc, t - 1) if t >= 2 else None
                        if c:
                            pe.matmul(b_y[:, INNER:], cT[b % 2][3][:, c * P:(c + 1) * P],
                                      state[:].rearrange("p h d -> p (h d)"), start=True, stop=True)
                        pe.wait_ge(s_mm, t + 1)
                        for h in range(HEADS):
                            pe.matmul(b_y[:, h * HD:(h + 1) * HD], mm[i][:, h, :], xdt[i][:, h, :], start=True, stop=True)
                        pe.wait_ge(s_xw, t + 1)
                        pe.matmul(b_up[:, 0:INNER], tok[i][:, INNER:INNER + STATE], xw[i][:].rearrange("p h d -> p (h d)"),
                                  start=True, stop=True).then_inc(s_mid, 1)

                    def turn_y(t):
                        pe.wait_ge(s_y, t + 1)
                        pe.wait_ge(s_st, t + 1)
                        for k in range(2):
                            last = pe.transpose(b_up[:, INNER + k * P:INNER + (k + 1) * P],
                                                y[t % 2][:].rearrange("p h d -> p (h d)")[:, k * P:(k + 1) * P], ident[:])
                        last.then_inc(s_yt, 1)

                    def project(t):
                        pe.wait_ge(s_yc, t + 1)
                        z_bank_free(pe)
                        for k in range(2):
                            last = pe.matmul(b_z[:, 0:D], yT[:, k * P:(k + 1) * P], w_out[:, k, :],
                                             start=(k == 0), stop=(k == 1))
                        last.then_inc(s_o, 1)
                        used[1] += 1

                    pe.wait_ge(s_zz, 2)
                    turn(0)
                    for g in range(8):
                        conv(0, g)
                    for c in range(CT):
                        zdt(0, c)
                    turn(1)
                    conv(1, 0)
                    conv(1, 1)
                    front(0)
                    conv(1, 2)
                    for t in range(TILES):
                        b, c = divmod(t, CT)
                        more = b + 1 < B
                        if t + 1 < TILES:
                            front(t + 1)
                        if c == 5 and b + 2 < B:
                            turn(b + 2)
                        convs = [(b + ahead, g) for ahead, g in CONVS[c] if b + ahead < B]
                        if convs:
                            conv(*convs[0], 0, 1)
                        if t >= 1:
                            turn_y(t - 1)
                        if more and c < ZSTEPS:
                            zdt(b + 1, 2 * c)
                        for n, (seq, g) in enumerate(convs):
                            conv(seq, g, 2 if n == 0 else 0)
                        if t >= 1:
                            project(t - 1)
                        mid(t)
                        if more and c < ZSTEPS:
                            zdt(b + 1, 2 * c + 1)
                    turn_y(TILES - 1)
                    project(TILES - 1)

                @block.scalar
                def _(act):
                    def x_high(b):
                        for h in range(2):
                            act.wait_ge(s_tr, 2 * b + h + 1)
                            if b:
                                act.wait_ge(s_z, CT * b)
                                act.wait_ge(s_cv, 8 * b)
                            nc.scalar.activation(xTb[0][:, 4 + 512 * h:516 + 512 * h], b_acc[h][:], ACT.Copy).then_inc(s_xh, 1)

                    def norm(b, h):
                        act.wait_ge(s_lv, b + 1)
                        for t in range(CT * b + 4 * h, CT * b + 4 * h + 4):
                            last = nc.scalar.activation(xn_sb[:, t, :], x_sb[:, t, :], ACT.Identity,
                                                        bias=shb[:, t % CT:t % CT + 1], scale=rsb[:, t % CT:t % CT + 1])
                        last.then_inc(s_xn, 1)

                    def conv_copy(b, g):
                        n = 8 * b + g
                        k, h = groups[g]
                        act.wait_ge(s_cv, n + 1)
                        if b >= 2:
                            act.wait_ge(s_mid, CT * (b - 2) + 4 * h + 4)
                        nc.scalar.activation(cT[b % 2][k][:, 512 * h:512 * (h + 1)], b_acc[n % 2][:], ACT.Identity,
                                             bias=conv_b[:, k:k + 1]).then_inc(s_ce, 1)

                    def z_copy(b, c):
                        act.wait_ge(s_z, CT * b + c + 1)
                        nc.scalar.activation(zr[b % 2][:, c, :], b_z[:, 0:ZW], ACT.Copy).then_inc(s_zc, 1)

                    def silus(b):
                        act.wait_ge(s_ce, 8 * b + 8)
                        act.wait_ge(s_zc, CT * b + CT)
                        act.wait_ge(s_d0, b + 1)
                        for k in (2, 3, 0, 1):
                            last = nc.scalar.activation(cT[b % 2][k][:], cT[b % 2][k][:], ACT.Silu)
                        last.then_inc(s_si, 1)
                        nc.scalar.activation(zr[b % 2][:, :, 0:INNER], zr[b % 2][:, :, 0:INNER], ACT.Silu).then_inc(s_sz, 1)

                    def dt_exp(b):
                        act.wait_ge(s_d0, b + 1)
                        nc.scalar.activation(e2[:], e1[:], ACT.Exp, scale=-1.0).then_inc(s_d1, 1)

                    def front(t):
                        i = t % 2
                        act.wait_ge(s_tk, t + 1)
                        if t >= 2:
                            act.wait_ge(s_mid, t - 1)
                            act.wait_ge(s_y, t - 1)
                            act.wait_ge(s_xd, t - 1)
                        n = INNER + STATE
                        nc.scalar.activation(tok[i][:, 0:n], b_tok[:, 0:n], ACT.Copy).then_inc(s_tc, 1)
                        nc.scalar.activation(exs[i][:], b_tok[:, n:n + 2 * HEADS], ACT.Exp)
                        act.wait_ge(s_sg, t + 1)
                        nc.scalar.activation(seg[i][:].rearrange("p h i -> p (h i)"), b_seg[:], ACT.Exp).then_inc(s_eg, 1)

                    def y_copy(t):
                        act.wait_ge(s_yt, t + 1)
                        if t >= 1:
                            act.wait_ge(s_o, t)
                        nc.scalar.activation(yT[:], b_up[:, INNER:], ACT.Copy).then_inc(s_yc, 1)
                        if t % CT == 0 and t >= 2 * CT:
                            act.wait_ge(s_x2, t // CT - 1)
                        if t >= 1:
                            act.wait_ge(s_q1, t)
                        nc.scalar.activation(junk[:], y[t % 2][:].rearrange("p h d -> p (h d)"), ACT.Square,
                                             accum_out=ssq[t // CT % 2][:, t % CT:t % CT + 1]).then_inc(s_q1, 1)

                    def out_copy(t):
                        b, c = divmod(t, CT)
                        act.wait_ge(s_o, t + 1)
                        nc.scalar.activation(ob[b % 2][:, c, :], b_z[:, 0:D], ACT.Copy).then_inc(s_oc, 1)
                        if t >= 1:
                            act.wait_ge(s_q2, t)
                        nc.scalar.activation(junk2[:], b_z[:, 0:D], ACT.Square,
                                             accum_out=ssq2[b % 2][:, c:c + 1]).then_inc(s_q2, 1)

                    norm(0, 0)
                    norm(0, 1)
                    x_high(0)
                    for g in range(8):
                        conv_copy(0, g)
                    for c in range(CT):
                        z_copy(0, c)
                    dt_exp(0)
                    norm(1, 0)
                    norm(1, 1)
                    x_high(1)
                    silus(0)
                    conv_copy(1, 0)
                    conv_copy(1, 1)
                    front(0)
                    conv_copy(1, 2)
                    for t in range(TILES):
                        b, c = divmod(t, CT)
                        more = b + 1 < B
                        if t + 1 < TILES:
                            front(t + 1)
                        if b + 2 < B and c == 5:
                            x_high(b + 2)
                        if t >= 1:
                            y_copy(t - 1)
                        if more and c < ZSTEPS:
                            z_copy(b + 1, 2 * c)
                        for ahead, g in CONVS[c]:
                            if b + ahead < B:
                                conv_copy(b + ahead, g)
                        if t >= 1:
                            out_copy(t - 1)
                        if more and c < ZSTEPS:
                            z_copy(b + 1, 2 * c + 1)
                        if more and c == 4:
                            dt_exp(b + 1)
                        if b + 2 < B and c == 4:
                            norm(b + 2, 0)
                            norm(b + 2, 1)
                        if more and c == 5:
                            silus(b + 1)
                    y_copy(TILES - 1)
                    out_copy(TILES - 1)

                @block.vector
                def _(dve):
                    ch = Chain(dve, s_c)

                    def residual(t):
                        c = t % CT
                        dve.wait_ge(s_yi[t % 4], 32 * (t // 4 + 1))
                        nc.vector.scalar_tensor_tensor(out=x_sb[:, t, :], in0=y_in[t % 4][0][:], scalar=gate[:, 0, t:t + 1],
                                                       in1=x_sb[:, t, :], op0=ALU.mult, op1=ALU.add).then_inc(s_ya, 1)
                        dve.wait_ge(s_ya, t + 1)
                        nc.vector.scalar_tensor_tensor(out=x_sb[:, t, :], in0=y_in[t % 4][1][:], scalar=gate[:, 1, t:t + 1],
                                                       in1=x_sb[:, t, :], op0=ALU.mult, op1=ALU.add).then_inc(s_yb, 1)
                        dve.wait_ge(s_yb, t + 1)
                        ch(nc.vector.bn_stats(st[:, c, :], x_sb[:, t, :]))

                    def normalise(b):
                        for c in range(CT):
                            last = nc.vector.bn_aggr(mvb[:, c, :], st[:, c, :])
                        ch(last)
                        ch(nc.vector.tensor_scalar(var[:], mvb[:, :, 1], LN_EPS, None, ALU.add))
                        if b:
                            dve.wait_ge(s_xn, 2 * b)
                        rsqrt(ch, rsb[:], var[:], tn[:])
                        nc.vector.scalar_tensor_tensor(out=shb[:], in0=mvb[:, :, 0], scalar=-1.0, in1=rsb[:],
                                                       op0=ALU.mult, op1=ALU.mult).then_inc(s_lv, 1)

                    def x_low(b):
                        for h in range(2):
                            dve.wait_ge(s_xh, 2 * b + h + 1)
                            cols = slice(4 + 512 * h, 516 + 512 * h)
                            nc.vector.tensor_tensor(xTb[1][:, cols], b_acc[h][:], xTb[0][:, cols].bitcast(fp32),
                                                    ALU.subtract).then_inc(s_xl, 1)

                    def dt_raw(b):
                        z = zr[b % 2]
                        dve.wait_ge(s_zc, CT * b + CT)
                        d = dt[b % 2]
                        ch(nc.vector.tensor_tensor(d[:], z[:, :, INNER:], bc(dt_bias[:].unsqueeze(1), [P, CT, HEADS]), ALU.add))
                        ch(nc.vector.tensor_scalar(e3[:], d[:], -1.0, None, ALU.mult))
                        nc.vector.tensor_tensor(e1[:], d[:], e3[:], ALU.max).then_inc(s_d0, 1)

                    def dt_end(b):
                        d = dt[b % 2]
                        dve.wait_ge(s_d1, b + 1)
                        ch(nc.vector.tensor_scalar(e3[:], e2[:], 2.0, None, ALU.add))
                        ch(nc.vector.reciprocal(e3[:], e3[:]))
                        ch(nc.vector.tensor_tensor(e2[:], e2[:], e3[:], ALU.mult))
                        ch(nc.vector.tensor_tensor(e1[:], e2[:], e2[:], ALU.mult))
                        ch(nc.vector.tensor_scalar(e3[:], e1[:], 2.0 / 15, None, ALU.mult))
                        for n in (13, 11, 9, 7, 5, 3):
                            ch(nc.vector.scalar_tensor_tensor(out=e3[:], in0=e3[:], scalar=2.0 / n, in1=e1[:], op0=ALU.add, op1=ALU.mult))
                        ch(nc.vector.scalar_tensor_tensor(out=e3[:], in0=e3[:], scalar=2.0, in1=e2[:], op0=ALU.add, op1=ALU.mult))
                        ch(nc.vector.scalar_tensor_tensor(out=d[:], in0=d[:], scalar=0.0, in1=e3[:], op0=ALU.max, op1=ALU.add))
                        ch(nc.vector.tensor_tensor(da[b % 2][:], d[:], bc(neg_a[:].unsqueeze(1), [P, CT, HEADS]), ALU.mult))
                        nc.vector.tensor_scalar(da[b % 2][:], da[b % 2][:], FLOOR, None, ALU.max).then_inc(s_da, 1)
                        dve.wait_ge(s_da, b + 1)

                    def mix(t):
                        b, c = divmod(t, CT)
                        i = t % 2
                        dve.wait_ge(s_g, t + 1)
                        if t >= 1:
                            dve.wait_ge(s_mm, t)
                        nc.vector.tensor_tensor(gm[:], b_g[:, 0:P], upto[:], ALU.mult).then_inc(s_gm, 1)
                        dve.wait_ge(s_tc, t + 1)
                        if t >= 2:
                            dve.wait_ge(s_mid, t - 1)
                        hd = [P, HEADS, HD]
                        nc.vector.tensor_tensor(xdt[i][:], tok[i][:, 0:INNER].rearrange("p (h d) -> p h d", d=HD),
                                                bc(dt[b % 2][:, c, :].unsqueeze(2), hd), ALU.mult).then_inc(s_x1, 1)
                        dve.wait_ge(s_eg, t + 1)
                        dve.wait_ge(s_gm, t + 1)
                        nc.vector.tensor_tensor(mm[i][:], seg[i][:], bc(gm[:].unsqueeze(1), [P, HEADS, P]), ALU.mult
                                                ).then_inc(s_mm, 1)
                        dve.wait_ge(s_x1, t + 1)
                        nc.vector.tensor_tensor(xw[i][:], xdt[i][:], bc(seg[i][:, :, P - 1:P], hd), ALU.mult).then_inc(s_xw, 1)

                    def after_mid(t):
                        b, c = divmod(t, CT)
                        i = t % 2
                        hd = [P, HEADS, HD]
                        up = b_up[:, 0:INNER].rearrange("p (h d) -> p h d", d=HD)
                        yd, yo = (b_y[:, n * INNER:(n + 1) * INNER].rearrange("p (h d) -> p h d", d=HD) for n in range(2))
                        if c:
                            ch(nc.vector.tensor_tensor(stmp[:], state[:], bc(exs[i][:, HEADS:].unsqueeze(2), hd), ALU.mult))
                        dve.wait_ge(s_mid, t + 1)
                        if c:
                            nc.vector.tensor_tensor(state[:], stmp[:], up, ALU.add).then_inc(s_st, 1)
                        else:
                            nc.vector.tensor_copy(state[:], up).then_inc(s_st, 1)
                        if t >= 2:
                            dve.wait_ge(s_yt, t - 1)
                            dve.wait_ge(s_q1, t - 1)
                        dve.wait_ge(s_xd, t + 1)
                        if c:
                            ch(nc.vector.tensor_tensor(y[i][:], yo, bc(exs[i][:, 0:HEADS].unsqueeze(2), hd), ALU.mult))
                            ch(nc.vector.tensor_tensor(y[i][:], y[i][:], xsd[i][:], ALU.add))
                            nc.vector.tensor_tensor(y[i][:], y[i][:], yd, ALU.add).then_inc(s_yd, 1)
                        else:
                            nc.vector.tensor_tensor(y[i][:], xsd[i][:], yd, ALU.add).then_inc(s_yd, 1)
                        dve.wait_ge(s_yd, t + 1)
                        dve.wait_ge(s_sz, b + 1)
                        nc.vector.tensor_tensor(y[i][:], y[i][:], zr[b % 2][:, c, 0:INNER].rearrange("p (h d) -> p h d", d=HD),
                                                ALU.mult).then_inc(s_y, 1)
                        dve.wait_ge(s_st, t + 1)

                    def finish_scale(b):
                        s = b % 2
                        dve.wait_ge(s_q2, CT * b + CT)
                        ch(nc.vector.tensor_scalar(var2[:], ssq[s][:], 1.0 / INNER, LN_EPS, ALU.mult, ALU.add))
                        ch(nc.vector.tensor_scalar(tn[:], ssq2[s][:], 1.0 / D, None, ALU.mult))
                        ch(nc.vector.scalar_tensor_tensor(out=var2[:], in0=var2[:], scalar=LN_EPS, in1=tn[:],
                                                          op0=ALU.mult, op1=ALU.add))
                        rsqrt(ch, r2[:], var2[:], tn[:])
                        dve.wait_ge(s_xn, 2 * b + 2)
                        rows = slice(CT * b, CT * b + CT)
                        ch(nc.vector.tensor_tensor(x_sb[:, rows, :], x_sb[:, rows, :], xn_sb[:, rows, :], ALU.add))

                    def finish_rows(b):
                        for c in range(CT):
                            last = nc.vector.scalar_tensor_tensor(out=x_sb[:, CT * b + c, :], in0=ob[b % 2][:, c, :],
                                                                  scalar=r2[:, c:c + 1], in1=x_sb[:, CT * b + c, :],
                                                                  op0=ALU.mult, op1=ALU.add)
                        last.then_inc(s_x2, 1)
                        dve.wait_ge(s_x2, b + 1)

                    for t in range(CT):
                        residual(t)
                    normalise(0)
                    x_low(0)
                    for t in range(CT, 2 * CT):
                        residual(t)
                    normalise(1)
                    dt_raw(0)
                    x_low(1)
                    dt_end(0)
                    for t in range(2 * CT, AHEAD):
                        residual(t)
                    mix(0)
                    for t in range(TILES):
                        b, c = divmod(t, CT)
                        if b + 1 < B and c == 4:
                            dt_raw(b + 1)
                        if t + 1 < TILES:
                            mix(t + 1)
                        if b + 2 < B and c == 5:
                            x_low(b + 2)
                        after_mid(t)
                        if t + AHEAD < TILES:
                            residual(t + AHEAD)
                        if b >= 1 and c == 1:
                            finish_scale(b - 1)
                        if b >= 1 and c == 2:
                            finish_rows(b - 1)
                        if b + 2 < B and c == 3:
                            normalise(b + 2)
                        if b + 1 < B and c == 5:
                            dt_end(b + 1)
                    finish_scale(B - 1)
                    finish_rows(B - 1)

        def combine_only(tag):
            y_in = [[sb(f"{tag}_y_in{i}{k}", [P, D]) for k in range(2)] for i in range(4)]
            s_y = [sem(f"{tag}_rows_back{i}") for i in range(4)]
            s_a = sem(f"{tag}_first_added")
            s_b = sem(f"{tag}_second_added")
            s_o = sem(f"{tag}_stored")
            with nc.Block() as block:
                @block.gpsimd
                def _(pool):
                    for t in range(TILES):
                        if t >= 4:
                            pool.wait_ge(s_b, t - 3)
                        for k in range(2):
                            pool.indirect_dma_start(out=y_in[t % 4][k][:], out_offset=None, in_=yd_dram,
                                                    in_offset=bass.IndirectOffsetOnAxis(ap=row_y[k][:, t:t + 1], axis=0)
                                                    ).then_inc(s_y[t % 4], 16)

                @block.vector
                def _(dve):
                    for t in range(TILES):
                        dve.wait_ge(s_y[t % 4], 32 * (t // 4 + 1))
                        nc.vector.scalar_tensor_tensor(out=x_sb[:, t, :], in0=y_in[t % 4][0][:], scalar=gate[:, 0, t:t + 1],
                                                       in1=x_sb[:, t, :], op0=ALU.mult, op1=ALU.add).then_inc(s_a, 1)
                        dve.wait_ge(s_a, t + 1)
                        nc.vector.scalar_tensor_tensor(out=x_sb[:, t, :], in0=y_in[t % 4][1][:], scalar=gate[:, 1, t:t + 1],
                                                       in1=x_sb[:, t, :], op0=ALU.mult, op1=ALU.add).then_inc(s_b, 1)

                @block.sync
                def _(sp):
                    for g in range(8):
                        sp.wait_ge(s_b, 8 * (g + 1))
                        sp.dma_start(out[g * SEQ:(g + 1) * SEQ, :].rearrange("(t p) d -> p t d", p=P),
                                     x_sb[:, 8 * g:8 * g + 8, :]).then_inc(s_o, 16)
                    sp.wait_ge(s_o, 128)

        route("r1")
        experts("f1")
        with ExitStack() as tmp:
            mixer(tmp)
        route("r2")
        experts("f2")
        combine_only("c2")


_INS = ['x', 'router_wT', 'w_gate', 'w_up', 'w_down', 'W_in', 'conv_wT', 'conv_bT', 'dt_bias', 'A_log', 'D', 'norm_wT', 'W_out']


def kernel(**inputs):
    import numpy as np
    import concourse.bacc as bacc
    from concourse.bass_utils import run_bass_kernel_spmd as run

    given = {k.replace("L0_attn_", "").replace("L0_ffn_", ""): np.asarray(v) for k, v in inputs.items()}
    given["x"] = given["x"].reshape(N, D)
    given["router_wT"] = given["router_w"].T
    given["conv_wT"] = given["conv_w"].T
    given["conv_bT"] = given["conv_b"].reshape(CH, P).T
    given["norm_wT"] = given["norm_w"].reshape(2, P).T
    nc = bacc.Bacc("TRN2", target_bir_lowering=False, num_devices=1)
    arrays, io = {}, {}
    for name in _INS:
        a = np.ascontiguousarray(given[name])
        arrays[f"in_{name}_dram"] = a
        io[name] = nc.dram_tensor(f"in_{name}_dram", a.shape, mybir.dt.from_np(a.dtype), kind="ExternalInput").ap()
    out = nc.dram_tensor("out_dram", (N, D), fp32, kind="ExternalOutput").ap()
    build(nc, io, out)
    r = run(nc, [arrays], core_ids=[0])
    return r.results[0]["out_dram"].reshape(BATCH, SEQ, D)
```

```python
import concourse.bass as bass
from concourse import mybir
from contextlib import ExitStack

P = 128
D = 128
BATCH, SEQ = 8, 1024
N = BATCH * SEQ
TILES = N // P
E = 8
H = 256
XB = 4
T = 512
HALF = TILES // 2
SLOTS = N // T + E - 1
REGION = N // 2 + T
WROW = 2 * H + 2 * D
LN_EPS = 1e-5
INNER = 2 * D
HEADS, HD = 4, 64
STATE = 128
CONV = INNER + 2 * STATE
CH = CONV // P
CONV_K = 4
ZW = INNER + HEADS
CT = SEQ // P
FLOOR = -110.0

fp32 = mybir.dt.float32
f32r = mybir.dt.float32r
bf16 = mybir.dt.bfloat16
i32 = mybir.dt.int32
ALU = mybir.AluOpType
ACT = mybir.ActivationFunctionType
AX = mybir.AxisListType
ds = bass.ds


class Chain:

    def __init__(self, eng, sem, base=0):
        self.eng, self.sem, self.base, self.n = eng, sem, base, 0

    def __call__(self, ins):
        ins.then_inc(self.sem, 1)
        self.n += 1
        self.eng.wait_ge(self.sem, self.base + self.n)


def bc(ap, shape):
    return ap.broadcast_to(shape)


def build(nc, io, out):
    ctx = ExitStack()
    with ctx:
        def sb(name, shape, dt=fp32):
            return ctx.enter_context(nc.sbuf_tensor(name, shape, dt))

        def sem(name):
            return ctx.enter_context(nc.semaphore(name))

        banks = [ctx.enter_context(nc.psum_tensor(f"bank{i}", [P, 512], fp32)) for i in range(8)]

        x_sb = sb("x_sb", [P, TILES, D])
        xn_sb = sb("xn_sb", [P, TILES, D])

        ident = sb("ident", [P, P])
        before_bf = sb("before_bf", [P, P], bf16)
        ones_bf = sb("ones_bf", [P, P], bf16)
        upto = sb("upto", [P, P])
        after = sb("after", [P, P])
        ones = sb("ones", [P, P])
        rank8 = sb("rank8", [P, E])
        earlier8 = sb("earlier8", [P, E, E])
        thresh = sb("thresh", [P, N // 2 // T])
        region = sb("region", [P, E])
        region_step = sb("region_step", [P, E])
        zeros = sb("zeros", [P, T // P * D])
        slot_no = sb("slot_no", [P, SLOTS])

        rw_sb = sb("rw_sb", [D, E])

        wc = [sb("wc_high", [D, CONV_K, CONV], f32r), sb("wc_low", [D, CONV_K, CONV], f32r)]
        wz = [sb("wz_high", [D, ZW], f32r), sb("wz_low", [D, ZW], f32r)]
        conv_b = sb("conv_b", [P, CH])
        w_out = sb("w_out", [P, 2, D])
        dt_bias = sb("dt_bias", [P, HEADS])
        neg_a = sb("neg_a", [P, HEADS])
        d_skip = sb("d_skip", [P, HEADS])

        w_dram = nc.dram_tensor("w_split", (E * P, 2 * WROW), fp32, kind="Internal").ap()
        xd_dram = [nc.dram_tensor(f"x_dispatched{h}", (E * REGION, D), fp32, kind="Internal").ap() for h in range(2)]
        yd_dram = [nc.dram_tensor(f"y_dispatched{h}", (SLOTS * T, D), fp32, kind="Internal").ap() for h in range(2)]

        class Norms:
            s_factors = sem("ln_factors")
            s_done = sem("ln_done")
            s_chain = sem("ln_chain")
            chained = 0

            def __init__(self):
                self.st = sb("ln_stats", [P, CT, 6])
                self.mv = sb("ln_moments", [P, CT, 2])
                self.var = sb("ln_var", [P, CT])
                self.tmp = sb("ln_newton", [P, CT])
                self.rstd = sb("ln_rstd", [P, CT])
                self.shift = sb("ln_shift", [P, CT])

            def stats(self, chain, t):
                chain(nc.vector.bn_stats(self.st[:, t % CT, :], x_sb[:, t, :]))

            def factors(self, dve, chain, b):
                for c in range(CT):
                    last = nc.vector.bn_aggr(self.mv[:, c, :], self.st[:, c, :])
                chain(last)
                chain(nc.vector.tensor_scalar(self.var[:], self.mv[:, :, 1], LN_EPS, None, ALU.add))
                if b:
                    dve.wait_ge(self.s_done, 2 * b)
                rsqrt(chain, self.rstd[:], self.var[:], self.tmp[:])
                nc.vector.scalar_tensor_tensor(out=self.shift[:], in0=self.mv[:, :, 0], scalar=-1.0, in1=self.rstd[:],
                                               op0=ALU.mult, op1=ALU.mult).then_inc(self.s_factors, 1)

            def act(self, act, b, h):
                act.wait_ge(self.s_factors, b + 1)
                for c in range(4 * h, 4 * h + 4):
                    last = nc.scalar.activation(xn_sb[:, CT * b + c, :], x_sb[:, CT * b + c, :], ACT.Identity,
                                                bias=self.shift[:, c:c + 1], scale=self.rstd[:, c:c + 1])
                last.then_inc(self.s_done, 1)

        norms = Norms()

        class MixerWeights:
            STEPS = CONV_K + 2

            def __init__(self, tb):
                self.w_in = tb("w_in", [D, ZW + CONV])
                self.cw = tb("conv_w_rows", [D, CONV_K, CONV])
                self.scaled = tb("w_scaled", [D, CONV])
                self.norm_w = tb("norm_w", [P, 2])
                self.s_in = sem("mixer_weights_in")
                self.s_a = sem("mixer_a_exp")
                self.s_al = sem("mixer_a_clamped")
                self.s_chain = sem("mixer_weights_chain")

            def load(self, sp):
                for to, of in ((self.w_in[:], io["W_in"]), (self.cw[:], io["conv_wT"].partition_broadcast(P)),
                               (conv_b[:], io["conv_bT"]), (w_out[:], io["W_out"].rearrange("(c p) d -> p c d", p=P)),
                               (self.norm_w[:], io["norm_wT"]), (dt_bias[:], io["dt_bias"].partition_broadcast(P)),
                               (neg_a[:], io["A_log"].partition_broadcast(P)), (d_skip[:], io["D"].partition_broadcast(P))):
                    sp.dma_start(to, of).then_inc(self.s_in, 16)

            def start(self, dve):
                self.c = Chain(dve, self.s_chain)
                dve.wait_ge(self.s_in, 16 * 8)

            def split(self, high, low, of):
                self.c(nc.vector.tensor_copy(high, of))
                self.c(nc.vector.tensor_tensor(low, of, high.bitcast(fp32), ALU.subtract))

            def dve(self, dve, step):
                c = self.c
                if step < CONV_K:
                    c(nc.vector.tensor_tensor(self.scaled[:], self.w_in[:, INNER:INNER + CONV], self.cw[:, step, :], ALU.mult))
                    self.split(wc[0][:, step, :], wc[1][:, step, :], self.scaled[:])
                elif step == CONV_K:
                    for to, of in ((slice(0, INNER), slice(0, INNER)), (slice(INNER, ZW), slice(INNER + CONV, ZW + CONV))):
                        self.split(wz[0][:, to], wz[1][:, to], self.w_in[:, of])
                else:
                    for k in range(2):
                        c(nc.vector.tensor_scalar(w_out[:, k, :], w_out[:, k, :], self.norm_w[:, k:k + 1], None, ALU.mult))
                    nc.vector.tensor_scalar(neg_a[:], neg_a[:], 88.0, None, ALU.min).then_inc(self.s_al, 1)

            def act_end(self, act):
                act.wait_ge(self.s_al, 1)
                nc.scalar.activation(neg_a[:], neg_a[:], ACT.Exp).then_inc(self.s_a, 1)

            def dve_end(self, dve):
                dve.wait_ge(self.s_a, 1)
                self.c(nc.vector.tensor_scalar(neg_a[:], neg_a[:], -1.0, None, ALU.mult))

        class Setup:

            def __init__(self, tb):
                self.w_raw = tb("w_raw", [P, 2, WROW])
                self.w_two = [tb(f"w_two{i}", [P, 2 * WROW], f32r) for i in range(2)]
                self.s_x = [sem(f"x_loaded{b}") for b in range(BATCH // 2)]
                self.s_rw = sem("router_loaded")
                self.s_const = sem("constants_made")
                self.s_raw = [sem("raw_loaded0"), sem("raw_loaded1")]
                self.s_high = sem("weights_high")
                self.s_split = sem("weights_split")
                self.s_wst = [sem("weights_stored0"), sem("weights_stored1")]

            def sp(self, sp):
                for b in range(BATCH):
                    sp.dma_start(x_sb[:, CT * b:CT * b + CT, :],
                                 io["x"][b * SEQ:(b + 1) * SEQ, :].rearrange("(t p) d -> p t d", p=P)).then_inc(self.s_x[b // 2], 16)
                    if b == 0:
                        sp.dma_start(rw_sb[:], io["router_wT"]).then_inc(self.s_rw, 16)
                mixer_weights.load(sp)
                for e in range(E):
                    if e >= 2:
                        sp.wait_ge(self.s_split, e - 1)
                    raw = self.w_raw[:, e % 2, :]
                    sp.dma_start(raw[:, 0:H], io["w_gate"][e]).then_inc(self.s_raw[e % 2], 16)
                    sp.dma_start(raw[:, H:2 * H], io["w_up"][e]).then_inc(self.s_raw[e % 2], 16)
                    sp.dma_start(raw[:, 2 * H:].rearrange("p (c d) -> p c d", c=2),
                                 io["w_down"][e].rearrange("(c p) d -> p c d", p=P)).then_inc(self.s_raw[e % 2], 16)

            def act(self, act, q):
                act.wait_ge(self.s_split, q + 1)
                act.dma_start(w_dram[q * P:(q + 1) * P, :], self.w_two[q % 2][:].bitcast(fp32)).then_inc(self.s_wst[q % 2], 16)

            def act_end(self, act):
                for i in range(2):
                    act.wait_ge(self.s_wst[i], 16 * E // 2)

            def dve(self, dve, e):
                dve.wait_ge(self.s_raw[e % 2], 48 * (e // 2 + 1))
                if e >= 2:
                    dve.wait_ge(self.s_wst[e % 2], 16 * (e // 2))
                w = self.w_two[e % 2]
                nc.vector.tensor_copy(w[:, 0:WROW], self.w_raw[:, e % 2, :]).then_inc(self.s_high, 1)
                dve.wait_ge(self.s_high, e + 1)
                nc.vector.tensor_tensor(w[:, WROW:], self.w_raw[:, e % 2, :], w[:, 0:WROW].bitcast(fp32),
                                        ALU.subtract).then_inc(self.s_split, 1)

            def pool(self, pool):
                c = Chain(pool, sem("constants_chain"))
                nc.gpsimd.memset(ones[:], 1.0)
                nc.gpsimd.memset(ones_bf[:], 1.0)
                nc.gpsimd.memset(ident[:], 0.0)
                nc.gpsimd.memset(earlier8[:], 1.0)
                nc.gpsimd.memset(zeros[:], 0.0)
                c(nc.gpsimd.memset(region_step[:], float(REGION)))
                up = dict(pattern=[[1, P]], base=0, channel_multiplier=-1, fill=0.0)
                down = dict(pattern=[[-1, P]], base=0, channel_multiplier=1)
                nc.gpsimd.affine_select(out=ident[:], in_=ident[:], compare_op=ALU.not_equal, fill=1.0, **down)
                nc.gpsimd.affine_select(out=before_bf[:], in_=ones_bf[:], compare_op=ALU.is_gt, **up)
                nc.gpsimd.affine_select(out=upto[:], in_=ones[:], compare_op=ALU.is_ge, **up)
                nc.gpsimd.affine_select(out=after[:], in_=ones[:], compare_op=ALU.is_gt, fill=0.0, **down)
                nc.gpsimd.affine_select(out=earlier8[:], in_=earlier8[:], compare_op=ALU.is_gt,
                                        pattern=[[1, E], [-1, E]], base=0, channel_multiplier=0, fill=0.0)
                nc.gpsimd.memset(region_step[:, 0:1], 0.0)
                for to, pattern, base in ((rank8, [[-1, E]], E), (thresh, [[T, N // 2 // T]], 0), (slot_no, [[1, SLOTS]], 0),
                                          (region, [[REGION, E]], 0)):
                    last = nc.gpsimd.iota(to[:], pattern=pattern, base=base, channel_multiplier=0,
                                          allow_small_or_imprecise_dtypes=True)
                c(last)
                pool.sem_inc(self.s_const, 1)

        gate = sb("gate", [P, 2, TILES])
        slots_used = sb("slots_used", [P, 2], i32)
        slot_at = sb("slot_at", [P, 2, 2, SLOTS], i32)
        row = [sb("row1", [P, TILES], i32), sb("row2", [P, TILES], i32)]
        row_y = [sb("row_y1", [P, TILES], i32), sb("row_y2", [P, TILES], i32)]

        def rsqrt(c, r, v, tmp):
            c(nc.vector.tensor_scalar(r.bitcast(i32), v.bitcast(i32), -0.5, float(0x5F3759DF), ALU.mult, ALU.add))
            for _ in range(3):
                c(nc.vector.tensor_tensor(tmp, r, r, ALU.mult))
                c(nc.vector.scalar_tensor_tensor(out=tmp, in0=tmp, scalar=-0.5, in1=v, op0=ALU.mult, op1=ALU.mult))
                c(nc.vector.scalar_tensor_tensor(out=r, in0=tmp, scalar=1.5, in1=r, op0=ALU.add, op1=ALU.mult))

        def scatter(t, sent):
            for k in range(2):
                nc.gpsimd.indirect_dma_start(out=xd_dram[t // HALF], in_=xn_sb[:, t, :], in_offset=None,
                                             out_offset=bass.IndirectOffsetOnAxis(ap=row[k][:, t:t + 1], axis=0)
                                             ).then_inc(sent, 16)

        def gather(t, to, back):
            for k in range(2):
                nc.gpsimd.indirect_dma_start(out=to[k][:], out_offset=None, in_=yd_dram[t // HALF],
                                             in_offset=bass.IndirectOffsetOnAxis(ap=row_y[k][:, t:t + 1], axis=0)
                                             ).then_inc(back, 16)

        class Combine:
            s_back = [sem(f"rows_back{i}") for i in range(4)]
            s_one = sem("first_added")
            s_both = sem("both_added")

            def __init__(self, tb, layer):
                self.shift = TILES * layer
                self.y_in = [[tb(f"y_in{i}{k}", [P, D]) for k in range(2)] for i in range(4)]

            def wait_done(self, eng, tiles):
                eng.wait_ge(self.s_both, tiles + self.shift)

            def pool(self, pool, t):
                n = t + self.shift
                if n >= 4:
                    pool.wait_ge(self.s_both, n - 3)
                gather(t, self.y_in[n % 4], self.s_back[n % 4])

            def dve(self, dve, t):
                n = t + self.shift
                dve.wait_ge(self.s_back[n % 4], 32 * (n // 4 + 1))
                y = self.y_in[n % 4]
                nc.vector.scalar_tensor_tensor(out=x_sb[:, t, :], in0=y[0][:], scalar=gate[:, 0, t:t + 1],
                                               in1=x_sb[:, t, :], op0=ALU.mult, op1=ALU.add).then_inc(self.s_one, 1)
                dve.wait_ge(self.s_one, n + 1)
                nc.vector.scalar_tensor_tensor(out=x_sb[:, t, :], in0=y[1][:], scalar=gate[:, 1, t:t + 1],
                                               in1=x_sb[:, t, :], op0=ALU.mult, op1=ALU.add).then_inc(self.s_both, 1)

        G = 16
        XG = G // 4
        Q = TILES // G
        QH = Q // 2
        ROUTED = Q - 1

        def router(tag, tb):
            stats = tb("stats", [P, 2, G, 6])
            mv = tb("mv", [P, 2, G, 2])
            var = tb("var", [P, G])
            rstd = tb("rstd", [P, 2, G])
            shift = tb("shift", [P, 2, G])
            ntmp = tb("newton", [P, G])
            logit = tb("logit", [P, G, E])
            sel = tb("sel", [P, 2, TILES, E])
            best = tb("best", [P, 2, TILES])
            gsum = tb("gsum", [P, TILES])
            work = tb("work", [P, G, E])
            work2 = tb("work2", [P, G])
            selb = [tb(f"selb{i}", [P, G, E], bf16) for i in range(2)]
            carry = [tb(f"carry{i}", [P, E], bf16) for i in range(2)]
            tsum = tb("tsum", [P, E])
            at = tb("at", [P, G, E])
            cmp8t = tb("cmp8t", [P, E, N // 2 // T])
            need = tb("need", [P, E])
            total = tb("total", [P, 1])
            count = tb("count", [P, E])
            cmp8 = tb("cmp8", [P, E, E])
            first = tb("first", [P, E])
            offset = tb("offset", [P, E])
            step = tb("step", [P, E])
            cmpslot = tb("cmpslot", [P, SLOTS, E])
            slotf = tb("slotf", [P, 2, SLOTS])
            pad_at = tb("pad_at", [P, 2, E], i32)
            big = tb("big", [P, HALF, E])
            big2 = tb("big2", [P, HALF])

            s_ms = sem(f"{tag}_moments")
            s_xn = sem(f"{tag}_normed")
            s_tr = sem(f"{tag}_transposed")
            s_xT = sem(f"{tag}_xT_in_sbuf")
            s_lg = sem(f"{tag}_logits_made")
            s_ch = sem(f"{tag}_chain")
            s_gt = sem(f"{tag}_sigmoid")
            s_lread = sem(f"{tag}_logits_read")
            s_cread = sem(f"{tag}_counts_read")
            s_selb = sem(f"{tag}_selected")
            s_cnt = sem(f"{tag}_counted")
            s_row = sem(f"{tag}_rows_known")
            s_total = sem(f"{tag}_totals")
            s_tread = sem(f"{tag}_totals_read")
            s_pad = sem(f"{tag}_pads_known")
            s_pw = sem(f"{tag}_pads_written")
            s_sent = sem(f"{tag}_rows_sent")

            class Router:
                signals = dict(chain=s_ch, logits_read=s_lread, counts_read=s_cread, turned_read=s_xT, rows=s_row,
                               chosen=s_selb, sigmoid=s_gt, pads=s_pad, pads_written=s_pw, sent=s_sent, total_read=s_tread)
                chained = 0
                xT = None

                @staticmethod
                def stats(dve, c, q, tiles):
                    if q >= 2:
                        dve.wait_ge(s_xn, XG * (q - 1))
                    for j in tiles:
                        last = nc.vector.bn_stats(stats[:, q % 2, j, :], x_sb[:, G * q + j, :])
                    c(last)

                @staticmethod
                def moments(dve, c, q):
                    i = q % 2
                    for j in range(G):
                        last = nc.vector.bn_aggr(mv[:, i, j, :], stats[:, i, j, :])
                    c(last)
                    c(nc.vector.tensor_scalar(var[:], mv[:, i, :, 1], LN_EPS, None, ALU.add))
                    rsqrt(c, rstd[:, i, :], var[:], ntmp[:])
                    nc.vector.scalar_tensor_tensor(out=shift[:, i, :], in0=mv[:, i, :, 0], scalar=-1.0,
                                                   in1=rstd[:, i, :], op0=ALU.mult, op1=ALU.mult).then_inc(s_ms, 1)

                @staticmethod
                def choose(dve, c, q, bank):
                    i = q % 2
                    tiles = slice(G * q, G * q + G)
                    full = [P, G, E]
                    dve.wait_ge(s_lg, q + 1)
                    nc.vector.tensor_copy(logit[:], bank[:, 0:G * E].rearrange("p (j e) -> p j e", e=E)).then_inc(s_lread, 1)
                    dve.wait_ge(s_lread, q + 1)
                    for k in range(2):
                        c(nc.vector.tensor_reduce(best[:, k, tiles], logit[:], AX.X, ALU.max))
                        c(nc.vector.tensor_tensor(work[:], logit[:], bc(best[:, k, tiles].unsqueeze(2), full), ALU.is_equal))
                        c(nc.vector.tensor_tensor(work[:], work[:], bc(rank8[:].unsqueeze(1), full), ALU.mult))
                        c(nc.vector.tensor_reduce(work2[:], work[:], AX.X, ALU.max))
                        c(nc.vector.tensor_tensor(sel[:, k, tiles, :], work[:], bc(work2[:].unsqueeze(2), full), ALU.is_equal))
                        if k == 0:
                            c(nc.vector.scalar_tensor_tensor(out=logit[:], in0=sel[:, 0, tiles, :], scalar=-3e38,
                                                             in1=logit[:], op0=ALU.mult, op1=ALU.add))
                    nc.vector.tensor_tensor(selb[i][:], sel[:, 0, tiles, :], sel[:, 1, tiles, :], ALU.add
                                            ).then_inc(s_selb, 1)
                    dve.wait_ge(s_selb, q + 1)
                    c(nc.vector.tensor_reduce(tsum[:], selb[i][:].rearrange("p t e -> p e t"), AX.X, ALU.add))
                    if q >= 1:
                        dve.wait_ge(s_cnt, q)
                    if q % QH:
                        c(nc.vector.tensor_tensor(carry[(q + 1) % 2][:], carry[i][:], tsum[:], ALU.add))
                    else:
                        c(nc.vector.tensor_copy(carry[(q + 1) % 2][:], tsum[:]))

                @staticmethod
                def place(dve, c, q, bank):
                    tiles = slice(G * q, G * q + G)
                    dve.wait_ge(s_cnt, q + 1)
                    nc.vector.tensor_tensor(at[:], bank[:, 0:G * E].rearrange("p (j e) -> p j e", e=E),
                                              bc(region[:].unsqueeze(1), [P, G, E]), ALU.add).then_inc(s_cread, 1)
                    dve.wait_ge(s_cread, q + 1)
                    for k in range(2):
                        c(nc.vector.tensor_tensor(work[:], at[:], sel[:, k, tiles, :], ALU.mult))
                        c(nc.vector.tensor_reduce(work2[:], work[:], AX.X, ALU.add))
                        c(nc.vector.tensor_copy(row[k][:, tiles], work2[:]))
                    nc.vector.tensor_copy(work2[:, 0:1], row[0][:, G * q:G * q + 1]).then_inc(s_row, 1)

                @staticmethod
                def slots(dve, c, h, bank):
                    dve.wait_ge(s_total, h + 1)
                    nc.vector.tensor_copy(count[:], bank[:, G * E:G * E + E]).then_inc(s_tread, 1)
                    dve.wait_ge(s_tread, h + 1)
                    c(nc.vector.tensor_tensor(step[:], count[:], region[:], ALU.add))
                    nc.vector.tensor_copy(pad_at[:, h, :], step[:]).then_inc(s_pad, 1)
                    ns = [P, E, N // 2 // T]
                    c(nc.vector.tensor_tensor(cmp8t[:], bc(count[:].unsqueeze(2), ns), bc(thresh[:].unsqueeze(1), ns), ALU.is_gt))
                    c(nc.vector.tensor_reduce(need[:], cmp8t[:], AX.X, ALU.add))
                    c(nc.vector.tensor_reduce(total[:], need[:], AX.X, ALU.add))
                    c(nc.vector.tensor_copy(slots_used[:, h:h + 1], total[:]))
                    c(nc.vector.tensor_tensor(cmp8[:], bc(need[:].unsqueeze(1), [P, E, E]), earlier8[:], ALU.mult))
                    c(nc.vector.tensor_reduce(first[:], cmp8[:], AX.X, ALU.add))
                    c(nc.vector.scalar_tensor_tensor(out=offset[:], in0=first[:], scalar=-float(T), in1=region[:],
                                                     op0=ALU.mult, op1=ALU.add))
                    c(nc.vector.tensor_copy(step[:], region_step[:]))
                    c(nc.vector.scalar_tensor_tensor(out=step[:, 1:], in0=need[:, 0:E - 1], scalar=-float(T),
                                                     in1=region_step[:, 1:], op0=ALU.mult, op1=ALU.add))
                    ns = [P, SLOTS, E]
                    c(nc.vector.tensor_tensor(cmpslot[:], bc(slot_no[:].unsqueeze(2), ns), bc(first[:].unsqueeze(1), ns), ALU.is_ge))
                    c(nc.vector.tensor_reduce(slotf[:, 0, :], cmpslot[:], AX.X, ALU.add))
                    c(nc.vector.tensor_scalar(slotf[:, 0, :], slotf[:, 0, :], -1.0, float(P), ALU.add, ALU.mult))
                    c(nc.vector.tensor_tensor(cmpslot[:], cmpslot[:], bc(step[:].unsqueeze(1), ns), ALU.mult))
                    c(nc.vector.tensor_reduce(slotf[:, 1, :], cmpslot[:], AX.X, ALU.add))
                    c(nc.vector.scalar_tensor_tensor(out=slotf[:, 1, :], in0=slot_no[:], scalar=float(T), in1=slotf[:, 1, :],
                                                     op0=ALU.mult, op1=ALU.add))
                    c(nc.vector.scalar_tensor_tensor(out=slotf[:, 1, :], in0=slot_no[:], scalar=total[:, 0:1],
                                                     in1=slotf[:, 1, :], op0=ALU.is_lt, op1=ALU.mult))
                    c(nc.vector.tensor_copy(slot_at[:, h, :, :], slotf[:]))
                    full = [P, HALF, E]
                    tiles = slice(HALF * h, HALF * h + HALF)
                    for k in range(2):
                        c(nc.vector.tensor_tensor(big[:], sel[:, k, tiles, :], bc(offset[:].unsqueeze(1), full), ALU.mult))
                        c(nc.vector.tensor_reduce(big2[:], big[:], AX.X, ALU.add))
                        c(nc.vector.tensor_tensor(row_y[k][:, tiles], row[k][:, tiles], big2[:], ALU.subtract))

                @staticmethod
                def norm(act, q, h):
                    i = q % 2
                    act.wait_ge(s_ms, q + 1)
                    for j in range(4 * h, 4 * h + 4):
                        last = nc.scalar.activation(xn_sb[:, G * q + j, :], x_sb[:, G * q + j, :], ACT.Identity,
                                                    bias=shift[:, i, j:j + 1], scale=rstd[:, i, j:j + 1])
                    last.then_inc(s_xn, 1)

                @staticmethod
                def xT_copy(act, q, h, bank):
                    xT = Router.xT
                    if q >= len(xT):
                        act.wait_ge(s_lg, q - len(xT) + 1)
                    act.wait_ge(s_tr, XG * q + h + 1)
                    nc.scalar.activation(xT[q % len(xT)][:, 512 * h:512 * h + 512], bank[:], ACT.Copy).then_inc(s_xT, 1)

                @staticmethod
                def turn(pe, q, h, bank):
                    pe.wait_ge(s_xn, XG * q + h + 1)
                    if q >= 1:
                        pe.wait_ge(s_xT, XG * (q - 1) + h + 1)
                    for j in range(4):
                        last = pe.transpose(bank[:, j * P:(j + 1) * P], xn_sb[:, G * q + 4 * h + j, :], ident[:])
                    last.then_inc(s_tr, 1)

                @staticmethod
                def logits(pe, q, bank):
                    xT = Router.xT
                    if q >= 2:
                        pe.wait_ge(s_lread, q - 1)
                    for j in range(G):
                        if j % 4 == 0:
                            pe.wait_ge(s_xT, XG * q + j // 4 + 1)
                        last = pe.matmul(bank[:, j * E:(j + 1) * E], xT[q % len(xT)][:, j * P:(j + 1) * P], rw_sb[:],
                                         start=True, stop=True)
                    last.then_inc(s_lg, 1)

                @staticmethod
                def counts(pe, q, bank):
                    pe.wait_ge(s_selb, q + 1)
                    if q >= 2:
                        pe.wait_ge(s_cread, q - 1)
                    s = selb[q % 2]
                    out3 = bank[:, 0:G * E]
                    pe.matmul(out3, before_bf[:], s[:].rearrange("p t e -> p (t e)"), start=True, stop=False)
                    if q % QH:
                        pe.matmul(out3.rearrange("p (t e) -> p t e", e=E), ones_bf[:],
                                  bc(carry[q % 2][:].unsqueeze(1), [P, G, E]), start=False, stop=False)
                    for j in range(G - 1):
                        last = pe.matmul(bank[:, (j + 1) * E:G * E].rearrange("p (t e) -> p t e", e=E), ones_bf[:],
                                         bc(s[:, j:j + 1, :], [P, G - 1 - j, E]), start=False, stop=(j == G - 2))
                    last.then_inc(s_cnt, 1)

                @staticmethod
                def total(pe, h, bank):
                    pe.wait_ge(s_row, QH * (h + 1))
                    pe.matmul(bank[:, G * E:G * E + E], ones_bf[:], carry[QH * (h + 1) % 2][:], start=True,
                              stop=True).then_inc(s_total, 1)

                @staticmethod
                def gates(dve, c):
                    dve.wait_ge(s_gt, 1)
                    c(nc.vector.tensor_tensor(gsum[:], gate[:, 0, :], gate[:, 1, :], ALU.add))
                    c(nc.vector.tensor_scalar(gsum[:], gsum[:], 1e-10, None, ALU.add))
                    c(nc.vector.reciprocal(gsum[:], gsum[:]))
                    for k in range(2):
                        c(nc.vector.scalar_tensor_tensor(out=gate[:, k, :], in0=gate[:, k, :], scalar=0.5, in1=gsum[:],
                                                         op0=ALU.mult, op1=ALU.mult))

                @staticmethod
                def sigmoid(act):
                    act.wait_ge(s_selb, Q)
                    nc.scalar.activation(gate[:], best[:], ACT.Sigmoid).then_inc(s_gt, 1)

                @staticmethod
                def scatter(pool, t):
                    if t % G == 0:
                        pool.wait_ge(s_row, t // G + 1)
                    scatter(t, s_sent)

                @staticmethod
                def pads(sp, h):
                    sp.wait_ge(s_pad, h + 1)
                    for e in range(E):
                        at_e = sp.value_load(pad_at[0:1, h, e:e + 1], min_val=0, max_val=E * REGION - T)
                        sp.dma_start(xd_dram[h][ds(at_e, T), :].rearrange("(p j) d -> p (j d)", p=P),
                                     zeros[:]).then_inc(s_pw, 16)

            return Router

        def route(r, tb, setup, start=0):
            b_x, b_l, b_p = banks[0:4], banks[4:6], banks[6:8]
            r.xT = [tb(f"xT{i}", [D, G * P]) for i in range(2)]
            with nc.Block() as block:
                @block.vector
                def _(dve):
                    c = Chain(dve, r.signals["chain"], r.chained)
                    for q in range(start, min(start + 2, Q)):
                        if setup:
                            dve.wait_ge(setup.s_x[q], 32)
                        r.stats(dve, c, q, range(G))
                        r.moments(dve, c, q)
                    if setup:
                        dve.wait_ge(setup.s_const, 1)
                    if start >= QH:
                        r.slots(dve, c, 0, b_p[0])
                    for q in range(start, Q):
                        r.choose(dve, c, q, b_l[q % 2])
                        if q == start:
                            r.place(dve, c, q, b_p[q % 2])
                        if q + 2 < Q:
                            if setup:
                                dve.wait_ge(setup.s_x[q + 2], 32)
                            r.stats(dve, c, q + 2, range(G))
                            r.moments(dve, c, q + 2)
                        if q > start:
                            r.place(dve, c, q, b_p[q % 2])
                        if setup:
                            for e in range(E // Q * q, E // Q * (q + 1)):
                                setup.dve(dve, e)
                        if q % QH == QH - 1:
                            r.slots(dve, c, q // QH, b_p[0])
                    r.gates(dve, c)

                @block.scalar
                def _(act):
                    if setup:
                        act.wait_ge(setup.s_x[0], 32)
                    for h in range(XG):
                        r.norm(act, start, h)
                        if h >= 1:
                            r.xT_copy(act, start, h - 1, b_x[h - 1])
                    r.xT_copy(act, start, XG - 1, b_x[XG - 1])
                    if setup:
                        act.wait_ge(setup.s_x[1], 32)
                    if start + 1 < Q:
                        for h in range(XG):
                            r.norm(act, start + 1, h)
                    for q in range(start, Q):
                        if q + 1 < Q:
                            for h in range(XG):
                                r.xT_copy(act, q + 1, h, b_x[h])
                        if q + 2 < Q:
                            if setup:
                                act.wait_ge(setup.s_x[q + 2], 32)
                            for h in range(XG):
                                r.norm(act, q + 2, h)
                        if setup and q >= 1:
                            for e in range(E // Q * (q - 1), E // Q * q):
                                setup.act(act, e)
                    if setup:
                        for e in range(E // Q * (Q - 1), E):
                            setup.act(act, e)
                    r.sigmoid(act)
                    if setup:
                        setup.act_end(act)

                @block.tensor
                def _(pe):
                    def turn(q):
                        for h in range(XG):
                            r.turn(pe, q, h, b_x[h])

                    if setup:
                        pe.wait_ge(setup.s_const, 1)
                        pe.wait_ge(setup.s_rw, 16)
                    if start >= QH:
                        r.total(pe, 0, b_p[0])
                    turn(start)
                    r.logits(pe, start, b_l[start % 2])
                    if start + 1 < Q:
                        turn(start + 1)
                    for q in range(start, Q):
                        if q == start:
                            r.counts(pe, q, b_p[q % 2])
                        if q + 1 < Q:
                            r.logits(pe, q + 1, b_l[(q + 1) % 2])
                        if q > start:
                            if q == QH:
                                pe.wait_ge(r.signals["total_read"], 1)
                            r.counts(pe, q, b_p[q % 2])
                        if q % QH == QH - 1:
                            r.total(pe, q // QH, b_p[0])
                        if q + 2 < Q:
                            turn(q + 2)

                @block.gpsimd
                def _(pool):
                    if setup:
                        setup.pool(pool)
                    if start == 0:
                        for t in range(HALF):
                            r.scatter(pool, t)
                    pool.wait_ge(r.signals["sent"], 16 * 2 * HALF)

                @block.sync
                def _(sp):
                    if setup:
                        setup.sp(sp)
                    for h in range(2):
                        r.pads(sp, h)
                    sp.wait_ge(r.signals["pads_written"], 16 * 2 * E)

        def experts(tag, besides):
            with ExitStack() as tmp:
                experts_in(tag, besides, lambda name, shape, dt=fp32: tmp.enter_context(nc.sbuf_tensor(f"{tag}_{name}", shape, dt)))

        def experts_in(tag, besides, tb):
            w_slot = [tb(f"w_slot{i}", [P, 2 * WROW], f32r) for i in range(3)]
            xr = [tb(f"xr{i}", [P, 4, D]) for i in range(XB)]
            xh = [tb(f"xh{i}", [D, T], f32r) for i in range(2)]
            xl = [tb(f"xl{i}", [D, T], f32r) for i in range(2)]
            sg = [tb(f"sg{i}", [P, T]) for i in range(2)]
            hf = [tb(f"hf{i}", [P, T]) for i in range(2)]
            hh = [[tb(f"hh{i}{c}", [P, T], f32r) for c in range(2)] for i in range(2)]
            hl = [[tb(f"hl{i}{c}", [P, T], f32r) for c in range(2)] for i in range(2)]
            oT = [tb(f"oT{i}", [D, T]) for i in range(2)]
            yr = [tb(f"yr{i}", [P, 4, D]) for i in range(2)]
            s_w = [sem(f"{tag}_weights_in{i}") for i in range(3)]
            s_xr = [sem(f"{tag}_rows_in{i}") for i in range(XB)]
            s_tr = sem(f"{tag}_x_turned")
            s_xh = sem(f"{tag}_x_high")
            s_xl = sem(f"{tag}_x_low")
            s_gu = sem(f"{tag}_gate_up")
            s_sg = sem(f"{tag}_silu")
            s_hf = sem(f"{tag}_hidden")
            s_hh = [sem(f"{tag}_hidden_high{c}") for c in range(2)]
            s_hl = sem(f"{tag}_hidden_low")
            s_dn = sem(f"{tag}_down")
            s_oT = sem(f"{tag}_down_copied")
            s_ot = sem(f"{tag}_out_turned")
            s_yr = sem(f"{tag}_out_rows")
            s_yo = [sem(f"{tag}_out_stored{i}") for i in range(2)]
            s_sent = sem(f"{tag}_rows_sent")
            combine = Combine(tb, int(tag == "f2"))
            yd = [y.rearrange("(t p j) d -> t p j d", p=P, j=4) for y in yd_dram]
            TOTAL = 2 * SLOTS
            MIN_SLOTS = N // T
            LAST = TOTAL - 1
            COMBINE = SLOTS + 4
            b_x, b_g, b_u, b_d, b_o = banks[0], banks[1:3], banks[3:5], banks[5], banks[6]

            class Used:

                def __init__(self, eng):
                    self.eng = eng
                    self.used = [eng.alloc_register(f"{tag}_used{h}") for h in range(2)]
                    for h in range(2):
                        eng.reg_load(self.used[h], slots_used[0:1, h:h + 1])

                def __call__(self, t, piece):
                    h, n = divmod(t, SLOTS)
                    if n < MIN_SLOTS:
                        piece(True)
                        return
                    with self.eng.If_cmp(self.used[h], n, "IS_GT"):
                        piece(True)
                    with self.eng.Else():
                        piece(False)

            with nc.Block() as block:
                @block.sync
                def _(sp):
                    used = Used(sp)

                    def load(t, real):
                        h, n = divmod(t, SLOTS)
                        s = t % XB
                        if t >= XB:
                            sp.wait_ge(s_tr, t - XB + 1)
                        if t == SLOTS:
                            sp.wait_ge(s_sent, 16 * 2 * HALF)
                        if real:
                            at = sp.value_load(slot_at[0:1, h, 1, n:n + 1], min_val=0, max_val=E * REGION - T)
                            sp.dma_start(xr[s][:], xd_dram[h][ds(at, T), :].rearrange("(p j) d -> p j d", p=P)).then_inc(s_xr[s], 16)
                        else:
                            sp.sem_inc(s_xr[s], 16)

                    def load_weights(t, real):
                        h, n = divmod(t, SLOTS)
                        if t >= 3:
                            sp.wait_ge(s_dn, t - 2)
                        if real:
                            at = sp.value_load(slot_at[0:1, h, 0, n:n + 1], min_val=0, max_val=(E - 1) * P)
                            sp.dma_start(w_slot[t % 3][:].bitcast(fp32), w_dram[ds(at, P), :]).then_inc(s_w[t % 3], 16)
                        else:
                            sp.sem_inc(s_w[t % 3], 16)

                    def store(t, real):
                        sp.wait_ge(s_yr, t + 1)
                        if t >= 2:
                            sp.wait_ge(s_yo[t % 2], 16 * (t // 2))
                        of = yr[t % 2][:] if real else zeros[:].rearrange("p (j d) -> p j d", d=D)
                        sp.dma_start(yd[t // SLOTS][t % SLOTS], of).then_inc(s_yo[t % 2], 16)

                    for t in range(XB):
                        load(t, True)
                        if t < 3:
                            load_weights(t, True)
                    for t in range(XB, TOTAL + XB + 2):
                        if t < TOTAL:
                            used(t, lambda real: load(t, real))
                        if t - 1 < TOTAL:
                            used(t - 1, lambda real: load_weights(t - 1, real))
                        if t >= XB + 2:
                            used(t - XB - 2, lambda real: store(t - XB - 2, real))
                    for s in range(2):
                        sp.wait_ge(s_yo[s], 16 * ((TOTAL + 1 - s) // 2))

                @block.gpsimd
                def _(pool):
                    for t in range(HALF, TILES):
                        scatter(t, s_sent)
                    pool.wait_ge(s_sent, 16 * 2 * HALF)
                    for s in range(2):
                        pool.wait_ge(s_yo[s], 16 * ((SLOTS + 1 - s) // 2))
                    for t in range(HALF):
                        combine.pool(pool, t)

                @block.tensor
                def _(pe):
                    def skip(bank, signal):
                        pe.matmul(bank[0:E, 0:E], rw_sb[:], rw_sb[:], start=True, stop=True).then_inc(signal, 1)

                    def turn(t, real=True):
                        s = t % XB
                        pe.wait_ge(s_xr[s], 16 * (t // XB + 1))
                        if not isinstance(t, int) or t >= 1:
                            pe.wait_ge(s_xl, t)
                        if not real:
                            skip(b_x, s_tr)
                            return
                        for j in range(4):
                            last = pe.transpose(b_x[:, j * P:(j + 1) * P], xr[s][:, j, :], ident[:])
                        last.then_inc(s_tr, 1)

                    def gate_up(t, s, later, real):
                        w = w_slot[t % 3]
                        pe.wait_ge(s_w[t % 3], 16 * (t // 3 + 1))
                        pe.wait_ge(s_xl, t + 1)
                        for c in range(2):
                            if later:
                                pe.wait_ge(s_hf, 2 * t - 1 + c)
                            if not real:
                                skip(b_g[c], s_gu)
                                continue
                            for bank, at in ((b_g[c], c * P), (b_u[c], H + c * P)):
                                high, low = w[:, at:at + P], w[:, WROW + at:WROW + at + P]
                                pe.matmul(bank[:], high, xh[s][:], start=True, stop=False)
                                pe.matmul(bank[:], high, xl[s][:], start=False, stop=False)
                                last = pe.matmul(bank[:], low, xh[s][:], start=False, stop=True)
                            last.then_inc(s_gu, 1)

                    def down(t, s, later, real):
                        w = w_slot[t % 3]
                        if later:
                            pe.wait_ge(s_oT, t)
                        for c in range(2):
                            pe.wait_ge(s_hl, 2 * t + c + 1)
                            if not real:
                                continue
                            at = 2 * H + c * D
                            high, low = w[:, at:at + D], w[:, WROW + at:WROW + at + D]
                            pe.matmul(b_d[:], high, hh[s][c][:], start=(c == 0), stop=False)
                            pe.matmul(b_d[:], high, hl[s][c][:], start=False, stop=False)
                            last = pe.matmul(b_d[:], low, hh[s][c][:], start=False, stop=(c == 1))
                        if real:
                            last.then_inc(s_dn, 1)
                        else:
                            skip(b_d, s_dn)

                    def turn_out(t, later, real):
                        pe.wait_ge(s_oT, t + 1)
                        if later:
                            pe.wait_ge(s_yr, t)
                        if not real:
                            skip(b_o, s_ot)
                            return
                        for j in range(4):
                            last = pe.transpose(b_o[:, j * P:(j + 1) * P], oT[t % 2][:, j * P:(j + 1) * P], ident[:])
                        last.then_inc(s_ot, 1)

                    used = Used(pe)
                    turn(0)
                    for t in range(TOTAL + 2):
                        if t < LAST:
                            used(t + 1, lambda real: turn(t + 1, real))
                        if t <= LAST:
                            used(t, lambda real: gate_up(t, t % 2, t >= 1, real))
                        if 1 <= t <= LAST + 1:
                            used(t - 1, lambda real: down(t - 1, (t - 1) % 2, t >= 2, real))
                        if t >= 2:
                            used(t - 2, lambda real: turn_out(t - 2, t >= 3, real))

                @block.scalar
                def _(act):
                    def run(real, signal, out_, in_, func):
                        if real:
                            nc.scalar.activation(out_, in_, func).then_inc(signal, 1)
                        else:
                            nc.scalar.activation(out_[:, 0:1], ones[:, 0:1], ACT.Copy).then_inc(signal, 1)

                    def x_high(t, s, later, real=True):
                        act.wait_ge(s_tr, t + 1)
                        if later:
                            act.wait_ge(s_gu, 2 * t - 2)
                        run(real, s_xh, xh[s][:], b_x[:], ACT.Copy)

                    def silu(t, later, real):
                        for c in range(2):
                            act.wait_ge(s_gu, 2 * t + c + 1)
                            if later:
                                act.wait_ge(s_hf, 2 * t - 1 + c)
                            run(real, s_sg, sg[c][:], b_g[c][:], ACT.Silu)

                    def hidden_high(t, s, later, real):
                        act.wait_ge(s_hf, 2 * t + 2)
                        if later:
                            act.wait_ge(s_dn, t - 1)
                        run(real, s_hh[1], hh[s][1][:], hf[1][:], ACT.Copy)

                    def down_copy(t, real):
                        act.wait_ge(s_dn, t + 1)
                        if t >= 2:
                            act.wait_ge(s_ot, t - 1)
                        run(real, s_oT, oT[t % 2][:], b_d[:], ACT.Copy)

                    def out_copy(t, s, later2, real):
                        act.wait_ge(s_ot, t + 1)
                        if later2:
                            act.wait_ge(s_yo[s], later2)
                        run(real, s_yr, yr[s][:].rearrange("p j d -> p (j d)"), b_o[:], ACT.Copy)

                    used = Used(act)
                    x_high(0, 0, False)
                    for t in range(TOTAL + 2):
                        if t < LAST:
                            used(t + 1, lambda real: x_high(t + 1, (t + 1) % 2, t >= 1, real))
                        if t <= LAST:
                            used(t, lambda real: silu(t, t >= 1, real))
                        if 1 <= t <= LAST + 1:
                            used(t - 1, lambda real: down_copy(t - 1, real))
                        if t <= LAST:
                            used(t, lambda real: hidden_high(t, t % 2, t >= 2, real))
                        if t >= 2:
                            used(t - 2, lambda real: out_copy(t - 2, t % 2, 16 * ((t - 2) // 2), real))
                    if besides:
                        for h in range(2):
                            norms.act(act, 0, h)
                        besides.act_end(act)

                @block.vector
                def _(dve):
                    def run(real, signal, out_, in0, in1, op):
                        if real:
                            nc.vector.tensor_tensor(out_, in0, in1, op).then_inc(signal, 1)
                        else:
                            nc.vector.tensor_copy(out_[:, 0:1], ones[:, 0:1]).then_inc(signal, 1)

                    def x_low(t, s, real=True):
                        dve.wait_ge(s_xh, t + 1)
                        run(real, s_xl, xl[s][:], b_x[:], xh[s][:].bitcast(fp32), ALU.subtract)

                    def hidden(t, s, later, real):
                        for c in range(2):
                            dve.wait_ge(s_sg, 2 * t + c + 1)
                            if t >= 1:
                                dve.wait_ge(s_hl, 2 * t + c - 1)
                            run(real, s_hf, hf[c][:], sg[c][:], b_u[c][:], ALU.mult)
                        if later:
                            dve.wait_ge(s_dn, t - 1)
                        dve.wait_ge(s_hf, 2 * t + 1)
                        width = T if real else 1
                        nc.vector.tensor_copy(hh[s][0][:, 0:width], hf[0][:, 0:width]).then_inc(s_hh[0], 1)
                        for c in range(2):
                            dve.wait_ge(s_hh[c], t + 1)
                            run(real, s_hl, hl[s][c][:], hf[c][:], hh[s][c][:].bitcast(fp32), ALU.subtract)

                    used = Used(dve)
                    x_low(0, 0)
                    if besides:
                        besides.start(dve)
                    for t in range(TOTAL):
                        s = t % 2
                        if t < LAST:
                            used(t + 1, lambda real: x_low(t + 1, 1 - s, real))
                        used(t, lambda real: hidden(t, s, t >= 2, real))
                        if besides and 2 <= t < 2 + besides.STEPS:
                            besides.dve(dve, t - 2)
                        if 0 <= t - COMBINE < HALF // 2:
                            for n in range(2):
                                combine.dve(dve, 2 * (t - COMBINE) + n)
                    combine.wait_done(dve, HALF)
                    if besides:
                        ln_chain = Chain(dve, norms.s_chain)
                        for t in range(CT):
                            norms.stats(ln_chain, t)
                        norms.factors(dve, ln_chain, 0)
                        norms.chained = ln_chain.n
                        besides.dve_end(dve)

        def mixer(tmp, r):
            def tb(name, shape, dt=fp32):
                return tmp.enter_context(nc.sbuf_tensor(name, shape, dt))

            combine = Combine(tb, 0)
            r.xT = [tb("xT_routed", [D, G * P])]
            xTb = [tb("xT_high", [D, 4 + SEQ], f32r), tb("xT_low", [D, 4 + SEQ], f32r)]
            cT = [[tb(f"cT{s}{k}", [P, SEQ]) for k in range(CH)] for s in range(2)]
            zr = [tb(f"z{s}", [P, CT, ZW]) for s in range(2)]
            dt = [tb(f"dt{s}", [P, CT, HEADS]) for s in range(2)]
            da = [tb(f"da{s}", [P, CT, HEADS]) for s in range(2)]
            e1 = tb("softplus_e", [P, CT, HEADS])
            e2 = tb("softplus_s", [P, CT, HEADS])
            e3 = tb("softplus_q", [P, CT, HEADS])
            tok = [tb(f"tok{i}", [P, INNER + STATE + 2 * HEADS]) for i in range(2)]
            exs = [tb(f"chunk_decay{i}", [P, 2 * HEADS]) for i in range(3)]
            dam = [tb(f"da_masked{i}", [P, HEADS, P]) for i in range(2)]
            seg = [tb(f"decay{i}", [P, HEADS, P]) for i in range(2)]
            gm = tb("g_masked", [P, P])
            mm = [tb(f"mix{i}", [P, HEADS, P]) for i in range(2)]
            xdt = [tb(f"x_dt{i}", [P, HEADS, HD]) for i in range(2)]
            xw = [tb(f"x_end{i}", [P, HEADS, HD]) for i in range(2)]
            xsd = [tb(f"x_skip{i}", [P, HEADS, HD]) for i in range(2)]
            state = tb("state", [STATE, HEADS, HD])
            y = [tb(f"y{i}", [P, HEADS, HD]) for i in range(2)]
            junk = tb("squares", [P, INNER])
            junk2 = tb("squares2", [P, D])
            yT = tb("yT", [P, INNER])
            ob = [tb(f"out_rows{s}", [P, CT, D]) for s in range(2)]
            ssq = [tb(f"ssq{s}", [P, CT]) for s in range(2)]
            ssq2 = [tb(f"ssq2{s}", [P, CT]) for s in range(2)]
            tn = tb("newton", [P, CT])
            var2 = tb("rms_var", [P, CT])
            stmp = tb("state_decayed", [STATE, HEADS, HD])
            r2 = tb("r2", [P, CT])

            b_acc, b_z, b_seg, b_g, b_tok, b_y, b_up = banks[0:2], banks[2], banks[3], banks[4], banks[5], banks[6], banks[7]

            s_tr = sem("m_turned")
            s_xh = sem("m_xT_high")
            s_xl = sem("m_xT_low")
            s_cv = sem("m_conv")
            s_ce = sem("m_conv_copied")
            s_z = sem("m_z")
            s_zc = sem("m_z_copied")
            s_si = sem("m_silu")
            s_sz = sem("m_silu_z")
            s_d0 = sem("m_dt_raw")
            s_d1 = sem("m_dt_exp")
            s_da = sem("m_da")
            s_dm = sem("m_da_masked")
            s_xd = sem("m_x_skip")
            s_tk = sem("m_tokens_turned")
            s_tc = sem("m_tokens_copied")
            s_g = sem("m_g")
            s_gm = sem("m_g_masked")
            s_sg = sem("m_segments")
            s_eg = sem("m_decays")
            s_mm = sem("m_mix")
            s_x1 = sem("m_x_dt")
            s_xw = sem("m_x_end")
            s_mid = sem("m_y_and_update")
            s_st = sem("m_state")
            s_yd = sem("m_y_read")
            s_y = sem("m_y")
            s_yt = sem("m_y_turned")
            s_yc = sem("m_y_copied")
            s_o = sem("m_out")
            s_q1 = sem("m_ssq1")
            s_q2 = sem("m_ssq2")
            s_x2 = sem("m_new_x")
            s_zz = sem("m_pad")

            B = BATCH
            groups = [(k, h) for h in range(2) for k in range(CH)]
            CONVS = [[(1, 3)], [(1, 4)], [(1, 5)], [(1, 6)], [(1, 7)], [], [(2, 0), (2, 1)], [(2, 2)]]
            EARLY = (2, 0)
            ZSTEPS = CT // 2
            STATS, MOMENTS, NORM, TURN = (4, 6), 7, 8, 9
            LOGITS = [14] * (ROUTED - 1) + [13]
            COUNTS = [16] * (ROUTED - 1) + [15]
            SCATTER = 17

            FREE = TILES - 2 * CT + 5

            def turned_y(t):
                return b_up[:, INNER:] if t < FREE else b_acc[t % 2][:, 0:INNER]

            def since(t, q, stage):
                return t - (G * (q + 1) + stage)

            AHEAD = 2 * CT + 4

            with nc.Block() as block:
                @block.gpsimd
                def _(pool):
                    nc.gpsimd.memset(xTb[0][:, 0:4].bitcast(fp32), 0.0).then_inc(s_zz, 1)
                    nc.gpsimd.memset(xTb[1][:, 0:4].bitcast(fp32), 0.0).then_inc(s_zz, 1)

                    def mask(t):
                        b, c = divmod(t, CT)
                        pool.wait_ge(s_da, b + 1)
                        if t >= 2:
                            pool.wait_ge(s_sg, t - 1)
                        nc.gpsimd.tensor_tensor(dam[t % 2][:], bc(da[b % 2][:, c, :].unsqueeze(2), [P, HEADS, P]),
                                                bc(upto[:].unsqueeze(1), [P, HEADS, P]), ALU.mult).then_inc(s_dm, 1)

                    def skip(t):
                        pool.wait_ge(s_tc, t + 1)
                        if t >= 2:
                            pool.wait_ge(s_y, t - 1)
                        nc.gpsimd.tensor_tensor(xsd[t % 2][:], tok[t % 2][:, 0:INNER].rearrange("p (h d) -> p h d", d=HD),
                                                bc(d_skip[:].unsqueeze(2), [P, HEADS, HD]), ALU.mult).then_inc(s_xd, 1)

                    mask(0)
                    skip(0)
                    for t in range(TILES):
                        if t + 1 < TILES:
                            mask(t + 1)
                            skip(t + 1)
                        if HALF <= t + AHEAD + 2 < TILES:
                            combine.pool(pool, t + AHEAD + 2)
                        if 0 <= since(t, 0, SCATTER) < HALF:
                            r.scatter(pool, since(t, 0, SCATTER))
                    for n in range(since(TILES, 0, SCATTER), HALF):
                        r.scatter(pool, n)

                @block.tensor
                def _(pe):
                    def turn(b):
                        for h in range(2):
                            pe.wait_ge(norms.s_done, 2 * b + h + 1)
                            if b or h:
                                pe.wait_ge(s_ce, 8 * b)
                            for j in range(4):
                                last = pe.transpose(b_acc[h][:, j * P:(j + 1) * P], xn_sb[:, CT * b + 4 * h + j, :], ident[:])
                            last.then_inc(s_tr, 1)

                    def conv(b, g, first_tap=0, last_tap=CONV_K - 1):
                        n = 8 * b + g
                        k, h = groups[g]
                        if first_tap == 0:
                            pe.wait_ge(s_xl, 2 * b + 2)
                            if g >= 2:
                                pe.wait_ge(s_ce, n - 1)
                        acc = b_acc[n % 2]
                        for tap in range(first_tap, last_tap + 1):
                            at = 1 + tap + 512 * h
                            for i, (w, x) in enumerate(((0, 0), (0, 1), (1, 0))):
                                last = pe.matmul(acc[:], wc[w][:, tap, k * P:(k + 1) * P], xTb[x][:, at:at + 512],
                                                 start=(tap == 0 and i == 0), stop=(tap == CONV_K - 1 and i == 2))
                        if last_tap == CONV_K - 1:
                            last.then_inc(s_cv, 1)

                    def zdt(b, c):
                        n = CT * b + c
                        pe.wait_ge(s_xl, 2 * b + 2)
                        z_bank_free(pe)
                        at = 4 + P * c
                        for i, (x, w) in enumerate(((0, 0), (0, 1), (1, 0))):
                            last = pe.matmul(b_z[:, 0:ZW], xTb[x][:, at:at + P], wz[w][:], start=(i == 0), stop=(i == 2))
                        last.then_inc(s_z, 1)
                        used[0] += 1

                    used = [0, 0]

                    def z_bank_free(pe):
                        if used[0]:
                            pe.wait_ge(s_zc, used[0])
                        if used[1]:
                            pe.wait_ge(s_q2, used[1])

                    g_read = [None]

                    def g_bank_free(pe):
                        if g_read[0]:
                            pe.wait_ge(*g_read[0])

                    def front(t):
                        b, c = divmod(t, CT)
                        cols = slice(c * P, (c + 1) * P)
                        cs = cT[b % 2]
                        pe.wait_ge(s_si, b + 1)
                        if t >= 1:
                            pe.wait_ge(s_eg, t)
                        for j, k in enumerate((0, 1, 2)):
                            pe.transpose(b_tok[:, j * P:(j + 1) * P], cs[k][:, cols], ident[:])
                        pe.wait_ge(s_da, b + 1)
                        at = INNER + STATE
                        pe.matmul(b_tok[:, at:at + HEADS], upto[:], da[b % 2][:, c, :], start=True, stop=True)
                        pe.matmul(b_tok[:, at + HEADS:at + 2 * HEADS], ones[:], da[b % 2][:, c, :], start=True,
                                  stop=True).then_inc(s_tk, 1)
                        g_bank_free(pe)
                        pe.matmul(b_g[:, 0:P], cs[2][:, cols], cs[3][:, cols], start=True, stop=True).then_inc(s_g, 1)
                        g_read[0] = (s_gm, t + 1)
                        pe.wait_ge(s_dm, t + 1)
                        pe.matmul(b_seg[:], after[:], dam[t % 2][:].rearrange("p h i -> p (h i)"), start=True,
                                  stop=True).then_inc(s_sg, 1)

                    def mid(t):
                        b, c = divmod(t, CT)
                        i = t % 2
                        if t >= 1:
                            pe.wait_ge(s_yd, t)
                            pe.wait_ge(s_st, t)
                            if 2 <= t <= FREE:
                                pe.wait_ge(s_yc, t - 1)
                        if c:
                            pe.matmul(b_y[:, INNER:], cT[b % 2][3][:, c * P:(c + 1) * P],
                                      state[:].rearrange("p h d -> p (h d)"), start=True, stop=True)
                        pe.wait_ge(s_mm, t + 1)
                        for h in range(HEADS):
                            pe.matmul(b_y[:, h * HD:(h + 1) * HD], mm[i][:, h, :], xdt[i][:, h, :], start=True, stop=True)
                        pe.wait_ge(s_xw, t + 1)
                        pe.matmul(b_up[:, 0:INNER], tok[i][:, INNER:INNER + STATE], xw[i][:].rearrange("p h d -> p (h d)"),
                                  start=True, stop=True).then_inc(s_mid, 1)

                    def turn_y(t):
                        pe.wait_ge(s_y, t + 1)
                        if t < FREE:
                            pe.wait_ge(s_st, t + 1)
                        else:
                            pe.wait_ge(s_ce, 8 * B)
                            pe.wait_ge(s_yc, t - 1)
                        for k in range(2):
                            last = pe.transpose(turned_y(t)[:, k * P:(k + 1) * P],
                                                y[t % 2][:].rearrange("p h d -> p (h d)")[:, k * P:(k + 1) * P], ident[:])
                        last.then_inc(s_yt, 1)

                    def project(t):
                        pe.wait_ge(s_yc, t + 1)
                        z_bank_free(pe)
                        for k in range(2):
                            last = pe.matmul(b_z[:, 0:D], yT[:, k * P:(k + 1) * P], w_out[:, k, :],
                                             start=(k == 0), stop=(k == 1))
                        last.then_inc(s_o, 1)
                        used[1] += 1

                    pe.wait_ge(s_zz, 2)
                    turn(0)
                    for g in range(8):
                        conv(0, g)
                        zdt(0, g)
                    turn(1)
                    conv(1, 0)
                    conv(1, 1)
                    front(0)
                    conv(1, 2)
                    for t in range(TILES):
                        b, c = divmod(t, CT)
                        more = b + 1 < B
                        if t + 1 < TILES:
                            front(t + 1)
                        if c == 5 and b + 2 < B:
                            turn(b + 2)
                        convs = [(b + ahead, g) for ahead, g in CONVS[c] if b + ahead < B and (ahead, g) != EARLY]
                        if convs:
                            conv(*convs[0], 0, 1)
                        if t > FREE:
                            mid(t)
                        if t >= 1:
                            turn_y(t - 1)
                        if more and c < ZSTEPS:
                            zdt(b + 1, 2 * c)
                        for n, (seq, g) in enumerate(convs):
                            conv(seq, g, 2 if n == 0 else 0)
                        if t >= 1:
                            project(t - 1)
                        if t <= FREE:
                            mid(t)
                        if more and c < ZSTEPS:
                            zdt(b + 1, 2 * c + 1)
                        if c == 5 and b + 2 < B:
                            conv(b + 2, EARLY[1])
                        for q in range(ROUTED):
                            h = since(t, q, TURN)
                            if 0 <= h < XG:
                                g_bank_free(pe)
                                r.turn(pe, q, h, b_g)
                                g_read[0] = (r.signals["turned_read"], XG * q + h + 1)
                            if since(t, q, LOGITS[q]) == 0:
                                g_bank_free(pe)
                                r.logits(pe, q, b_g)
                                g_read[0] = (r.signals["logits_read"], q + 1)
                            if since(t, q, COUNTS[q]) == 0:
                                g_bank_free(pe)
                                r.counts(pe, q, b_g)
                                g_read[0] = (r.signals["counts_read"], q + 1)
                    turn_y(TILES - 1)
                    project(TILES - 1)

                @block.scalar
                def _(act):
                    def x_high(b):
                        for h in range(2):
                            act.wait_ge(s_tr, 2 * b + h + 1)
                            if b:
                                act.wait_ge(s_z, CT * b)
                                act.wait_ge(s_cv, 8 * b)
                            nc.scalar.activation(xTb[0][:, 4 + 512 * h:516 + 512 * h], b_acc[h][:], ACT.Copy).then_inc(s_xh, 1)

                    def conv_copy(b, g):
                        n = 8 * b + g
                        k, h = groups[g]
                        act.wait_ge(s_cv, n + 1)
                        if b >= 2:
                            act.wait_ge(s_mid, CT * (b - 2) + 4 * h + 4)
                        nc.scalar.activation(cT[b % 2][k][:, 512 * h:512 * (h + 1)], b_acc[n % 2][:], ACT.Identity,
                                             bias=conv_b[:, k:k + 1]).then_inc(s_ce, 1)

                    def z_copy(b, c):
                        act.wait_ge(s_z, CT * b + c + 1)
                        nc.scalar.activation(zr[b % 2][:, c, :], b_z[:, 0:ZW], ACT.Copy).then_inc(s_zc, 1)

                    def silus(b):
                        act.wait_ge(s_ce, 8 * b + 8)
                        act.wait_ge(s_zc, CT * b + CT)
                        act.wait_ge(s_d0, b + 1)
                        for k in (2, 3, 0, 1):
                            last = nc.scalar.activation(cT[b % 2][k][:], cT[b % 2][k][:], ACT.Silu)
                        last.then_inc(s_si, 1)
                        nc.scalar.activation(zr[b % 2][:, :, 0:INNER], zr[b % 2][:, :, 0:INNER], ACT.Silu).then_inc(s_sz, 1)

                    def dt_exp(b):
                        act.wait_ge(s_d0, b + 1)
                        nc.scalar.activation(e2[:], e1[:], ACT.Exp, scale=-1.0).then_inc(s_d1, 1)

                    def front(t):
                        i = t % 2
                        act.wait_ge(s_tk, t + 1)
                        if t >= 2:
                            act.wait_ge(s_mid, t - 1)
                            act.wait_ge(s_xd, t - 1)
                        n = INNER + STATE
                        nc.scalar.activation(tok[i][:, 0:n], b_tok[:, 0:n], ACT.Copy).then_inc(s_tc, 1)
                        if t >= 3:
                            act.wait_ge(s_y, t - 2)
                        nc.scalar.activation(exs[t % 3][:], b_tok[:, n:n + 2 * HEADS], ACT.Exp)
                        act.wait_ge(s_sg, t + 1)
                        nc.scalar.activation(seg[i][:].rearrange("p h i -> p (h i)"), b_seg[:], ACT.Exp).then_inc(s_eg, 1)

                    def y_copy(t):
                        act.wait_ge(s_yt, t + 1)
                        if t >= 1:
                            act.wait_ge(s_o, t)
                        nc.scalar.activation(yT[:], turned_y(t), ACT.Copy).then_inc(s_yc, 1)
                        if t % CT == 0 and t >= 2 * CT:
                            act.wait_ge(s_x2, t // CT - 1)
                        if t >= 1:
                            act.wait_ge(s_q1, t)
                        nc.scalar.activation(junk[:], y[t % 2][:].rearrange("p h d -> p (h d)"), ACT.Square,
                                             accum_out=ssq[t // CT % 2][:, t % CT:t % CT + 1]).then_inc(s_q1, 1)

                    def out_copy(t):
                        b, c = divmod(t, CT)
                        act.wait_ge(s_o, t + 1)
                        nc.scalar.activation(ob[b % 2][:, c, :], b_z[:, 0:D], ACT.Copy)
                        if t >= 1:
                            act.wait_ge(s_q2, t)
                        nc.scalar.activation(junk2[:], b_z[:, 0:D], ACT.Square,
                                             accum_out=ssq2[b % 2][:, c:c + 1]).then_inc(s_q2, 1)

                    x_high(0)
                    for g in range(8):
                        conv_copy(0, g)
                        z_copy(0, g)
                        if g in (4, 5):
                            norms.act(act, 1, g - 4)
                    x_high(1)
                    dt_exp(0)
                    silus(0)
                    conv_copy(1, 0)
                    conv_copy(1, 1)
                    front(0)
                    conv_copy(1, 2)
                    for t in range(TILES):
                        b, c = divmod(t, CT)
                        more = b + 1 < B
                        if t + 1 < TILES:
                            front(t + 1)
                        if b + 2 < B and c == 5:
                            x_high(b + 2)
                        if t >= 1:
                            y_copy(t - 1)
                        if more and c < ZSTEPS:
                            z_copy(b + 1, 2 * c)
                        for ahead, g in CONVS[c]:
                            if b + ahead < B:
                                conv_copy(b + ahead, g)
                        if t >= 1:
                            out_copy(t - 1)
                        if more and c < ZSTEPS:
                            z_copy(b + 1, 2 * c + 1)
                        for q in range(ROUTED):
                            if 0 <= since(t, q, TURN) < XG:
                                r.xT_copy(act, q, since(t, q, TURN), b_g)
                            if 0 <= since(t, q, NORM) < XG:
                                r.norm(act, q, since(t, q, NORM))
                        if more and c == 4:
                            dt_exp(b + 1)
                        if b + 2 < B and c == 4:
                            norms.act(act, b + 2, 0)
                            norms.act(act, b + 2, 1)
                        if more and c == 5:
                            silus(b + 1)
                    y_copy(TILES - 1)
                    out_copy(TILES - 1)

                @block.vector
                def _(dve):
                    ch = Chain(dve, norms.s_chain, norms.chained)
                    rc = Chain(dve, r.signals["chain"])

                    def residual(t):
                        if t >= HALF:
                            combine.dve(dve, t)
                            combine.wait_done(dve, t + 1)
                        norms.stats(ch, t)

                    def x_low(b):
                        for h in range(2):
                            dve.wait_ge(s_xh, 2 * b + h + 1)
                            cols = slice(4 + 512 * h, 516 + 512 * h)
                            nc.vector.tensor_tensor(xTb[1][:, cols], b_acc[h][:], xTb[0][:, cols].bitcast(fp32),
                                                    ALU.subtract).then_inc(s_xl, 1)

                    def dt_raw(b):
                        z = zr[b % 2]
                        dve.wait_ge(s_zc, CT * b + CT)
                        d = dt[b % 2]
                        ch(nc.vector.tensor_tensor(d[:], z[:, :, INNER:], bc(dt_bias[:].unsqueeze(1), [P, CT, HEADS]), ALU.add))
                        ch(nc.vector.tensor_scalar(e3[:], d[:], -1.0, None, ALU.mult))
                        nc.vector.tensor_tensor(e1[:], d[:], e3[:], ALU.max).then_inc(s_d0, 1)

                    def dt_end(b):
                        d = dt[b % 2]
                        dve.wait_ge(s_d1, b + 1)
                        ch(nc.vector.tensor_scalar(e3[:], e2[:], 2.0, None, ALU.add))
                        ch(nc.vector.reciprocal(e3[:], e3[:]))
                        ch(nc.vector.tensor_tensor(e2[:], e2[:], e3[:], ALU.mult))
                        ch(nc.vector.tensor_tensor(e1[:], e2[:], e2[:], ALU.mult))
                        ch(nc.vector.tensor_scalar(e3[:], e1[:], 2.0 / 15, None, ALU.mult))
                        for n in (13, 11, 9, 7, 5, 3):
                            ch(nc.vector.scalar_tensor_tensor(out=e3[:], in0=e3[:], scalar=2.0 / n, in1=e1[:], op0=ALU.add, op1=ALU.mult))
                        ch(nc.vector.scalar_tensor_tensor(out=e3[:], in0=e3[:], scalar=2.0, in1=e2[:], op0=ALU.add, op1=ALU.mult))
                        ch(nc.vector.scalar_tensor_tensor(out=d[:], in0=d[:], scalar=0.0, in1=e3[:], op0=ALU.max, op1=ALU.add))
                        ch(nc.vector.tensor_tensor(da[b % 2][:], d[:], bc(neg_a[:].unsqueeze(1), [P, CT, HEADS]), ALU.mult))
                        nc.vector.tensor_scalar(da[b % 2][:], da[b % 2][:], FLOOR, None, ALU.max).then_inc(s_da, 1)
                        dve.wait_ge(s_da, b + 1)

                    def mix(t):
                        b, c = divmod(t, CT)
                        i = t % 2
                        dve.wait_ge(s_g, t + 1)
                        if t >= 1:
                            dve.wait_ge(s_mm, t)
                        nc.vector.tensor_tensor(gm[:], b_g[:, 0:P], upto[:], ALU.mult).then_inc(s_gm, 1)
                        dve.wait_ge(s_tc, t + 1)
                        if t >= 2:
                            dve.wait_ge(s_mid, t - 1)
                        hd = [P, HEADS, HD]
                        nc.vector.tensor_tensor(xdt[i][:], tok[i][:, 0:INNER].rearrange("p (h d) -> p h d", d=HD),
                                                bc(dt[b % 2][:, c, :].unsqueeze(2), hd), ALU.mult).then_inc(s_x1, 1)
                        dve.wait_ge(s_eg, t + 1)
                        dve.wait_ge(s_gm, t + 1)
                        nc.vector.tensor_tensor(mm[i][:], seg[i][:], bc(gm[:].unsqueeze(1), [P, HEADS, P]), ALU.mult
                                                ).then_inc(s_mm, 1)
                        dve.wait_ge(s_x1, t + 1)
                        nc.vector.tensor_tensor(xw[i][:], xdt[i][:], bc(seg[i][:, :, P - 1:P], hd), ALU.mult).then_inc(s_xw, 1)

                    def after_mid(t):
                        b, c = divmod(t, CT)
                        i = t % 2
                        hd = [P, HEADS, HD]
                        up = b_up[:, 0:INNER].rearrange("p (h d) -> p h d", d=HD)
                        yd, yo = (b_y[:, n * INNER:(n + 1) * INNER].rearrange("p (h d) -> p h d", d=HD) for n in range(2))
                        if c:
                            ch(nc.vector.tensor_tensor(stmp[:], state[:], bc(exs[t % 3][:, HEADS:].unsqueeze(2), hd), ALU.mult))
                        dve.wait_ge(s_mid, t + 1)
                        if c:
                            nc.vector.tensor_tensor(state[:], stmp[:], up, ALU.add).then_inc(s_st, 1)
                        else:
                            nc.vector.tensor_copy(state[:], up).then_inc(s_st, 1)
                        if t >= 2:
                            dve.wait_ge(s_yt, t - 1)
                            dve.wait_ge(s_q1, t - 1)
                        dve.wait_ge(s_xd, t + 1)
                        if c:
                            ch(nc.vector.tensor_tensor(y[i][:], yo, bc(exs[t % 3][:, 0:HEADS].unsqueeze(2), hd), ALU.mult))
                            ch(nc.vector.tensor_tensor(y[i][:], y[i][:], xsd[i][:], ALU.add))
                            nc.vector.tensor_tensor(y[i][:], y[i][:], yd, ALU.add).then_inc(s_yd, 1)
                        else:
                            nc.vector.tensor_tensor(y[i][:], xsd[i][:], yd, ALU.add).then_inc(s_yd, 1)
                        dve.wait_ge(s_yd, t + 1)
                        dve.wait_ge(s_sz, b + 1)
                        nc.vector.tensor_tensor(y[i][:], y[i][:], zr[b % 2][:, c, 0:INNER].rearrange("p (h d) -> p h d", d=HD),
                                                ALU.mult).then_inc(s_y, 1)
                        dve.wait_ge(s_st, t + 1)

                    def finish_scale(b):
                        s = b % 2
                        dve.wait_ge(s_q2, CT * b + CT)
                        ch(nc.vector.tensor_scalar(var2[:], ssq[s][:], 1.0 / INNER, LN_EPS, ALU.mult, ALU.add))
                        ch(nc.vector.tensor_scalar(tn[:], ssq2[s][:], 1.0 / D, None, ALU.mult))
                        ch(nc.vector.scalar_tensor_tensor(out=var2[:], in0=var2[:], scalar=LN_EPS, in1=tn[:],
                                                          op0=ALU.mult, op1=ALU.add))
                        rsqrt(ch, r2[:], var2[:], tn[:])
                        dve.wait_ge(norms.s_done, 2 * b + 2)
                        rows = slice(CT * b, CT * b + CT)
                        ch(nc.vector.tensor_tensor(x_sb[:, rows, :], x_sb[:, rows, :], xn_sb[:, rows, :], ALU.add))

                    def finish_rows(b):
                        for c in range(CT):
                            last = nc.vector.scalar_tensor_tensor(out=x_sb[:, CT * b + c, :], in0=ob[b % 2][:, c, :],
                                                                  scalar=r2[:, c:c + 1], in1=x_sb[:, CT * b + c, :],
                                                                  op0=ALU.mult, op1=ALU.add)
                        last.then_inc(s_x2, 1)
                        dve.wait_ge(s_x2, b + 1)

                    x_low(0)
                    for t in range(CT, 2 * CT):
                        residual(t)
                    norms.factors(dve, ch, 1)
                    x_low(1)
                    dt_raw(0)
                    dt_end(0)
                    for t in range(2 * CT, AHEAD):
                        residual(t)
                    mix(0)
                    for t in range(TILES):
                        b, c = divmod(t, CT)
                        if b + 1 < B and c == 4:
                            dt_raw(b + 1)
                        if t + 1 < TILES:
                            mix(t + 1)
                        if b + 2 < B and c == 5:
                            x_low(b + 2)
                        after_mid(t)
                        if t + AHEAD < TILES:
                            residual(t + AHEAD)
                        if b >= 1 and c == 1:
                            finish_scale(b - 1)
                        if b >= 1 and c == 2:
                            finish_rows(b - 1)
                        if b + 2 < B and c == 3:
                            norms.factors(dve, ch, b + 2)
                        if b + 1 < B and c == 5:
                            dt_end(b + 1)
                        for q in range(ROUTED):
                            for n in range(2):
                                if since(t, q, STATS[n]) == 0:
                                    r.stats(dve, rc, q, range(CT * n, CT * n + CT))
                            if since(t, q, MOMENTS) == 0:
                                r.moments(dve, rc, q)
                            if since(t, q, LOGITS[q]) == 0:
                                r.choose(dve, rc, q, b_g)
                            if since(t, q, COUNTS[q]) == 0:
                                r.place(dve, rc, q, b_g)
                    finish_scale(B - 1)
                    finish_rows(B - 1)
                    r.chained = rc.n


        def last_combine():
            combine = Combine(lambda name, shape: sb(f"c2_{name}", shape), 1)
            s_out = sem("c2_stored")
            with nc.Block() as block:
                @block.gpsimd
                def _(pool):
                    for t in range(HALF, TILES):
                        combine.pool(pool, t)

                @block.vector
                def _(dve):
                    for t in range(HALF, TILES):
                        combine.dve(dve, t)

                @block.sync
                def _(sp):
                    for b in range(BATCH):
                        combine.wait_done(sp, CT * (b + 1))
                        sp.dma_start(out[b * SEQ:(b + 1) * SEQ, :].rearrange("(t p) d -> p t d", p=P),
                                     x_sb[:, CT * b:CT * b + CT, :]).then_inc(s_out, 16)
                    sp.wait_ge(s_out, 16 * BATCH)

        with ExitStack() as tmp:
            mixer_weights = MixerWeights(lambda name, shape, dt=fp32: tmp.enter_context(nc.sbuf_tensor(name, shape, dt)))
            with ExitStack() as inner:
                tb = lambda name, shape, dt=fp32: inner.enter_context(nc.sbuf_tensor(f"r1_{name}", shape, dt))
                route(router("r1", tb), tb, Setup(tb))
            experts("f1", mixer_weights)
        with ExitStack() as tmp:
            r2 = router("r2", lambda name, shape, dt=fp32: tmp.enter_context(nc.sbuf_tensor(f"r2_{name}", shape, dt)))
            with ExitStack() as inner:
                mixer(inner, r2)
            route(r2, lambda name, shape: tmp.enter_context(nc.sbuf_tensor(f"r2_{name}", shape, fp32)), None, ROUTED)
        experts("f2", None)
        last_combine()


_INS = ['x', 'router_wT', 'w_gate', 'w_up', 'w_down', 'W_in', 'conv_wT', 'conv_bT', 'dt_bias', 'A_log', 'D', 'norm_wT', 'W_out']


def kernel(**inputs):
    import numpy as np
    import concourse.bacc as bacc
    from concourse.bass_utils import run_bass_kernel_spmd as run

    given = {k.replace("L0_attn_", "").replace("L0_ffn_", ""): np.asarray(v) for k, v in inputs.items()}
    given["x"] = given["x"].reshape(N, D)
    given["router_wT"] = given["router_w"].T
    given["conv_wT"] = given["conv_w"].T
    given["conv_bT"] = given["conv_b"].reshape(CH, P).T
    given["norm_wT"] = given["norm_w"].reshape(2, P).T
    nc = bacc.Bacc("TRN2", target_bir_lowering=False, num_devices=1)
    arrays, io = {}, {}
    for name in _INS:
        a = np.ascontiguousarray(given[name])
        arrays[f"in_{name}_dram"] = a
        io[name] = nc.dram_tensor(f"in_{name}_dram", a.shape, mybir.dt.from_np(a.dtype), kind="ExternalInput").ap()
    out = nc.dram_tensor("out_dram", (N, D), fp32, kind="ExternalOutput").ap()
    build(nc, io, out)
    r = run(nc, [arrays], core_ids=[0])
    return r.results[0]["out_dram"].reshape(BATCH, SEQ, D)
```
